# Optimizing a Trainium2 kernel written in Bass

```python
import numpy as np
import jax
import jax.numpy as jnp

def _softmax(x, axis=-1):
    return jax.nn.softmax(x, axis=axis)

def _gelu(x):
    return jax.nn.gelu(x, approximate=True)

def _silu(x):
    return jax.nn.silu(x)

def _sigmoid(x):
    return jax.nn.sigmoid(x)

def _layernorm(x, axis=-1, eps=1e-05):
    m = jnp.mean(x, axis=axis, keepdims=True)
    v = jnp.var(x, axis=axis, keepdims=True)
    return (x - m) / jnp.sqrt(v + eps)

def _scatter_add(tgt, idx, src, axis=0):
    return tgt.at[idx].add(src)

def _segment_sum(src, seg, n):
    return jax.ops.segment_sum(src, seg, n)
kernel_name = 'mk_adaln_attn_ffn_d2_seqx_r8_bf9afc'

def setup_inputs(seed: int=0):
    np.random.seed(seed)
    _w = jnp.asarray

    def _rec_inputs():
        import jax
        import jax.numpy as jnp
        _rk = jax.random.key(seed)
        x = -0.0003929 + 0.9999 * jax.random.normal(jax.random.fold_in(_rk, 1), (64, 32, 128), jnp.float32)
        _lenS = 32 - jax.random.randint(jax.random.fold_in(_rk, 7), (64,), 0, max(1, 32 // 4) + 1, jnp.int32)
        _lenS2 = 32 - jax.random.randint(jax.random.fold_in(_rk, 8), (64,), 0, max(1, 32 // 4) + 1, jnp.int32)
        itok_B_0_2 = jax.random.randint(jax.random.fold_in(_rk, 11), (64,), 0, 3, jnp.int32)
        condB_tauraws = -5.74692 + 0.777674 * jax.random.normal(jax.random.fold_in(_rk, 12), (64,), jnp.float32)
        cond_256 = -0.000235209 + 0.019331 * jax.random.normal(jax.random.fold_in(_rk, 13), (64, 32), jnp.float32)
        condB_bn2 = jnp.zeros((64,), jnp.float32)
        cond_1024 = -4.10585e-05 + 0.0199478 * jax.random.normal(jax.random.fold_in(_rk, 15), (64, 128), jnp.float32)
        itok_B_0_7 = jax.random.randint(jax.random.fold_in(_rk, 16), (64,), 0, 8, jnp.int32)
        itok_B_0_30 = jax.random.randint(jax.random.fold_in(_rk, 17), (64,), 0, 31, jnp.int32)
        return (x, itok_B_0_2, condB_tauraws, cond_256, condB_bn2, cond_1024, itok_B_0_7, itok_B_0_30)
    x, itok_B_0_2, condB_tauraws, cond_256, condB_bn2, cond_1024, itok_B_0_7, itok_B_0_30 = _rec_inputs()

    def _L0_cond_setup():
        import jax, jax.numpy as jnp
        import numpy as np
        NEG_INF = -1e+30
        key = jax.random.key(seed)
        k1, k2, k3, k4, k5 = jax.random.split(key, 5)
        B, S, D, A = (16, 128, 128, 32)
        hidden = jax.random.normal(k1, (B, S, D), dtype=jnp.float32)
        W1 = jax.random.normal(k2, (D, A), dtype=jnp.float32) / np.sqrt(D)
        b1 = jax.random.normal(k3, (A,), dtype=jnp.float32) * 0.01
        v = jax.random.normal(k4, (A,), dtype=jnp.float32) / np.sqrt(A)
        prompt_type_ids = jax.random.randint(k5, (B,), 0, 3, dtype=jnp.int32)
        return {'hidden': hidden, 'W1': W1, 'b1': b1, 'v': v, 'prompt_type_ids': prompt_type_ids}
    _L0_cond_all = _L0_cond_setup()
    _L0_cond_in = {k: v for k, v in _L0_cond_all.items() if k in ('W1', 'b1', 'v')}
    del _L0_cond_all

    def _L0_attn_setup():
        import jax, jax.numpy as jnp
        import numpy as np
        EMBED_DIM = 128
        NUM_HEADS = 16
        HEAD_DIM = EMBED_DIM // NUM_HEADS
        WINDOW = 128
        key = jax.random.key(seed)
        ks = jax.random.split(key, 9)
        B, T, C = (1, 256, EMBED_DIM)
        s = 1.0 / np.sqrt(C)
        inp = {'x': jax.random.normal(ks[0], (B, T, C), dtype=jnp.float32), 'wq': jax.random.normal(ks[1], (C, C), dtype=jnp.float32) * s, 'bq': jnp.zeros((C,), dtype=jnp.float32), 'wk': jax.random.normal(ks[2], (C, C), dtype=jnp.float32) * s, 'bk': jnp.zeros((C,), dtype=jnp.float32), 'wv': jax.random.normal(ks[3], (C, C), dtype=jnp.float32) * s, 'bv': jnp.zeros((C,), dtype=jnp.float32), 'wo': jax.random.normal(ks[4], (C, C), dtype=jnp.float32) * s, 'bo': jnp.zeros((C,), dtype=jnp.float32)}
        return inp
    _L0_attn_all = _L0_attn_setup()
    _L0_attn_in = {k: v for k, v in _L0_attn_all.items() if k in ('wq', 'bq', 'wk', 'bk', 'wv', 'bv', 'wo', 'bo')}
    del _L0_attn_all

    def _L0_cond2_setup():
        import jax, jax.numpy as jnp
        import numpy as np
        import math
        B, T, E, D = (4, 256, 128, 4)

        def _tau_init(t):
            a = 0.1 ** (1.0 / max(t - 1, 1))
            tt = -math.log(max(a, 1e-10))
            return math.log(math.exp(tt) - 1 + 1e-10)

        def causal_ema(b, tau_raw):
            alpha = jnp.exp(-jax.nn.softplus(tau_raw)).astype(b.dtype)

            def step(h, bt):
                h = alpha * h + bt
                return (h, h)
            h0 = jnp.zeros((b.shape[0], b.shape[2]), b.dtype)
            _, hs = jax.lax.scan(step, h0, jnp.swapaxes(b, 0, 1))
            return jnp.swapaxes(hs, 0, 1)
        key = jax.random.key(seed)
        ks = jax.random.split(key, 10)
        s = 0.02
        return {'x': jax.random.normal(ks[0], (B, T, E), jnp.float32), 'tau_ctx': jnp.float32(_tau_init(max(T // 2, 4))), 'tau_raws': jnp.array([_tau_init(max(T // 2 ** i, 2)) for i in range(D)], jnp.float32), 'Wg': jax.random.normal(ks[1], (E, 2 * E), jnp.float32) * s, 'bg': jnp.full((E,), -0.5, jnp.float32), 'Wn1': jax.random.normal(ks[2], (E // 4, E), jnp.float32) * s, 'bn1': jnp.zeros((E // 4,), jnp.float32), 'Wn2': jax.random.normal(ks[3], (D, E // 4), jnp.float32) * s, 'bn2': jnp.zeros((D,), jnp.float32), 'blend': jax.random.normal(ks[4], (D, E), jnp.float32) * s, 'Wsoma': jax.random.normal(ks[5], (E, E), jnp.float32) * s, 'bsoma': jnp.zeros((E,), jnp.float32), 'Wtemp': jax.random.normal(ks[6], (E, E), jnp.float32) * s, 'btemp': jnp.zeros((E,), jnp.float32), 'Wout': jax.random.normal(ks[7], (E, E), jnp.float32) * s, 'gamma': jnp.ones((E,), jnp.float32), 'beta': jnp.zeros((E,), jnp.float32)}
    _L0_cond2_all = _L0_cond2_setup()
    _L0_cond2_in = {k: v for k, v in _L0_cond2_all.items() if k in ('tau_ctx', 'Wg', 'bg', 'Wn1', 'bn1', 'Wsoma', 'bsoma', 'Wtemp', 'btemp', 'Wout', 'gamma', 'beta')}
    del _L0_cond2_all

    def _L0_ffn_setup():
        import jax, jax.numpy as jnp
        import numpy as np
        BLOCK = 32
        W_BITS = 4
        ACT_BITS = 16

        def act_qdq(x):
            qmax = 2.0 ** (ACT_BITS - 1) - 1.0
            scale = jnp.maximum(jnp.max(jnp.abs(x)) / qmax, 1e-12)
            return jnp.clip(jnp.round(x / scale), -qmax - 1.0, qmax) * scale

        def fixed_qdq_u16(x):
            scale = 1.0 / 65536.0
            return jnp.clip(jnp.round(x / scale), 0.0, 65535.0) * scale

        def lpbq_dequant(w):
            O, I = w.shape
            qmax = 2.0 ** (W_BITS - 1) - 1.0
            wb = w.reshape(O, I // BLOCK, BLOCK)
            s = jnp.maximum(jnp.max(jnp.abs(wb), axis=-1, keepdims=True) / qmax, 1e-12)
            wq = jnp.clip(jnp.round(wb / s), -qmax - 1.0, qmax) * s
            return wq.reshape(O, I)
        key = jax.random.key(seed)
        k1, k2, k3, k4 = jax.random.split(key, 4)
        B, S, H, I = (2, 512, 128, 384)
        x = jax.random.normal(k1, (B, S, H), jnp.float32)
        w_gate = jax.random.normal(k2, (I, H), jnp.float32) * 0.02
        w_up = jax.random.normal(k3, (I, H), jnp.float32) * 0.02
        w_down = jax.random.normal(k4, (H, I), jnp.float32) * 0.02
        return {'x': x, 'w_gate': w_gate, 'w_up': w_up, 'w_down': w_down}
    _L0_ffn_all = _L0_ffn_setup()
    _L0_ffn_in = {k: v for k, v in _L0_ffn_all.items() if k in ('w_gate', 'w_up', 'w_down')}
    del _L0_ffn_all

    def _L1_cond_setup():
        import jax, jax.numpy as jnp
        import numpy as np
        S, O, H = (8, 128, 128)
        B, N = (32, 64)
        key = jax.random.key(seed)
        k1, k2, k3, k4 = jax.random.split(key, 4)
        x = jax.random.normal(k1, (B, N, H), dtype=jnp.float32)
        subject_id = jax.random.randint(k2, (B,), 0, S)
        wbound = jnp.sqrt(2.0 / 6.0) * jnp.sqrt(3.0 / H)
        weight = jax.random.uniform(k3, (S, O, H), minval=-wbound, maxval=wbound, dtype=jnp.float32)
        bbound = 1.0 / jnp.sqrt(H)
        bias = jax.random.uniform(k4, (S, O), minval=-bbound, maxval=bbound, dtype=jnp.float32)
        return {'x': x, 'subject_id': subject_id, 'weight': weight, 'bias': bias}
    _L1_cond_all = _L1_cond_setup()
    _L1_cond_in = {k: v for k, v in _L1_cond_all.items() if k in ('weight', 'bias')}
    del _L1_cond_all

    def _L1_attn_setup():
        import jax, jax.numpy as jnp
        import numpy as np
        DIM = 128
        NUM_HEADS = 16
        HEAD_DIM = DIM // NUM_HEADS
        B, L = (4, 256)

        def _alibi_bias_causal(seq_len, dtype):
            h = jnp.arange(1, NUM_HEADS + 1, dtype=jnp.float32)
            slopes = jnp.power(2.0, -8.0 * h / NUM_HEADS)
            pos = jnp.arange(seq_len, dtype=jnp.float32)
            rel = jnp.abs(pos[:, None] - pos[None, :])
            bias = -slopes[:, None, None] * rel[None, :, :]
            causal = pos[:, None] >= pos[None, :]
            bias = jnp.where(causal[None, :, :], bias, -jnp.inf)
            return bias.astype(dtype)
        key = jax.random.key(seed)
        ks = jax.random.split(key, 9)
        s = 0.02
        return {'x': jax.random.normal(ks[0], (B, L, DIM), jnp.float32), 'Wq': jax.random.normal(ks[1], (DIM, DIM), jnp.float32) * s, 'bq': jax.random.normal(ks[2], (DIM,), jnp.float32) * s, 'Wk': jax.random.normal(ks[3], (DIM, DIM), jnp.float32) * s, 'bk': jax.random.normal(ks[4], (DIM,), jnp.float32) * s, 'Wv': jax.random.normal(ks[5], (DIM, DIM), jnp.float32) * s, 'bv': jax.random.normal(ks[6], (DIM,), jnp.float32) * s, 'Wo': jax.random.normal(ks[7], (DIM, DIM), jnp.float32) * s, 'bo': jax.random.normal(ks[8], (DIM,), jnp.float32) * s}
    _L1_attn_all = _L1_attn_setup()
    _L1_attn_in = {k: v for k, v in _L1_attn_all.items() if k in ('Wq', 'bq', 'Wk', 'bk', 'Wv', 'bv', 'Wo', 'bo')}
    del _L1_attn_all

    def _L1_cond2_setup():
        import jax, jax.numpy as jnp
        import numpy as np
        C, I, O = (32, 128, 128)
        B, T = (64, 64)
        key = jax.random.key(seed)
        kx, kc, kw, kb = jax.random.split(key, 4)
        x = jax.random.normal(kx, (B, T, I), dtype=jnp.float32)
        cat_ids = jax.random.randint(kc, (B,), 0, C)
        W = 0.02 * jax.random.normal(kw, (C, I, O), dtype=jnp.float32)
        b = jnp.zeros((C, O), dtype=jnp.float32)
        return {'x': x, 'cat_ids': cat_ids, 'W': W, 'b': b}
    _L1_cond2_all = _L1_cond2_setup()
    _L1_cond2_in = {k: v for k, v in _L1_cond2_all.items() if k in ('W', 'b')}
    del _L1_cond2_all

    def _L1_ffn_setup():
        import jax, jax.numpy as jnp
        import numpy as np
        H, I, E, NS, C = (128, 128, 6, 2, 2)
        TOPK = 2
        TEMP = 1.0
        EPS = 1e-06
        key = jax.random.key(seed)
        ks = jax.random.split(key, 20)
        sd = 0.02
        inp = {'x': jax.random.normal(ks[0], (4, 256, H), jnp.float32), 'router_W': jax.random.normal(ks[1], (C, H, E), jnp.float32) * sd, 'router_b': jax.random.normal(ks[2], (C, E), jnp.float32) * sd, 'gate_bias': jax.random.normal(ks[3], (C, E), jnp.float32) * sd, 'exp_Wup': jax.random.normal(ks[4], (E, H, I), jnp.float32) * sd, 'exp_bup': jnp.zeros((E, I), jnp.float32), 'exp_Wg': jax.random.normal(ks[5], (E, I, I), jnp.float32) * sd, 'exp_bg': jnp.zeros((E, I), jnp.float32), 'exp_Wdown': jax.random.normal(ks[6], (E, I, H), jnp.float32) * sd, 'exp_bdown': jnp.zeros((E, H), jnp.float32), 'share_Wup': jax.random.normal(ks[7], (H, NS * I), jnp.float32) * sd, 'share_bup': jnp.zeros((NS * I,), jnp.float32), 'share_Wg': jax.random.normal(ks[8], (I, I), jnp.float32) * sd, 'share_bg': jnp.zeros((I,), jnp.float32), 'share_Wdown': jax.random.normal(ks[9], (I, H), jnp.float32) * sd, 'share_bdown': jnp.zeros((H,), jnp.float32), 'norm_w': jnp.ones((C, H), jnp.float32)}
        return inp
    _L1_ffn_all = _L1_ffn_setup()
    _L1_ffn_in = {k: v for k, v in _L1_ffn_all.items() if k in ('router_W', 'router_b', 'gate_bias', 'exp_Wup', 'exp_bup', 'exp_Wg', 'exp_bg', 'exp_Wdown', 'exp_bdown', 'share_Wup', 'share_bup', 'share_Wg', 'share_bg', 'share_Wdown', 'share_bdown', 'norm_w')}
    del _L1_ffn_all
    return {'x': x, 'itok_B_0_2': itok_B_0_2, 'condB_tauraws': condB_tauraws, 'cond_256': cond_256, 'condB_bn2': condB_bn2, 'cond_1024': cond_1024, 'itok_B_0_7': itok_B_0_7, 'itok_B_0_30': itok_B_0_30, 'L0_cond_W1': _L0_cond_in['W1'], 'L0_cond_b1': _L0_cond_in['b1'], 'L0_cond_v': _L0_cond_in['v'], 'L0_attn_wq': _L0_attn_in['wq'], 'L0_attn_bq': _L0_attn_in['bq'], 'L0_attn_wk': _L0_attn_in['wk'], 'L0_attn_bk': _L0_attn_in['bk'], 'L0_attn_wv': _L0_attn_in['wv'], 'L0_attn_bv': _L0_attn_in['bv'], 'L0_attn_wo': _L0_attn_in['wo'], 'L0_attn_bo': _L0_attn_in['bo'], 'L0_cond2_tau_ctx': _L0_cond2_in['tau_ctx'], 'L0_cond2_Wg': _L0_cond2_in['Wg'], 'L0_cond2_bg': _L0_cond2_in['bg'], 'L0_cond2_Wn1': _L0_cond2_in['Wn1'], 'L0_cond2_bn1': _L0_cond2_in['bn1'], 'L0_cond2_Wsoma': _L0_cond2_in['Wsoma'], 'L0_cond2_bsoma': _L0_cond2_in['bsoma'], 'L0_cond2_Wtemp': _L0_cond2_in['Wtemp'], 'L0_cond2_btemp': _L0_cond2_in['btemp'], 'L0_cond2_Wout': _L0_cond2_in['Wout'], 'L0_cond2_gamma': _L0_cond2_in['gamma'], 'L0_cond2_beta': _L0_cond2_in['beta'], 'L0_ffn_w_gate': _L0_ffn_in['w_gate'], 'L0_ffn_w_up': _L0_ffn_in['w_up'], 'L0_ffn_w_down': _L0_ffn_in['w_down'], 'L1_cond_weight': _L1_cond_in['weight'], 'L1_cond_bias': _L1_cond_in['bias'], 'L1_attn_Wq': _L1_attn_in['Wq'], 'L1_attn_bq': _L1_attn_in['bq'], 'L1_attn_Wk': _L1_attn_in['Wk'], 'L1_attn_bk': _L1_attn_in['bk'], 'L1_attn_Wv': _L1_attn_in['Wv'], 'L1_attn_bv': _L1_attn_in['bv'], 'L1_attn_Wo': _L1_attn_in['Wo'], 'L1_attn_bo': _L1_attn_in['bo'], 'L1_cond2_W': _L1_cond2_in['W'], 'L1_cond2_b': _L1_cond2_in['b'], 'L1_ffn_router_W': _L1_ffn_in['router_W'], 'L1_ffn_router_b': _L1_ffn_in['router_b'], 'L1_ffn_gate_bias': _L1_ffn_in['gate_bias'], 'L1_ffn_exp_Wup': _L1_ffn_in['exp_Wup'], 'L1_ffn_exp_bup': _L1_ffn_in['exp_bup'], 'L1_ffn_exp_Wg': _L1_ffn_in['exp_Wg'], 'L1_ffn_exp_bg': _L1_ffn_in['exp_bg'], 'L1_ffn_exp_Wdown': _L1_ffn_in['exp_Wdown'], 'L1_ffn_exp_bdown': _L1_ffn_in['exp_bdown'], 'L1_ffn_share_Wup': _L1_ffn_in['share_Wup'], 'L1_ffn_share_bup': _L1_ffn_in['share_bup'], 'L1_ffn_share_Wg': _L1_ffn_in['share_Wg'], 'L1_ffn_share_bg': _L1_ffn_in['share_bg'], 'L1_ffn_share_Wdown': _L1_ffn_in['share_Wdown'], 'L1_ffn_share_bdown': _L1_ffn_in['share_bdown'], 'L1_ffn_norm_w': _L1_ffn_in['norm_w']}

def reference(x, itok_B_0_2, condB_tauraws, cond_256, condB_bn2, cond_1024, itok_B_0_7, itok_B_0_30, L0_cond_W1, L0_cond_b1, L0_cond_v, L0_attn_wq, L0_attn_bq, L0_attn_wk, L0_attn_bk, L0_attn_wv, L0_attn_bv, L0_attn_wo, L0_attn_bo, L0_cond2_tau_ctx, L0_cond2_Wg, L0_cond2_bg, L0_cond2_Wn1, L0_cond2_bn1, L0_cond2_Wsoma, L0_cond2_bsoma, L0_cond2_Wtemp, L0_cond2_btemp, L0_cond2_Wout, L0_cond2_gamma, L0_cond2_beta, L0_ffn_w_gate, L0_ffn_w_up, L0_ffn_w_down, L1_cond_weight, L1_cond_bias, L1_attn_Wq, L1_attn_bq, L1_attn_Wk, L1_attn_bk, L1_attn_Wv, L1_attn_bv, L1_attn_Wo, L1_attn_bo, L1_cond2_W, L1_cond2_b, L1_ffn_router_W, L1_ffn_router_b, L1_ffn_gate_bias, L1_ffn_exp_Wup, L1_ffn_exp_bup, L1_ffn_exp_Wg, L1_ffn_exp_bg, L1_ffn_exp_Wdown, L1_ffn_exp_bdown, L1_ffn_share_Wup, L1_ffn_share_bup, L1_ffn_share_Wg, L1_ffn_share_bg, L1_ffn_share_Wdown, L1_ffn_share_bdown, L1_ffn_norm_w):
    import jax
    import jax.numpy as jnp

    def _L0_cond_ref(hidden, W1, b1, v, prompt_type_ids):
        import jax, jax.numpy as jnp
        import numpy as np
        NEG_INF = -1e+30
        B, S, D = hidden.shape
        attn_in = jnp.tanh(jnp.einsum('bsd,da->bsa', hidden, W1) + b1)
        scores = jnp.einsum('bsa,a->bs', attn_in, v)
        idx = jnp.arange(S)
        j = idx[:, None]
        l = idx[None, :]
        prefix_m = l <= j
        postfix_m = l >= j
        cloze_m = l != j
        pt = prompt_type_ids[:, None, None]
        mask = jnp.where(pt == 0, prefix_m[None], jnp.where(pt == 1, postfix_m[None], cloze_m[None]))
        masked_scores = jnp.where(mask, scores[:, None, :], NEG_INF)
        p = jax.nn.softmax(masked_scores, axis=-1)
        cnt = jnp.sum(mask, axis=-1).astype(hidden.dtype)
        pooled = jnp.einsum('bjl,bld->bjd', p, hidden) / cnt[..., None]
        return pooled

    def _L0_attn_ref(x, wq, bq, wk, bk, wv, bv, wo, bo):
        import jax, jax.numpy as jnp
        import numpy as np
        EMBED_DIM = 128
        NUM_HEADS = 16
        HEAD_DIM = EMBED_DIM // NUM_HEADS
        WINDOW = 128
        B, T, C = x.shape
        H, D, W = (NUM_HEADS, HEAD_DIM, WINDOW)

        def proj(w, b):
            return (x @ w.T + b).reshape(B, T, H, D).transpose(0, 2, 1, 3)
        q = proj(wq, bq)
        k = proj(wk, bk)
        v = proj(wv, bv)
        idx = jnp.arange(T)[:, None] + jnp.arange(W)[None, :] - (W - 1)
        valid = idx >= 0
        idxc = jnp.clip(idx, 0, T - 1)
        kw = k[:, :, idxc]
        vw = v[:, :, idxc] * valid[None, None, :, :, None]
        scores = jnp.einsum('bhtd,bhtwd->bhtw', q, kw)
        scores = jnp.where(valid[None, None], scores, 0.0) / np.sqrt(D)
        attn = jax.nn.softmax(scores, axis=-1)
        ctx = jnp.einsum('bhtw,bhtwd->bhtd', attn, vw)
        out = ctx.transpose(0, 2, 1, 3).reshape(B, T, C)
        return out @ wo.T + bo

    def _L0_cond2_ref(x, tau_ctx, tau_raws, Wg, bg, Wn1, bn1, Wn2, bn2, blend, Wsoma, bsoma, Wtemp, btemp, Wout, gamma, beta):
        import jax, jax.numpy as jnp
        import numpy as np
        import math
        B, T, E, D = (4, 256, 128, 4)

        def _tau_init(t):
            a = 0.1 ** (1.0 / max(t - 1, 1))
            tt = -math.log(max(a, 1e-10))
            return math.log(math.exp(tt) - 1 + 1e-10)

        def causal_ema(b, tau_raw):
            alpha = jnp.exp(-jax.nn.softplus(tau_raw)).astype(b.dtype)

            def step(h, bt):
                h = alpha * h + bt
                return (h, h)
            h0 = jnp.zeros((b.shape[0], b.shape[2]), b.dtype)
            _, hs = jax.lax.scan(step, h0, jnp.swapaxes(b, 0, 1))
            return jnp.swapaxes(hs, 0, 1)
        ctx = causal_ema(x, tau_ctx)
        gate_in = jnp.concatenate([x, ctx], axis=-1)
        wg = jax.nn.sigmoid(jnp.einsum('btc,ec->bte', gate_in, Wg) + bg)
        gated = x * wg
        h1 = jax.nn.gelu(jnp.einsum('btc,hc->bth', x, Wn1) + bn1, approximate=False)
        mod = 0.5 + jax.nn.sigmoid(jnp.einsum('bth,dh->btd', h1, Wn2) + bn2)
        traces = jax.vmap(lambda tau, m: causal_ema(gated * m[..., None], tau))(tau_raws, jnp.moveaxis(mod, -1, 0))
        blend_w = jax.nn.softmax(blend, axis=0)
        temporal = jnp.einsum('dbtc,dc->btc', traces, blend_w)
        gate = jax.nn.sigmoid(jnp.einsum('btc,ec->bte', temporal, Wtemp) + btemp)
        soma = jax.nn.gelu(jnp.einsum('btc,ec->bte', x, Wsoma) + bsoma, approximate=False)
        out = jnp.einsum('btc,ec->bte', soma * gate, Wout)
        mu = out.mean(-1, keepdims=True)
        var = out.var(-1, keepdims=True)
        return (out - mu) / jnp.sqrt(var + 1e-05) * gamma + beta

    def _L0_ffn_ref(x, w_gate, w_up, w_down):
        import jax, jax.numpy as jnp
        import numpy as np
        BLOCK = 32
        W_BITS = 4
        ACT_BITS = 16

        def act_qdq(x):
            qmax = 2.0 ** (ACT_BITS - 1) - 1.0
            scale = jnp.maximum(jnp.max(jnp.abs(x)) / qmax, 1e-12)
            return jnp.clip(jnp.round(x / scale), -qmax - 1.0, qmax) * scale

        def fixed_qdq_u16(x):
            scale = 1.0 / 65536.0
            return jnp.clip(jnp.round(x / scale), 0.0, 65535.0) * scale

        def lpbq_dequant(w):
            O, I = w.shape
            qmax = 2.0 ** (W_BITS - 1) - 1.0
            wb = w.reshape(O, I // BLOCK, BLOCK)
            s = jnp.maximum(jnp.max(jnp.abs(wb), axis=-1, keepdims=True) / qmax, 1e-12)
            wq = jnp.clip(jnp.round(wb / s), -qmax - 1.0, qmax) * s
            return wq.reshape(O, I)
        x = act_qdq(x)
        up = act_qdq(x @ lpbq_dequant(w_up).T)
        gate = act_qdq(x @ lpbq_dequant(w_gate).T)
        sig = fixed_qdq_u16(jax.nn.sigmoid(gate))
        gate = act_qdq(gate * sig)
        o = act_qdq(gate * up)
        return o @ lpbq_dequant(w_down).T

    def _L1_cond_ref(x, subject_id, weight, bias):
        import jax, jax.numpy as jnp
        import numpy as np
        S, O, H = (8, 128, 128)
        B, N = (32, 64)
        W = weight[subject_id]
        b = bias[subject_id]
        y = jnp.einsum('bnh,boh->bno', x, W) + b[:, None, :]
        return y

    def _L1_attn_ref(x, Wq, bq, Wk, bk, Wv, bv, Wo, bo):
        import jax, jax.numpy as jnp
        import numpy as np
        DIM = 128
        NUM_HEADS = 16
        HEAD_DIM = DIM // NUM_HEADS
        B, L = (4, 256)

        def _alibi_bias_causal(seq_len, dtype):
            h = jnp.arange(1, NUM_HEADS + 1, dtype=jnp.float32)
            slopes = jnp.power(2.0, -8.0 * h / NUM_HEADS)
            pos = jnp.arange(seq_len, dtype=jnp.float32)
            rel = jnp.abs(pos[:, None] - pos[None, :])
            bias = -slopes[:, None, None] * rel[None, :, :]
            causal = pos[:, None] >= pos[None, :]
            bias = jnp.where(causal[None, :, :], bias, -jnp.inf)
            return bias.astype(dtype)
        b, l, d = x.shape
        q = (jnp.einsum('bld,ed->ble', x, Wq) + bq).reshape(b, l, NUM_HEADS, HEAD_DIM).transpose(0, 2, 1, 3)
        k = (jnp.einsum('bld,ed->ble', x, Wk) + bk).reshape(b, l, NUM_HEADS, HEAD_DIM).transpose(0, 2, 1, 3)
        v = (jnp.einsum('bld,ed->ble', x, Wv) + bv).reshape(b, l, NUM_HEADS, HEAD_DIM).transpose(0, 2, 1, 3)
        scale = 1.0 / np.sqrt(HEAD_DIM)
        scores = jnp.einsum('bhqd,bhkd->bhqk', q, k) * scale
        scores = scores + _alibi_bias_causal(l, scores.dtype)[None]
        attn = jax.nn.softmax(scores, axis=-1)
        out = jnp.einsum('bhqk,bhkd->bhqd', attn, v)
        out = out.transpose(0, 2, 1, 3).reshape(b, l, d)
        return jnp.einsum('bld,ed->ble', out, Wo) + bo

    def _L1_cond2_ref(x, cat_ids, W, b):
        import jax, jax.numpy as jnp
        import numpy as np
        C, I, O = (32, 128, 128)
        B, T = (64, 64)
        selected_W = W[cat_ids]
        selected_b = b[cat_ids]
        if x.ndim == 2:
            return jnp.einsum('bi,bio->bo', x, selected_W) + selected_b
        return jnp.einsum('bti,bio->bto', x, selected_W) + selected_b[:, None, :]

    def _L1_ffn_ref(x, router_W, router_b, gate_bias, exp_Wup, exp_bup, exp_Wg, exp_bg, exp_Wdown, exp_bdown, share_Wup, share_bup, share_Wg, share_bg, share_Wdown, share_bdown, norm_w):
        import jax, jax.numpy as jnp
        import numpy as np
        H, I, E, NS, C = (128, 128, 6, 2, 2)
        TOPK = 2
        TEMP = 1.0
        EPS = 1e-06
        B, S, Hd = x.shape
        xf = x.reshape(-1, Hd)
        for j in range(C):
            residual = xf
            gate = (xf @ router_W[j] + router_b[j]) / TEMP
            biased = gate + gate_bias[j]
            _, ids = jax.lax.top_k(biased, TOPK)
            sel = (ids[:, :, None] == jnp.arange(E)[None, None, :]).any(axis=1)
            weights = jax.nn.softmax(jnp.where(sel, gate, -jnp.inf), axis=-1)
            h = jnp.einsum('nh,ehi->eni', xf, exp_Wup) + exp_bup[:, None, :]
            h = jax.nn.silu(jnp.einsum('eni,eij->enj', h, exp_Wg) + exp_bg[:, None, :]) * h
            eo = jnp.einsum('eni,eih->enh', h, exp_Wdown) + exp_bdown[:, None, :]
            combined = jnp.einsum('ne,enh->nh', weights, eo)
            s = (xf @ share_Wup + share_bup).reshape(-1, NS, I)
            s = jax.nn.silu(s @ share_Wg + share_bg) * s
            share_out = (s @ share_Wdown + share_bdown).sum(axis=1)
            z = combined + share_out
            y = residual + z
            y = y * jax.lax.rsqrt(jnp.mean(y * y, axis=-1, keepdims=True) + EPS) * norm_w[j]
            xf = y
        return xf.reshape(B, S, Hd)
    x = x + _L0_attn_ref(_L0_cond_ref(x, L0_cond_W1, L0_cond_b1, L0_cond_v, itok_B_0_2), L0_attn_wq, L0_attn_bq, L0_attn_wk, L0_attn_bk, L0_attn_wv, L0_attn_bv, L0_attn_wo, L0_attn_bo)
    x = x + _L0_ffn_ref(_L0_cond2_ref(x, L0_cond2_tau_ctx, condB_tauraws, L0_cond2_Wg, L0_cond2_bg, L0_cond2_Wn1, L0_cond2_bn1, cond_256, condB_bn2, cond_1024, L0_cond2_Wsoma, L0_cond2_bsoma, L0_cond2_Wtemp, L0_cond2_btemp, L0_cond2_Wout, L0_cond2_gamma, L0_cond2_beta), L0_ffn_w_gate, L0_ffn_w_up, L0_ffn_w_down)
    x = x + _L1_attn_ref(_L1_cond_ref(x, itok_B_0_7, L1_cond_weight, L1_cond_bias), L1_attn_Wq, L1_attn_bq, L1_attn_Wk, L1_attn_bk, L1_attn_Wv, L1_attn_bv, L1_attn_Wo, L1_attn_bo)
    x = x + _L1_ffn_ref(_L1_cond2_ref(x, itok_B_0_30, L1_cond2_W, L1_cond2_b), L1_ffn_router_W, L1_ffn_router_b, L1_ffn_gate_bias, L1_ffn_exp_Wup, L1_ffn_exp_bup, L1_ffn_exp_Wg, L1_ffn_exp_bg, L1_ffn_exp_Wdown, L1_ffn_exp_bdown, L1_ffn_share_Wup, L1_ffn_share_bup, L1_ffn_share_Wg, L1_ffn_share_bg, L1_ffn_share_Wdown, L1_ffn_share_bdown, L1_ffn_norm_w)
    return x

_drawn_inputs = setup_inputs


def setup_inputs(seed=0):
    import zlib

    import numpy as np

    out = dict(_drawn_inputs(seed))
    spreads = {'condB_bn2': (0.0, 0.8),
     'L0_attn_bq': (0.0, 0.8),
     'L0_attn_bk': (0.0, 0.8),
     'L0_attn_bv': (0.0, 0.471),
     'L0_attn_bo': (0.0, 0.1),
     'L0_cond2_bg': (-0.5, 0.6),
     'L0_cond2_bn1': (0.0, 0.8),
     'L0_cond2_bsoma': (0.0, 0.731),
     'L0_cond2_btemp': (0.0, 0.8),
     'L0_cond2_gamma': (1.0, 0.6),
     'L0_cond2_beta': (0.0, 0.8),
     'L1_cond2_b': (0.0, 0.441),
     'L1_ffn_exp_bup': (0.0, 2.0),
     'L1_ffn_exp_bg': (0.0, 2.0),
     'L1_ffn_exp_bdown': (0.0, 2.0),
     'L1_ffn_share_bup': (0.0, 0.8),
     'L1_ffn_share_bg': (0.0, 2.0),
     'L1_ffn_share_bdown': (0.0, 2.0),
     'L1_ffn_norm_w': (1.0, 0.54)}
    factors = {'condB_tauraws': 8.0,
     'cond_256': 8.0,
     'cond_1024': 8.0,
     'L0_cond_W1': 8.0,
     'L0_cond_b1': 8.0,
     'L0_cond_v': 8.0,
     'L0_attn_wq': 8.0,
     'L0_attn_wk': 8.0,
     'L0_attn_wv': 5.143,
     'L0_attn_wo': 3.302,
     'L0_cond2_Wg': 8.0,
     'L0_cond2_Wn1': 8.0,
     'L0_cond2_Wsoma': 4.079,
     'L0_cond2_Wtemp': 8.0,
     'L0_cond2_Wout': 4.047,
     'L0_ffn_w_gate': 3.877,
     'L0_ffn_w_up': 3.785,
     'L0_ffn_w_down': 3.907,
     'L1_cond_weight': 3.938,
     'L1_cond_bias': 8.0,
     'L1_attn_Wq': 8.0,
     'L1_attn_bq': 8.0,
     'L1_attn_Wk': 8.0,
     'L1_attn_bk': 200.0,
     'L1_attn_Wv': 3.73,
     'L1_attn_bv': 31.17,
     'L1_attn_Wo': 3.758,
     'L1_ffn_exp_Wup': 8.0,
     'L1_ffn_exp_Wg': 8.0,
     'L1_ffn_exp_Wdown': 8.0,
     'L1_ffn_share_Wup': 8.0,
     'L1_ffn_share_Wg': 8.0,
     'L1_ffn_share_Wdown': 8.0,
     'L1_attn_bo': 24.315,
     'L1_ffn_router_b': 4.745,
     'L1_ffn_gate_bias': 4.153}
    for name, (base, spread) in spreads.items():
        noise = np.random.default_rng([zlib.crc32(name.encode()), seed]).standard_normal(out[name].shape)
        drawn = base * np.exp(spread * noise) if base else spread * noise
        out[name] = jnp.asarray(drawn.astype(out[name].dtype))
    for name, factor in factors.items():
        out[name] = (out[name] * factor).astype(out[name].dtype)
    return out
```

```python
import numpy as np
import concourse.bass as bass
from concourse import mybir
from contextlib import ExitStack

B, S, D = 64, 32, 128
N = B * S
P = 128
TILES = N // P
CH = 4
CT = N // CH
TPC = CT // P
CB = CT // S
HEADS, HD = 16, 8
G, HG = 4, 4
WINDOW = 128
TR = 64
F = 384
FT = F // P
QB = 32
NSUB, NCAT = 8, 32
E = 6
NEG = 1e30
STAGE = 5
MAGIC = 12582912.0
QMAX = 32767.0

CONST = [("ident", P), ("alibi", HG * S), ("causal", S), ("pre", S), ("post", S), ("cloze", S),
         ("empty", 1), ("hmask", HG), ("gmask", G), ("index", 1), ("tri", E * E), ("ones", P), ("magic", 1)]
COND = [("W1", 32), ("b1", 1), ("vrep", P), ("blend", 2 * TR), ("tau_raws", 1), ("tau_ctx", 1)]
ATTN = [("wq", P), ("wk", P), ("wv", P), ("wo", P), ("bv", P), ("bq", 1), ("bk", 1), ("bo", 1)]
CTX = [("Wg0", P), ("Wg1", P), ("Wsoma", P), ("Wtemp", P), ("Wout", P), ("Wn1", 32), ("Wn2", P),
       ("bg", 1), ("bn1", 1), ("bn2", 1), ("bsoma", 1), ("btemp", 1), ("gamma", 1), ("beta", 1)]
FFN = [("up", FT * P), ("gate", FT * P), ("down", FT * P)]
SEL = [("bias1", P), ("bias2", P)]
MOE = [("Wup", E * P), ("Wgt", E * P), ("Wdn", E * P), ("Sup", 2 * P), ("Sgt", P), ("Sdn", P),
       ("bdn", P), ("norm", 2 * P), ("rW", 2 * E), ("rb", 2 * E), ("gb", 2 * E),
       ("bup", E), ("bgt", E), ("sbup", 2), ("sbgt", 1)]
INTS = [("prompt", TILES), ("subject", B), ("category", B)]


def width(fields):
    return sum(w for _, w in fields)


def lags():
    out = []
    for lag in range(S):
        valid = S - lag
        even = valid + valid % 2
        nb = min(B, CT // S * (S // (1 << (even - 1).bit_length())))
        for b in range(0, B, nb):
            out.append((lag, b, nb, even, valid))
    return out


def program(nc, consts, cond, attn0, ctx_w, ffn_w, attn1, sel_w, moe_w, ints, x_fm, x_tm, w_subject, w_category,
            out, stage=9):
    f32, f32r, i32 = mybir.dt.float32, mybir.dt.float32r, mybir.dt.int32
    ALU, ACT, AX = mybir.AluOpType, mybir.ActivationFunctionType, mybir.AxisListType
    es = ExitStack()
    with es:
        def sb(name, cols, dt=f32):
            return es.enter_context(nc.sbuf_tensor(name, [P, cols], dt))

        def sem(name):
            return es.enter_context(nc.semaphore(name))

        def fields(t, spec):
            at, found = 0, {}
            for name, w in spec:
                found[name] = t[:, at:at + w]
                at += w
            return found

        def over(ap, axis, n):
            ap = ap.unsqueeze(axis)
            shape = list(ap.shape)
            shape[axis] = n
            return ap.broadcast_to(shape)

        t_const, t_cond = sb("t_const", width(CONST)), sb("t_cond", width(COND))
        t_attn = [sb("t_attn0", width(ATTN)), sb("t_attn1", width(ATTN))]
        t_ctx, t_ffn, t_sel = sb("t_ctx", width(CTX)), sb("t_ffn", width(FFN)), sb("t_sel", width(SEL))
        t_moe, t_int = sb("t_moe", width(MOE)), sb("t_int", width(INTS), i32)
        K, C0, W2, FW = fields(t_const, CONST), fields(t_cond, COND), fields(t_ctx, CTX), fields(t_ffn, FFN)
        AW = [fields(t, ATTN) for t in t_attn]
        SW, MW, IN = fields(t_sel, SEL), fields(t_moe, MOE), fields(t_int, INTS)
        X = sb("X", N)
        H = sb("H", N)
        chosen = sb("chosen", B * P)
        x_tok = chosen[:, S * P:S * P + N]
        powers = sb("powers", S * P, f32r)
        mod_high, mod_low = sb("mod_high", N, f32r), sb("mod_low", N, f32r)
        wT = sb("wT", 3 * FT * P)
        small = sb("small", 1280)
        ARENA = 21504
        arena = sb("arena", ARENA)
        PS = es.enter_context(nc.psum_tensor("PS", [P, 8 * CT], f32))

        def bank(i, n=1):
            return PS[:, i * CT:(i + n) * CT]

        def chunk(t, c):
            return t[:, c * CT:(c + 1) * CT]

        small_at, arena_at = [0], [0]

        def cols(n):
            small_at[0] += n
            assert small_at[0] <= 1280
            return small[:, small_at[0] - n:small_at[0]]

        def region(n):
            arena_at[0] += n
            assert arena_at[0] <= ARENA, arena_at
            return arena[:, arena_at[0] - n:arena_at[0]]

        l_const, l_x, l_int, l_attn0, l_ctx, l_ffn, l_attn1, l_sel, l_moe = [
            sem("loaded_" + n) for n in ("const", "x", "int", "attn0", "ctx", "ffn", "attn1", "sel", "moe")]
        chosen1, chosen2 = sem("chosen1_loaded"), sem("chosen2_loaded")
        dve_step = sem("dve_step")
        stored = [sem("stored_even"), sem("stored_odd")]

        vector_steps = [0]

        def note(ins):
            vector_steps[0] += 1
            ins.then_inc(dve_step, 1)

        def join():
            nc.vector.wait_ge(dve_step, vector_steps[0])

        def link(ins):
            note(ins)
            join()

        def mk(stage_name, *what):
            return {w: sem(stage_name + "_" + w) for w in what}

        a = mk("pool", "tanh_ps", "tanh", "score_ps", "masked", "exped", "mats", "zeroed", "ps", "h", "blend_max", "blend_exp",
               "power", "power0", "powers", "split")
        at = [mk(f"attn{i}", "zeroed", "q_ps", "k_ps", "v_ps", "qk", "v_act", "v_dve", "s_ps", "biased", "maxed",
                 "shifted", "exped", "recip", "normed", "probT", "o_ps", "o", "y_ps", "y", "scales", "emd") for i in range(2)]
        c2 = mk("ctx", "ones", "h1_ps", "h1", "soma_ps", "soma", "scanned", "wg_ps", "wg", "gated", "mod_ps",
                "mod", "mod_split", "zeroed", "lag_ps", "prod", "added", "temporal", "gate_ps", "gate", "somagate", "out_ps",
                "xc", "sq", "var", "std", "y", "y_ps", "yt", "bT_ps")
        ff = mk("ffn", "w", "wT_ps", "wT", "amax", "amaxT_ps", "gmax", "gmaxb_ps", "scale", "hq", "up_ps", "copied",
                "magic", "uq", "gq", "sig", "om", "o", "down_ps", "x")
        l1 = mk("sub", "hot", "ps", "tok", "tr_ps", "h")
        l2 = mk("cat", "hot", "ps", "tok", "tr_ps", "h")
        mo = mk("moe", "logit_ps", "logit", "masked", "exped", "w", "wT_ps", "wT", "up_ps", "h", "gt_ps", "s", "hh",
                "dn_ps", "eo", "acc_ps", "y", "sq", "ss", "rstd", "normed", "tr_ps", "xf", "fin", "half")

        block = es.enter_context(nc.Block())

        arena_at[0] = 0
        TH = region(N)
        MASK, NEGM, SC, EX = region(CT), region(CT), region(CT), region(CT)
        TMPM = region(CT)
        MATS = region(N)
        POW = chosen[:, 0:S * P]
        pt = cols(TILES); e0 = cols(TILES); e1 = cols(TILES); e2 = cols(TILES)
        pcnt, pmax, psum_ = cols(TILES), cols(TILES), cols(TILES)
        alpha = cols(1); alpha_t = cols(1); alpha_c = cols(1); alpha_ct = cols(1)
        bmax = cols(1); bsum = cols(1)
        arena_at[0] = 0
        Q2, K2, V2 = ([region(CB * P) for _ in range(2)] for _ in range(3))
        S2, T2 = ([region(CB * P) for _ in range(2)] for _ in range(2))
        OT = [region(CT) for _ in range(2)]
        qscale, qbias, kbias = cols(G), cols(G), cols(HG)
        NR = CB * HG
        smax, ssum, semt = ([cols(NR) for _ in range(2)] for _ in range(3))

        def qv(t):
            return t.rearrange("p (b g s) -> p b g s", b=CB, g=G)

        def pooling_pe(pe):
            pe.wait_ge(l_const, 32)
            pe.wait_ge(l_x, 32)
            for c in range(CH):
                pe.matmul(bank(c)[0:32, :], C0["W1"], chunk(X, c), start=True, stop=True).then_inc(a["tanh_ps"], 1)
            for c in range(CH):
                pe.wait_ge(a["tanh"], c + 1)
                pe.matmul(bank(4 + c), C0["vrep"][0:32, :], TH[0:32, c * CT:(c + 1) * CT], start=True, stop=True)\
                    .then_inc(a["score_ps"], 1)
            pe.wait_ge(a["mats"], 4)
            for t in range(TILES):
                ins = pe.matmul(PS[:, t * P:(t + 1) * P], x_tok[:, t * P:(t + 1) * P], MATS[:, t * P:(t + 1) * P],
                                start=True, stop=True)
                if t % TPC == TPC - 1:
                    ins.then_inc(a["ps"], 1)
            pe.wait_ge(a["blend_exp"], 1)
            pe.transpose(bank(4)[:, 0:P], C0["blend"], K["ident"]).then_inc(c2["bT_ps"], 1)

        def pooling_act(act):
            act.wait_ge(l_const, 32)
            for c in range(CH):
                act.wait_ge(a["tanh_ps"], c + 1)
                act.activation(TH[0:32, c * CT:(c + 1) * CT], bank(c)[0:32, :], ACT.Tanh, bias=C0["b1"][0:32, :])\
                    .then_inc(a["tanh"], 1)
            act.activation(alpha_t, C0["tau_raws"], ACT.Exp).then_inc(a["power"], 1)
            act.activation(alpha_ct, C0["tau_ctx"], ACT.Exp).then_inc(a["power"], 1)
            act.wait_ge(a["blend_max"], 1)
            act.activation(C0["blend"], C0["blend"], ACT.Exp).then_inc(a["exped"], 1)
            act.wait_ge(a["masked"], 1)
            act.activation(EX, SC, ACT.Exp).then_inc(a["exped"], 1)
            for c in range(CH):
                act.wait_ge(a["ps"], c + 1)
                act.activation(chunk(H, c), bank(c), ACT.Copy).then_inc(a["h"], 1)

        def pooling_pool(pool):
            pool.memset(MATS, 0.0).then_inc(a["zeroed"], 1)
            pool.memset(V2[0], 0.0).then_inc(at[0]["zeroed"], 1)
            pool.memset(V2[1], 0.0).then_inc(at[0]["zeroed"], 1)
            pool.wait_ge(a["power0"], 1)
            for lag in range(1, S):
                pool.tensor_scalar(POW[:, lag * P:(lag + 1) * P], POW[:, (lag - 1) * P:lag * P], alpha, None, ALU.mult)\
                    .then_inc(a["powers"], 1)
                pool.wait_ge(a["powers"], lag)

        def pooling_dve(dve):
            dve.wait_ge(l_const, 32)
            link(dve.tensor_reduce(bmax, C0["blend"][:, 0:TR], AX.X, ALU.max))
            dve.tensor_scalar(C0["blend"], C0["blend"], bmax, None, ALU.subtract).then_inc(a["blend_max"], 1)
            dve.wait_ge(a["power"], 2)
            link(dve.tensor_scalar(alpha_t, alpha_t, 1.0, None, ALU.add))
            link(dve.reciprocal(alpha, alpha_t))
            link(dve.tensor_scalar(alpha_ct, alpha_ct, 1.0, None, ALU.add))
            link(dve.reciprocal(alpha_c, alpha_ct))
            dve.wait_ge(a["exped"], 1)
            link(dve.tensor_reduce(bsum, C0["blend"][:, 0:TR], AX.X, ALU.add))
            link(dve.reciprocal(bsum, bsum))
            dve.tensor_scalar(C0["blend"], C0["blend"], bsum, None, ALU.mult).then_inc(a["blend_exp"], 1)
            dve.wait_ge(l_int, 16)
            link(dve.tensor_copy(pt, IN["prompt"]))
            note(dve.tensor_scalar(e0, pt, 0.0, None, ALU.is_equal))
            link(dve.tensor_scalar(e1, pt, 1.0, None, ALU.is_equal))
            link(dve.tensor_tensor(e2, e0, e1, ALU.add))
            link(dve.tensor_scalar(e2, e2, -1.0, 1.0, ALU.mult, ALU.add))
            m3 = MASK.rearrange("p (t s) -> p t s", t=TILES)
            tmp3 = TMPM.rearrange("p (t s) -> p t s", t=TILES)
            link(dve.tensor_tensor(m3, over(K["pre"], 1, TILES), over(e0, 2, S), ALU.mult))
            link(dve.tensor_tensor(tmp3, over(K["post"], 1, TILES), over(e1, 2, S), ALU.mult))
            link(dve.tensor_tensor(MASK, MASK, TMPM, ALU.add))
            link(dve.tensor_tensor(tmp3, over(K["cloze"], 1, TILES), over(e2, 2, S), ALU.mult))
            link(dve.tensor_tensor(MASK, MASK, TMPM, ALU.add))
            link(dve.tensor_reduce(pcnt, m3, AX.X, ALU.add))
            link(dve.tensor_scalar(NEGM, MASK, 1.0, NEG, ALU.subtract, ALU.mult))
            dve.wait_ge(a["score_ps"], CH)
            sc3 = SC.rearrange("p (t s) -> p t s", t=TILES)
            ps3 = bank(4, 4).rearrange("p (t q s) -> p t q s", t=TILES, q=4)
            for q in range(4):
                r = slice(32 * q, 32 * q + 32)
                note(dve.tensor_tensor(sc3[r], ps3[r, :, q, :], m3[r], ALU.mult))
            join()
            link(dve.tensor_tensor(SC, SC, NEGM, ALU.add))
            link(dve.tensor_reduce(pmax, sc3, AX.X, ALU.max))
            dve.tensor_tensor(sc3, sc3, over(pmax, 2, S), ALU.subtract).then_inc(a["masked"], 1)
            dve.wait_ge(a["exped"], 2)
            ex3 = EX.rearrange("p (t s) -> p t s", t=TILES)
            link(dve.tensor_reduce(psum_, ex3, AX.X, ALU.add))
            link(dve.tensor_tensor(psum_, psum_, pcnt, ALU.mult))
            link(dve.reciprocal(psum_, psum_))
            link(dve.tensor_tensor(ex3, ex3, over(psum_, 2, S), ALU.mult))
            dve.wait_ge(a["zeroed"], 1)
            mats = MATS.rearrange("p (t q s) -> p t q s", t=TILES, q=4)
            for q in range(4):
                r = slice(32 * q, 32 * q + 32)
                dve.transpose(mats[r, :, q, :], ex3[r]).then_inc(a["mats"], 1)
            dve.wait_ge(c2["bT_ps"], 1)
            dve.tensor_copy(POW[:, 0:P], bank(4)[:, 0:P]).then_inc(a["power0"], 1)

        def attention_pe(pe, i, src_ready):
            s, w = at[i], AW[i]
            pe.wait_ge((l_attn0, l_attn1)[i], 16)

            def project(c):
                src_ready(pe, c)
                if c:
                    pe.wait_ge(s["qk"], c)
                pe.matmul(bank(0), w["wq"], chunk(H, c), start=True, stop=True).then_inc(s["q_ps"], 1)
                pe.matmul(bank(1), w["wk"], chunk(H, c), start=True, stop=True).then_inc(s["k_ps"], 1)
                if c:
                    pe.wait_ge(s["v_act"], c)
                    pe.wait_ge(s["v_dve"], c)
                pe.matmul(bank(2), K["ones"][0:1, :], over(w["bv"][0:1, :], 1, TPC), start=True, stop=False)
                for t in range(TPC):
                    ins = pe.matmul(bank(2)[:, t * P:(t + 1) * P], H[:, c * CT + t * P:c * CT + (t + 1) * P], w["wv"],
                                    start=False, stop=t == TPC - 1)
                ins.then_inc(s["v_ps"], 1)
                pe.wait_ge(s["qk"], c + 1)
                for b in range(CB):
                    if b % 4 == 0 and c:
                        pe.wait_ge(s["biased"], 4 * (c - 1) + b // 4 + 1)
                    r = slice(b * P, (b + 1) * P)
                    ins = pe.matmul(PS[:, 3 * CT + b * P:3 * CT + (b + 1) * P], Q2[c % 2][:, r], K2[c % 2][:, r],
                                    start=True, stop=True)
                    if b % 4 == 3:
                        ins.then_inc(s["s_ps"], 1)

            def mix(c):
                pe.wait_ge(s["probT"], c + 1)
                pe.wait_ge(s["v_act"], c + 1)
                pe.wait_ge(s["v_dve"], c + 1)
                if c:
                    pe.wait_ge(s["y"], c)
                for b in range(CB):
                    for h in range(HG):
                        r = slice(b * P + h * S, b * P + (h + 1) * S)
                        ins = pe.matmul(bank(7)[32 * h:32 * h + 32, b * S:(b + 1) * S], V2[c % 2][:, r], T2[c % 2][:, r],
                                        start=True, stop=True, tile_position=(0, 32 * h))
                ins.then_inc(s["o_ps"], 1)
                pe.wait_ge(s["o"], c + 1)
                pe.matmul(bank(7), w["wo"], OT[c % 2], start=True, stop=True).then_inc(s["y_ps"], 1)

            for c in range(CH + 1):
                if c < CH:
                    project(c)
                if c:
                    mix(c - 1)

        def attention_act(act, i):
            s, w = at[i], AW[i]

            def evacuate(c):
                if c == 0:
                    act.wait_ge(s["scales"], 1)
                if c >= 2:
                    act.wait_ge(s["s_ps"], 4 * (c - 1))
                act.wait_ge(s["q_ps"], c + 1)
                q = bank(0).rearrange("p (b s) -> p b s", b=CB)
                for g in range(G):
                    act.activation(qv(Q2[c % 2])[:, :, g, :], q, ACT.Identity, bias=qbias[:, g:g + 1],
                                   scale=qscale[:, g:g + 1])
                act.wait_ge(s["k_ps"], c + 1)
                k = bank(1).rearrange("p (b s) -> p b s", b=CB)
                for h in range(HG):
                    ins = act.activation(qv(K2[c % 2])[:, :, h, :], k, ACT.Identity, bias=kbias[:, h:h + 1],
                                         scale=K["hmask"][:, h:h + 1])
                ins.then_inc(s["qk"], 1)
                move_v(act, s, c, 0, s["v_act"])

            def finish(c):
                act.wait_ge(s["o_ps"], c + 1)
                act.activation(OT[c % 2], bank(7), ACT.Copy).then_inc(s["o"], 1)

            for c in range(CH + 2):
                if c >= 2:
                    finish(c - 2)
                if c < CH:
                    evacuate(c)
                if 1 <= c <= CH:
                    act.wait_ge(s["shifted"], c)
                    act.activation(S2[(c - 1) % 2], S2[(c - 1) % 2], ACT.Exp).then_inc(s["exped"], 1)
                if i == 0 and 1 <= c <= CH:
                    act.activation(semt[(c - 1) % 2], smax[(c - 1) % 2], ACT.Exp, scale=-1.0).then_inc(s["emd"], 1)

        def move_v(eng, s, c, half, done):
            if c == 0:
                eng.wait_ge(s["zeroed"], 2)
            if c >= 2:
                eng.wait_ge(s["o_ps"], c - 1)
            eng.wait_ge(s["v_ps"], c + 1)
            v = bank(2).rearrange("p (t g h d) -> p t g h d", t=TPC, g=G, h=HG)
            dst = V2[c % 2].rearrange("p (t q h g d) -> p t q h g d", t=TPC, q=4, h=HG, g=G)
            for q in range(2 * half, 2 * half + 2):
                for g in range(G):
                    o, n = dst[32 * g:32 * g + 32, :, q, :, g, :], v[32 * q:32 * q + 32, :, g, :, :]
                    ins = eng.activation(o, n, ACT.Copy) if half == 0 else eng.tensor_copy(o, n)
            ins.then_inc(done, 1)

        def attention_pool(pool, i):
            s = at[i]
            if i == 1:
                pool.wait_ge(l1["tok"], CH)
                pool.memset(V2[0], 0.0).then_inc(s["zeroed"], 1)
                pool.memset(V2[1], 0.0).then_inc(s["zeroed"], 1)
            for c in range(CH):
                rows = S2[c % 2].rearrange("p (r s) -> p r s", s=S)
                pool.wait_ge(s["maxed"], c + 1)
                pool.tensor_tensor(rows, rows, over(smax[c % 2], 2, S), ALU.subtract).then_inc(s["shifted"], 1)
                pool.wait_ge(s["recip"], c + 1)
                pool.tensor_tensor(rows, rows, over(ssum[c % 2], 2, S), ALU.mult).then_inc(s["normed"], 1)

        def attention_dve(dve, i):
            s, w = at[i], AW[i]
            dve.wait_ge((l_attn0, l_attn1)[i], 16)
            scale = 1.0 / float(np.sqrt(HD))
            note(dve.tensor_scalar(kbias, K["hmask"], w["bk"], None, ALU.mult))
            link(dve.tensor_scalar(qscale, K["gmask"], scale, None, ALU.mult))
            dve.tensor_scalar(qbias, qscale, w["bq"], None, ALU.mult).then_inc(s["scales"], 1)

            def scores(c):
                move_v(dve, s, c, 1, s["v_dve"])
                if c >= 2:
                    dve.wait_ge(s["probT"], c - 1)
                for n in range(4):
                    dve.wait_ge(s["s_ps"], 4 * c + n + 1)
                    rows = S2[c % 2][:, n * CT:(n + 1) * CT]
                    if i == 0:
                        o = rows.rearrange("p (r s) -> p r s", s=S)
                        p_ = bank(3 + n).rearrange("p (r s) -> p r s", s=S)
                        bias = over(K["causal"], 1, 4 * HG)
                    else:
                        o = rows.rearrange("p (b r) -> p b r", b=4)
                        p_ = bank(3 + n).rearrange("p (b r) -> p b r", b=4)
                        bias = over(K["alibi"], 1, 4)
                    dve.tensor_tensor(o, p_, bias, ALU.add).then_inc(s["biased"], 1)
                dve.wait_ge(s["biased"], 4 * c + 4)
                rows = S2[c % 2].rearrange("p (r s) -> p r s", s=S)
                if i == 0:
                    link(dve.tensor_reduce(smax[c % 2], rows, AX.X, ALU.max))
                    dve.tensor_scalar(smax[c % 2], smax[c % 2], 0.0, None, ALU.max).then_inc(s["maxed"], 1)
                else:
                    dve.tensor_reduce(smax[c % 2], rows, AX.X, ALU.max).then_inc(s["maxed"], 1)

            def sums(c):
                rows = S2[c % 2].rearrange("p (r s) -> p r s", s=S)
                dve.wait_ge(s["exped"], c + 1)
                link(dve.tensor_reduce(ssum[c % 2], rows, AX.X, ALU.add))
                if i == 0:
                    dve.wait_ge(s["emd"], c + 1)
                    link(dve.scalar_tensor_tensor(ssum[c % 2], semt[c % 2], K["empty"], ssum[c % 2], ALU.mult, ALU.add))
                dve.reciprocal(ssum[c % 2], ssum[c % 2]).then_inc(s["recip"], 1)

            def transpose(c):
                dve.wait_ge(s["normed"], c + 1)
                if c >= 2:
                    dve.wait_ge(s["o_ps"], c - 1)
                dve.transpose(T2[c % 2], S2[c % 2]).then_inc(s["probT"], 1)

            def residual(c):
                dve.wait_ge(s["y_ps"], c + 1)
                dve.scalar_tensor_tensor(chunk(X, c), bank(7), w["bo"], chunk(X, c), ALU.add, ALU.add).then_inc(s["y"], 1)

            for c in range(CH + 2):
                if c < CH:
                    scores(c)
                if 1 <= c <= CH:
                    sums(c - 1)
                if c >= 2:
                    residual(c - 2)
                if 1 <= c <= CH:
                    transpose(c - 1)


        arena_at[0] = 0
        COEF, CTXT, WG, MOD, H1, SOMA, GATED, TPOOL, TDVE = (region(N) for _ in range(9))
        PP, PD = [region(CT) for _ in range(4)], [region(CT) for _ in range(2)]
        XC, SQ, YL, GATE, SOMAG = COEF, CTXT, GATED, WG, MOD
        nmean, nvar, nstd = cols(TILES), cols(TILES), cols(TILES)
        LAGS = lags()
        ON_DVE = [u % 3 == 2 for u in range(len(LAGS))]

        def ctx_pe(pe):
            pe.wait_ge(l_ctx, 16)
            pe.wait_ge(at[0]["y"], CH)
            for c in range(CH):
                pe.matmul(bank(c)[0:32, :], W2["Wn1"], chunk(X, c), start=True, stop=True).then_inc(c2["h1_ps"], 1)
            for c in range(CH):
                pe.matmul(bank(4 + c), W2["Wsoma"], chunk(X, c), start=True, stop=True).then_inc(c2["soma_ps"], 1)
            for c in range(CH):
                pe.wait_ge(c2["h1"], c + 1)
                pe.matmul(bank(c), W2["Wg0"], chunk(X, c), start=True, stop=False)
                pe.wait_ge(c2["scanned"], 1)
                pe.matmul(bank(c), W2["Wg1"], chunk(CTXT, c), start=False, stop=True).then_inc(c2["wg_ps"], 1)
            for c in range(CH):
                pe.wait_ge(c2["soma"], c + 1)
                pe.matmul(bank(4 + c), W2["Wn2"][0:32, :], H1[0:32, c * CT:(c + 1) * CT], start=True, stop=True)\
                    .then_inc(c2["mod_ps"], 1)
            pe.wait_ge(c2["mod_split"], 1)
            pe.wait_ge(c2["wg"], CH)
            pe.wait_ge(a["split"], 1)
            for u, (lag, b0, nb, even, valid) in enumerate(LAGS):
                if u >= 8:
                    pe.wait_ge(c2["prod"], u - 7)
                w = powers[:, lag * P:(lag + 1) * P]
                o = bank(u % 8)[:, 0:nb * even]
                for part in (mod_high, mod_low):
                    r = part[:, :].rearrange("p (b s) -> p b s", b=B)[:, b0:b0 + nb, 0:even]
                    ins = pe.matmul(o, w, r, start=part is mod_high, stop=part is mod_low)
                ins.then_inc(c2["lag_ps"], 1)
            for c in range(CH):
                pe.wait_ge(c2["temporal"], 1)
                pe.matmul(bank(c), W2["Wtemp"], chunk(TPOOL, c), start=True, stop=True).then_inc(c2["gate_ps"], 1)
            for t in range(TILES):
                if t % TPC == 0:
                    pe.wait_ge(c2["somagate"], t // TPC + 1)
                ins = pe.matmul(PS[:, 4 * CT + t * P:4 * CT + (t + 1) * P], SOMAG[:, t * P:(t + 1) * P], W2["Wout"],
                                start=True, stop=True)
                if t % TPC == TPC - 1:
                    ins.then_inc(c2["out_ps"], 1)
            pe.wait_ge(c2["gate"], CH)
            pe.wait_ge(ff["w"], 1)
            for k in range(3 * FT):
                ins = pe.transpose(PS[:, k * P:(k + 1) * P], t_ffn[:, k * P:(k + 1) * P], K["ident"])
            ins.then_inc(ff["wT_ps"], 1)
            pe.wait_ge(ff["wT"], 1)
            pe.wait_ge(c2["y"], 1)
            for t in range(TILES):
                ins = pe.transpose(PS[:, t * P:(t + 1) * P], YL[:, t * P:(t + 1) * P], K["ident"])
                if t % TPC == TPC - 1:
                    ins.then_inc(c2["y_ps"], 1)

        def ctx_act(act):
            for c in range(CH):
                act.wait_ge(c2["h1_ps"], c + 1)
                act.activation(H1[0:32, c * CT:(c + 1) * CT], bank(c)[0:32, :], ACT.Gelu, bias=W2["bn1"][0:32, :])\
                    .then_inc(c2["h1"], 1)
            for c in range(CH):
                act.wait_ge(c2["soma_ps"], c + 1)
                act.activation(chunk(SOMA, c), bank(4 + c), ACT.Gelu, bias=W2["bsoma"]).then_inc(c2["soma"], 1)
            for c in range(CH):
                act.wait_ge(c2["wg_ps"], c + 1)
                act.activation(chunk(WG, c), bank(c), ACT.Sigmoid, bias=W2["bg"]).then_inc(c2["wg"], 1)
            for c in range(CH):
                act.wait_ge(c2["mod_ps"], c + 1)
                act.activation(chunk(MOD, c), bank(4 + c), ACT.Sigmoid, bias=W2["bn2"]).then_inc(c2["mod"], 1)
            act.wait_ge(c2["gated"], 1)
            for c in range(CH):
                act.wait_ge(c2["gate_ps"], c + 1)
                act.activation(chunk(GATE, c), bank(c), ACT.Sigmoid, bias=W2["btemp"]).then_inc(c2["gate"], 1)
            act.wait_ge(ff["wT_ps"], 1)
            act.activation(wT[:, :], PS[:, 0:3 * FT * P], ACT.Copy).then_inc(ff["wT"], 1)
            act.wait_ge(c2["xc"], 1)
            act.activation(SQ, XC, ACT.Square).then_inc(c2["sq"], 1)
            act.wait_ge(c2["var"], 1)
            act.activation(nstd, nvar, ACT.Sqrt).then_inc(c2["std"], 1)
            for c in range(CH):
                act.wait_ge(c2["y_ps"], c + 1)
                act.activation(chunk(H, c), bank(c), ACT.Identity, bias=W2["beta"], scale=W2["gamma"]).then_inc(c2["yt"], 1)

        def ctx_pool(pool):
            pool.wait_ge(at[0]["y"], CH)
            first = COEF.rearrange("p (b s) -> p b s", s=S)
            pool.memset(first[:, :, 1:S], 1.0).then_inc(c2["ones"], 1)
            pool.memset(first[:, :, 0:1], 0.0).then_inc(c2["ones"], 1)
            pool.memset(TPOOL, 0.0).then_inc(c2["zeroed"], 1)
            pool.memset(TDVE, 0.0).then_inc(c2["zeroed"], 1)
            t3 = TPOOL.rearrange("p (b s) -> p b s", s=S)
            k = 0
            for u, (lag, b0, nb, even, valid) in enumerate(LAGS):
                if ON_DVE[u]:
                    continue
                pool.wait_ge(c2["prod"], u + 1)
                if k:
                    pool.wait_ge(c2["added"], k)
                else:
                    pool.wait_ge(c2["zeroed"], 2)
                o = t3[:, b0:b0 + nb, lag:S]
                pool.tensor_tensor(o, o, PP[k % 4][:, 0:nb * valid].rearrange("p (b s) -> p b s", b=nb), ALU.add)\
                    .then_inc(c2["added"], 1)
                k += 1

        def powers_dve(dve):
            dve.wait_ge(a["powers"], S - 1)
            link(dve.tensor_copy(powers[:, :], POW))
            dve.tensor_tensor(powers[TR:P, :], POW[TR:P], powers[TR:P, :].bitcast(f32), ALU.subtract).then_inc(a["split"], 1)

        def ctx_dve(dve):
            dve.wait_ge(c2["ones"], 2)
            link(dve.tensor_scalar(COEF, COEF, alpha_c, None, ALU.mult))
            dve.tensor_tensor_scan(CTXT, COEF, X[:, :], 0.0, ALU.mult, ALU.add).then_inc(c2["scanned"], 1)
            dve.wait_ge(l_ffn, 16)
            nb = 3 * FT * P // QB
            wb = t_ffn[:, :].rearrange("p (n b) -> p n b", b=QB)
            link(dve.tensor_reduce(wscale, wb, AX.X, ALU.max, apply_absolute_value=True))
            link(dve.tensor_scalar(wscale, wscale, 1.0 / 7.0, 1e-12, ALU.mult, ALU.max))
            link(dve.reciprocal(winv, wscale))
            link(dve.tensor_tensor(wb, wb, over(winv, 2, QB), ALU.mult))
            link(dve.tensor_scalar(t_ffn[:, :], t_ffn[:, :], MAGIC, MAGIC + 7.0, ALU.add, ALU.min))
            link(dve.tensor_scalar(t_ffn[:, :], t_ffn[:, :], MAGIC - 8.0, MAGIC, ALU.max, ALU.subtract))
            dve.tensor_tensor(wb, wb, over(wscale, 2, QB), ALU.mult).then_inc(ff["w"], 1)
            for c in range(CH):
                dve.wait_ge(c2["wg"], c + 1)
                ins = dve.tensor_tensor(chunk(GATED, c), chunk(X, c), chunk(WG, c), ALU.mult)
            ins.then_inc(c2["gated"], 1)
            dve.wait_ge(c2["mod"], CH)
            link(dve.tensor_scalar(MOD, MOD, 0.5, None, ALU.add))
            link(dve.tensor_copy(mod_high[:, :], MOD))
            dve.tensor_tensor(mod_low[:, :], MOD, mod_high[:, :].bitcast(f32), ALU.subtract).then_inc(c2["mod_split"], 1)
            dve.wait_ge(c2["gated"], 1)
            dve.wait_ge(c2["zeroed"], 2)
            g3 = GATED.rearrange("p (b s) -> p b s", s=S)
            t3 = TDVE.rearrange("p (b s) -> p b s", s=S)
            k = d = 0
            for u, (lag, b0, nb, even, valid) in enumerate(LAGS):
                dve.wait_ge(c2["lag_ps"], u + 1)
                if ON_DVE[u]:
                    to = PD[d % 2]
                    d += 1
                else:
                    if k >= 4:
                        dve.wait_ge(c2["added"], k - 3)
                    to = PP[k % 4]
                    k += 1
                prod = to[:, 0:nb * valid].rearrange("p (b s) -> p b s", b=nb)
                m = bank(u % 8)[:, 0:nb * even].rearrange("p (b s) -> p b s", b=nb)[:, :, 0:valid]
                dve.tensor_tensor(prod, m, g3[:, b0:b0 + nb, 0:valid], ALU.mult).then_inc(c2["prod"], 1)
                if ON_DVE[u]:
                    dve.wait_ge(c2["prod"], u + 1)
                    o = t3[:, b0:b0 + nb, lag:S]
                    link(dve.tensor_tensor(o, o, prod, ALU.add))
            dve.wait_ge(c2["added"], k)
            dve.tensor_tensor(TPOOL, TPOOL, TDVE, ALU.add).then_inc(c2["temporal"], 1)
            for c in range(CH):
                dve.wait_ge(c2["gate"], c + 1)
                dve.tensor_tensor(chunk(SOMAG, c), chunk(SOMA, c), chunk(GATE, c), ALU.mult).then_inc(c2["somagate"], 1)
            dve.wait_ge(c2["out_ps"], CH)
            o3 = bank(4, 4).rearrange("p (t d) -> p t d", t=TILES)
            x3 = XC.rearrange("p (t d) -> p t d", t=TILES)
            link(dve.tensor_reduce(nmean, o3, AX.X, ALU.add))
            link(dve.tensor_scalar(nmean, nmean, -1.0 / D, None, ALU.mult))
            dve.tensor_tensor(x3, o3, over(nmean, 2, D), ALU.add).then_inc(c2["xc"], 1)
            dve.wait_ge(c2["sq"], 1)
            link(dve.tensor_reduce(nvar, SQ.rearrange("p (t d) -> p t d", t=TILES), AX.X, ALU.add))
            dve.tensor_scalar(nvar, nvar, 1.0 / D, 1e-5, ALU.mult, ALU.add).then_inc(c2["var"], 1)
            dve.wait_ge(c2["std"], 1)
            link(dve.reciprocal(nstd, nstd))
            dve.tensor_tensor(YL.rearrange("p (t d) -> p t d", t=TILES), x3, over(nstd, 2, D), ALU.mult).then_inc(c2["y"], 1)

        arena_at[0] = 0
        U, GT, SG = (region(FT * N) for _ in range(3))
        wscale, winv = cols(3 * FT * P // QB), cols(3 * FT * P // QB)
        amx, amc, gsc = cols(2 * FT * CH), cols(4 + 1), cols(10)
        UNITS = [(f, c) for f in range(FT) for c in range(CH)]

        def span(t, f, c=None):
            return t[:, f * N:(f + 1) * N] if c is None else t[:, f * N + c * CT:f * N + (c + 1) * CT]

        MAXIMA = 5

        def global_max_pe(pe, n):
            pe.wait_ge(ff["amax"], n + 1)
            pe.transpose(bank(7)[0:1, 0:P], amc[:, n:n + 1], K["ident"]).then_inc(ff["amaxT_ps"], 1)
            pe.wait_ge(ff["gmax"], n + 1)
            pe.matmul(bank(7)[:, P:P + 2], K["ones"][0:1, :], over(gsc[0:1, 2 * n:2 * n + 1], 1, 2), start=True, stop=True)\
                .then_inc(ff["gmaxb_ps"], 1)

        def global_max_dve(dve, n, part):
            dve.tensor_reduce(amc[:, n:n + 1], part, AX.X, ALU.max).then_inc(ff["amax"], 1)
            dve.wait_ge(ff["amaxT_ps"], n + 1)
            dve.tensor_reduce(gsc[0:1, 2 * n:2 * n + 1], bank(7)[0:1, 0:P], AX.X, ALU.max).then_inc(ff["gmax"], 1)
            dve.wait_ge(ff["gmaxb_ps"], n + 1)
            link(dve.tensor_scalar(gsc[:, 2 * n:2 * n + 1], bank(7)[:, P:P + 1], 1.0 / QMAX, 1e-12, ALU.mult, ALU.max))
            dve.reciprocal(gsc[:, 2 * n + 1:2 * n + 2], gsc[:, 2 * n:2 * n + 1]).then_inc(ff["scale"], 1)

        def scale(n):
            return gsc[:, 2 * n:2 * n + 1]

        def inverse(n):
            return gsc[:, 2 * n + 1:2 * n + 2]

        def ffn_pe(pe):
            global_max_pe(pe, 0)
            pe.wait_ge(ff["hq"], 1)
            for v in range(2 * len(UNITS)):
                f, c = UNITS[v % len(UNITS)]
                if v >= 6:
                    pe.wait_ge(ff["copied"], v - 5)
                k = (0 if v < len(UNITS) else FT) + f
                pe.matmul(bank(v % 6), wT[:, k * P:(k + 1) * P], chunk(H, c), start=True, stop=True).then_inc(ff["up_ps"], 1)
            for n in (1, 2, 3, 4):
                global_max_pe(pe, n)
            for f in range(FT):
                pe.wait_ge(ff["o"], f + 1)
                for c in range(CH):
                    ins = pe.matmul(bank(c), wT[:, (2 * FT + f) * P:(2 * FT + f + 1) * P], span(U, f, c),
                                    start=f == 0, stop=f == FT - 1)
                    if f == FT - 1:
                        ins.then_inc(ff["down_ps"], 1)

        def ffn_act(act):
            act.wait_ge(ff["hq"], 1)
            for v in range(2 * len(UNITS)):
                f, c = UNITS[v % len(UNITS)]
                act.wait_ge(ff["up_ps"], v + 1)
                act.activation(span(U if v < len(UNITS) else GT, f, c), bank(v % 6), ACT.Copy).then_inc(ff["copied"], 1)

            def to_integers(t, n):
                for f in range(FT):
                    act.activation(span(t, f), span(t, f), ACT.Identity, bias=K["magic"], scale=inverse(n))\
                        .then_inc(ff["magic"], 1)

            act.wait_ge(ff["scale"], 2)
            act.wait_ge(ff["copied"], 2 * len(UNITS))
            to_integers(GT, 1)
            act.wait_ge(ff["scale"], 3)
            for f in range(FT):
                act.wait_ge(ff["gq"], f + 1)
                act.activation(span(SG, f), span(GT, f), ACT.Sigmoid).then_inc(ff["sig"], 1)
            to_integers(U, 2)
            act.wait_ge(ff["scale"], 4)
            to_integers(GT, 3)
            act.wait_ge(ff["scale"], 5)
            act.wait_ge(ff["magic"], 3 * FT)
            to_integers(U, 4)

        def clamp(eng, t, f):
            return eng.tensor_scalar(span(t, f), span(t, f), MAGIC + QMAX, MAGIC - QMAX - 1.0, ALU.min, ALU.max)

        def dequant(eng, t, f, n):
            return eng.tensor_scalar(span(t, f), span(t, f), MAGIC, scale(n), ALU.subtract, ALU.mult)

        def ffn_pool(pool):
            for f in range(FT):
                pool.wait_ge(ff["magic"], FT + f + 1)
                clamp(pool, U, f).then_inc(ff["uq"], 1)
                pool.wait_ge(ff["uq"], 2 * f + 1)
                dequant(pool, U, f, 2).then_inc(ff["uq"], 1)

        def ffn_dve(dve):
            for c in range(CH):
                dve.wait_ge(c2["yt"], c + 1)
                link(dve.tensor_reduce(amx[:, c:c + 1], chunk(H, c), AX.X, ALU.max, apply_absolute_value=True))
            global_max_dve(dve, 0, amx[:, 0:CH])
            dve.wait_ge(ff["scale"], 1)
            link(dve.tensor_scalar(H[:, :], H[:, :], inverse(0), MAGIC, ALU.mult, ALU.add))
            link(dve.tensor_scalar(H[:, :], H[:, :], MAGIC + QMAX, MAGIC - QMAX - 1.0, ALU.min, ALU.max))
            dve.tensor_scalar(H[:, :], H[:, :], MAGIC, scale(0), ALU.subtract, ALU.mult).then_inc(ff["hq"], 1)
            for v in range(2 * FT):
                dve.wait_ge(ff["copied"], CH * (v + 1))
                ins = dve.tensor_reduce(amx[:, v:v + 1], span(U if v < FT else GT, v % FT), AX.X, ALU.max,
                                        apply_absolute_value=True)
            link(ins)
            global_max_dve(dve, 1, amx[:, FT:2 * FT])
            global_max_dve(dve, 2, amx[:, 0:FT])
            for f in range(FT):
                dve.wait_ge(ff["magic"], f + 1)
                link(clamp(dve, GT, f))
                dequant(dve, GT, f, 1).then_inc(ff["gq"], 1)
            for f in range(FT):
                dve.wait_ge(ff["sig"], f + 1)
                link(dve.tensor_scalar(span(SG, f), span(SG, f), 65536.0, MAGIC, ALU.mult, ALU.add))
                link(dve.tensor_scalar(span(SG, f), span(SG, f), MAGIC, MAGIC + 65535.0, ALU.max, ALU.min))
                link(dve.tensor_scalar(span(SG, f), span(SG, f), MAGIC, 1.0 / 65536.0, ALU.subtract, ALU.mult))
                link(dve.tensor_tensor(span(GT, f), span(GT, f), span(SG, f), ALU.mult))
                link(dve.tensor_reduce(amx[:, f:f + 1], span(GT, f), AX.X, ALU.max, apply_absolute_value=True))
            global_max_dve(dve, 3, amx[:, 0:FT])
            for f in range(FT):
                dve.wait_ge(ff["magic"], 2 * FT + f + 1)
                link(clamp(dve, GT, f))
                link(dequant(dve, GT, f, 3))
                dve.wait_ge(ff["uq"], 2 * f + 2)
                dve.tensor_tensor(span(U, f), span(U, f), span(GT, f), ALU.mult).then_inc(ff["om"], 1)
                dve.wait_ge(ff["om"], f + 1)
                link(dve.tensor_reduce(amx[:, f:f + 1], span(U, f), AX.X, ALU.max, apply_absolute_value=True))
            global_max_dve(dve, 4, amx[:, 0:FT])
            for f in range(FT):
                dve.wait_ge(ff["magic"], 3 * FT + f + 1)
                link(clamp(dve, U, f))
                dequant(dve, U, f, 4).then_inc(ff["o"], 1)
            for c in range(CH):
                dve.wait_ge(ff["down_ps"], c + 1)
                dve.tensor_tensor(chunk(X, c), chunk(X, c), bank(c), ALU.add).then_inc(ff["x"], 1)

        arena_at[0] = 0
        TOK, HOT = region(N), region(N)
        idcol = cols(B)

        def own_pe(pe, s, loaded, bias, rows, x_ready):
            pe.wait_ge(s["hot"], 1)
            pe.wait_ge(l_sel, 16)
            pe.wait_ge(loaded, 16 * B)
            x_ready(pe)
            for t in range(TILES):
                o = PS[:, 4 * CT + t * P:4 * CT + (t + 1) * P]
                pe.matmul(o, HOT[0:rows, t * P:(t + 1) * P], bias[0:rows, :], start=True, stop=False)
                for q in range(4):
                    b = 4 * t + q
                    ins = pe.matmul(o[32 * q:32 * q + 32, :], X[:, b * S:(b + 1) * S], chosen[:, b * P:(b + 1) * P],
                                    start=False, stop=True, tile_position=(0, 32 * q))
                ins.then_inc(s["ps"], 1)
            for t in range(TILES):
                if t % TPC == 0:
                    pe.wait_ge(s["tok"], t // TPC + 1)
                ins = pe.transpose(PS[:, t * P:(t + 1) * P], TOK[:, t * P:(t + 1) * P], K["ident"])
                if t % TPC == TPC - 1:
                    ins.then_inc(s["tr_ps"], 1)

        def own_act(act, s):
            for c in range(CH):
                act.wait_ge(s["ps"], TPC * (c + 1))
                act.activation(chunk(TOK, c), bank(4 + c), ACT.Copy).then_inc(s["tok"], 1)
            for c in range(CH):
                act.wait_ge(s["tr_ps"], c + 1)
                act.activation(chunk(H, c), bank(c), ACT.Copy).then_inc(s["h"], 1)

        def own_dve(dve, s, ids):
            link(dve.tensor_copy(idcol, ids))
            dve.tensor_scalar(HOT.rearrange("p (b s) -> p b s", b=B), over(idcol, 2, S), K["index"], None, ALU.is_equal)\
                .then_inc(s["hot"], 1)

        arena_at[0] = 0
        _ = region(N)
        XF = region(N)
        HB, SB, HH = ([region(CT) for _ in range(3)] for _ in range(3))
        ACC, Y, YSQ, YN = region(CT), region(CT), region(CT), region(CT)
        OUTT = [region(CT) for _ in range(2)]
        WTX = region(CT)
        LG, BI, SEL_, TA = (cols(TPC * E) for _ in range(4))
        PAIR, PAIR2 = cols(TPC * E * E), cols(TPC * E * E)
        rmx, rsm, ss, rstd, half = (cols(TPC) for _ in range(5))
        WX = cols(TPC * 8)
        UN = 2 + E
        NCH = 2 * CH

        def source(n):
            return chunk(H if n < CH else XF, n % CH)

        def moe_pe(pe):
            pe.wait_ge(l_moe, 16)

            def wait_source(n):
                if n < CH:
                    pe.wait_ge(l2["h"], CH)
                else:
                    pe.wait_ge(mo["xf"], n - CH + 1)

            def weights(k):
                if k < 2:
                    return MW["Sup"][:, k * P:(k + 1) * P], MW["Sgt"], MW["Sdn"]
                return tuple(MW[x][:, (k - 2) * P:(k - 1) * P] for x in ("Wup", "Wgt", "Wdn"))

            def up(n, k):
                u = UN * n + k
                if u >= 2:
                    pe.wait_ge(mo["h"], u - 1)
                pe.matmul(bank(u % 2), weights(k)[0], source(n), start=True, stop=True).then_inc(mo["up_ps"], 1)

            def gate(n, k):
                u = UN * n + k
                pe.wait_ge(mo["h"], u + 1)
                if u >= 2:
                    pe.wait_ge(mo["s"], u - 1)
                pe.matmul(bank(2 + u % 2), weights(k)[1], HB[u % 3], start=True, stop=True).then_inc(mo["gt_ps"], 1)

            def down(n, k):
                u = UN * n + k
                pe.wait_ge(mo["hh"], u + 1)
                if k >= 2:
                    v = E * n + k - 2
                    if v >= 2:
                        pe.wait_ge(mo["eo"], v - 1)
                    to = bank(4 + v % 2)
                else:
                    to = bank(6)
                for t in range(TPC):
                    ins = pe.matmul(to[:, t * P:(t + 1) * P], HH[u % 3][:, t * P:(t + 1) * P], weights(k)[2],
                                    start=k >= 2, stop=k >= 2, skip_group_check=True)
                ins.then_inc(mo["dn_ps"], 1)

            def tail(n):
                if n < CH:
                    pe.wait_ge(mo["normed"], n + 1)
                for t in range(TPC):
                    src = YN if n < CH else chunk(X, n - CH)
                    ins = pe.transpose(bank(7)[:, t * P:(t + 1) * P], src[:, t * P:(t + 1) * P], K["ident"])
                ins.then_inc(mo["tr_ps"], 1)

            for n in range(NCH):
                wait_source(n)
                if n:
                    pe.wait_ge(mo["wT"], n)
                for t in range(TPC):
                    ins = pe.matmul(bank(7)[:, 8 * t:8 * t + E], source(n)[:, t * P:(t + 1) * P],
                                    MW["rW"][:, (n // CH) * E:(n // CH + 1) * E], start=True, stop=True)
                ins.then_inc(mo["logit_ps"], 1)
                if n:
                    pe.wait_ge(mo["y"], n)
                for t in range(TPC):
                    pe.matmul(bank(6)[:, t * P:(t + 1) * P], source(n)[:, t * P:(t + 1) * P], K["ident"],
                              start=t == 0, stop=False, skip_group_check=True)
                up(n, 0)
                for k in range(UN + 1):
                    if k + 1 < UN:
                        up(n, k + 1)
                    if k < UN:
                        gate(n, k)
                    if k:
                        down(n, k - 1)
                    if k == 3:
                        pe.wait_ge(mo["logit"], n + 1)
                        if n:
                            tail(n - 1)
                            pe.wait_ge(mo["xf"] if n <= CH else mo["fin"], n if n <= CH else n - CH)
                        pe.wait_ge(mo["w"], n + 1)
                        for t in range(TPC):
                            ins = pe.transpose(bank(7)[0:8, t * P:(t + 1) * P], WX[:, 8 * t:8 * t + 8], K["ident"])
                        ins.then_inc(mo["wT_ps"], 1)
                    if k == 6:
                        pe.wait_ge(mo["wT"], n + 1)
                        for t in range(TPC):
                            ins = pe.matmul(bank(6)[:, t * P:(t + 1) * P], WTX[0:8, t * P:(t + 1) * P], MW["bdn"][0:8, :],
                                            start=False, stop=True, skip_group_check=True)
                        ins.then_inc(mo["acc_ps"], 1)
            tail(NCH - 1)

        def moe_act(act):
            def h(n, k):
                u = UN * n + k
                bias = MW["sbup"][:, k:k + 1] if k < 2 else MW["bup"][:, k - 2:k - 1]
                act.wait_ge(mo["up_ps"], u + 1)
                if u >= 3:
                    act.wait_ge(mo["hh"], u - 2)
                act.activation(HB[u % 3], bank(u % 2), ACT.Identity, bias=bias).then_inc(mo["h"], 1)

            def s(n, k):
                u = UN * n + k
                bias = MW["sbgt"] if k < 2 else MW["bgt"][:, k - 2:k - 1]
                act.wait_ge(mo["gt_ps"], u + 1)
                if u >= 3:
                    act.wait_ge(mo["hh"], u - 2)
                act.activation(SB[u % 3], bank(2 + u % 2), ACT.Silu, bias=bias).then_inc(mo["s"], 1)

            for n in range(NCH):
                h(n, 0)
                for k in range(UN):
                    if k + 1 < UN:
                        h(n, k + 1)
                    s(n, k)
                    if k == 1:
                        act.wait_ge(mo["masked"], n + 1)
                        act.activation(TA, TA, ACT.Exp).then_inc(mo["exped"], 1)

        def moe_pool(pool):
            pool.memset(half, -0.5).then_inc(mo["half"], 1)
            pool.memset(WX, 1.0).then_inc(mo["half"], 1)
            pool.wait_ge(mo["half"], 2)

            def squares(n):
                pool.wait_ge(mo["y"], n + 1)
                pool.tensor_tensor(YSQ, Y, Y, ALU.mult).then_inc(mo["sq"], 1)
                pool.wait_ge(mo["ss"], n + 1)
                pool.tensor_tensor(rstd, ss, half, ALU.pow).then_inc(mo["rstd"], 1)

            for n in range(NCH):
                for k in range(UN):
                    u = UN * n + k
                    pool.wait_ge(mo["s"], u + 1)
                    if u >= 3:
                        pool.wait_ge(mo["dn_ps"], u - 2)
                    pool.tensor_tensor(HH[u % 3], SB[u % 3], HB[u % 3], ALU.mult).then_inc(mo["hh"], 1)
                    if k == 1 and n:
                        squares(n - 1)
            squares(NCH - 1)

        def moe_dve(dve):
            w3 = WX.rearrange("p (t e) -> p t e", t=TPC)[:, :, 0:E]

            def router(n):
                i = n // CH
                lg, bi, sel, ta = (x.rearrange("p (t e) -> p t e", t=TPC) for x in (LG, BI, SEL_, TA))
                p4, q4 = (x.rearrange("p (t e f) -> p t e f", t=TPC, e=E) for x in (PAIR, PAIR2))
                dve.wait_ge(mo["logit_ps"], n + 1)
                b7 = bank(7)[:, 0:8 * TPC].rearrange("p (t e) -> p t e", t=TPC)[:, :, 0:E]
                dve.tensor_tensor(lg, b7, over(MW["rb"][:, i * E:(i + 1) * E], 1, TPC), ALU.add).then_inc(mo["logit"], 1)
                dve.wait_ge(mo["logit"], n + 1)
                link(dve.tensor_tensor(bi, lg, over(MW["gb"][:, i * E:(i + 1) * E], 1, TPC), ALU.add))
                note(dve.tensor_tensor(p4, over(bi, 2, E), over(bi, 3, E), ALU.is_gt))
                link(dve.tensor_tensor(q4, over(bi, 2, E), over(bi, 3, E), ALU.is_equal))
                q3 = PAIR2.rearrange("p (t e) -> p t e", t=TPC)
                link(dve.tensor_tensor(q3, q3, over(K["tri"], 1, TPC), ALU.mult))
                link(dve.tensor_tensor(PAIR, PAIR, PAIR2, ALU.add))
                link(dve.tensor_reduce(sel, p4, AX.X, ALU.add))
                link(dve.tensor_scalar(SEL_, SEL_, 2.0, None, ALU.is_lt))
                note(dve.tensor_tensor(BI, LG, SEL_, ALU.mult))
                link(dve.tensor_scalar(TA, SEL_, 1.0, NEG, ALU.subtract, ALU.mult))
                link(dve.tensor_tensor(TA, TA, BI, ALU.add))
                link(dve.tensor_reduce(rmx, ta, AX.X, ALU.max))
                dve.tensor_tensor(ta, ta, over(rmx, 2, E), ALU.subtract).then_inc(mo["masked"], 1)

            def router_end(n):
                dve.wait_ge(mo["exped"], n + 1)
                if n == 0:
                    dve.wait_ge(mo["half"], 2)
                else:
                    dve.wait_ge(mo["wT_ps"], n)
                ta = TA.rearrange("p (t e) -> p t e", t=TPC)
                link(dve.tensor_reduce(rsm, ta, AX.X, ALU.add))
                link(dve.reciprocal(rsm, rsm))
                dve.tensor_tensor(w3, ta, over(rsm, 2, E), ALU.mult).then_inc(mo["w"], 1)
                dve.wait_ge(mo["w"], n + 1)

            def sum_squares(n):
                dve.wait_ge(mo["sq"], n + 1)
                link(dve.tensor_reduce(ss, YSQ.rearrange("p (t d) -> p t d", t=TPC), AX.X, ALU.add))
                dve.tensor_scalar(ss, ss, 1.0 / D, 1e-6, ALU.mult, ALU.add).then_inc(mo["ss"], 1)

            def norm(n):
                i = n // CH
                dve.wait_ge(mo["rstd"], n + 1)
                if 1 <= n < CH:
                    dve.wait_ge(mo["tr_ps"], n)
                if n >= CH:
                    dve.wait_ge(mo["tr_ps"], CH)
                if n > CH:
                    dve.wait_ge(mo["fin"], n - CH)
                for t in range(TPC):
                    r = slice(t * P, (t + 1) * P)
                    ins = dve.scalar_tensor_tensor(YN[:, r], Y[:, r], rstd[:, t:t + 1], MW["norm"][:, i * P:(i + 1) * P],
                                                   ALU.mult, ALU.mult)
                ins.then_inc(mo["normed"], 1)

            def finish(n):
                dve.wait_ge(mo["tr_ps"], n + 1)
                if n < CH:
                    dve.tensor_copy(chunk(XF, n), bank(7)).then_inc(mo["xf"], 1)
                else:
                    dve.wait_ge(mo["normed"], n + 1)
                    if n >= CH + 2:
                        dve.wait_ge(stored[n % 2], 16 * ((n - CH) // 2))
                    dve.tensor_tensor(OUTT[n % 2], YN, bank(7), ALU.add).then_inc(mo["fin"], 1)

            for n in range(NCH):
                router(n)
                if n:
                    sum_squares(n - 1)
                    norm(n - 1)
                    finish(n - 1)
                router_end(n)
                for e in range(E):
                    u, v = UN * n + 2 + e, E * n + e
                    dve.wait_ge(mo["dn_ps"], u + 1)
                    join()
                    for t in range(TPC):
                        r = slice(t * P, (t + 1) * P)
                        w = WX[:, 8 * t + e:8 * t + e + 1]
                        if e == 0:
                            ins = dve.tensor_scalar(ACC[:, r], bank(4 + v % 2)[:, r], w, None, ALU.mult)
                        else:
                            ins = dve.scalar_tensor_tensor(ACC[:, r], bank(4 + v % 2)[:, r], w, ACC[:, r], ALU.mult, ALU.add)
                    ins.then_inc(mo["eo"], 1)
                    dve.wait_ge(mo["eo"], v + 1)
                    if e == 0:
                        dve.wait_ge(mo["wT_ps"], n + 1)
                        dve.tensor_copy(WTX[0:8, :], bank(7)[0:8, :]).then_inc(mo["wT"], 1)
                dve.wait_ge(mo["acc_ps"], n + 1)
                dve.wait_ge(mo["dn_ps"], UN * n + 2)
                if n:
                    dve.wait_ge(mo["normed"], n)
                dve.tensor_tensor(Y, ACC, bank(6), ALU.add).then_inc(mo["y"], 1)
                dve.wait_ge(mo["y"], n + 1)
            sum_squares(NCH - 1)
            norm(NCH - 1)
            finish(NCH - 1)

        STAGES = stage

        @block.sync
        def _(sp):
            for dst, src, s in ((t_const, consts, l_const), (t_cond, cond, l_const), (X, x_fm, l_x), (x_tok, x_tm, l_x),
                                (t_int, ints, l_int), (t_attn[0], attn0, l_attn0), (t_ctx, ctx_w, l_ctx),
                                (t_ffn, ffn_w, l_ffn), (t_sel, sel_w, l_sel), (t_attn[1], attn1, l_attn1),
                                (t_moe, moe_w, l_moe)):
                sp.dma_start(dst[:, :], src).then_inc(s, 16)
            sp.wait_ge(l_int, 16)
            sp.wait_ge(a["split"], 1)
            for b in range(B):
                i = sp.value_load(IN["subject"][0:1, b:b + 1], min_val=0, max_val=NSUB - 1)
                sp.dma_start(chosen[:, b * P:(b + 1) * P],
                             w_subject[bass.ds(i, 1), :, :].rearrange("a p n -> p (a n)")).then_inc(chosen1, 16)
            if stage >= 5:
                sp.wait_ge(l1["ps"], TILES)
                for b in range(B):
                    i = sp.value_load(IN["category"][0:1, b:b + 1], min_val=0, max_val=NCAT - 1)
                    sp.dma_start(chosen[:, b * P:(b + 1) * P],
                                 w_category[bass.ds(i, 1), :, :].rearrange("a p n -> p (a n)")).then_inc(chosen2, 16)
                for j in range(CH):
                    sp.wait_ge(mo["fin"], j + 1)
                    sp.dma_start(out[:, j * CT:(j + 1) * CT], OUTT[j % 2]).then_inc(stored[j % 2], 16)
                for s in stored:
                    sp.wait_ge(s, 16 * CH // 2)
            else:
                last = {1: at[0]["y"], 2: c2["yt"], 3: ff["x"], 4: at[1]["y"], 6: l1["h"]}[stage]
                sp.wait_ge(last, CH)
                sp.wait_ge(chosen1, 16 * B)
                sp.dma_start(out, (H if stage == 2 else X)[:, :]).then_inc(stored[0], 16)
                sp.wait_ge(stored[0], 16)

        @block.tensor
        def _(pe):
            pooling_pe(pe)
            attention_pe(pe, 0, lambda e, c: e.wait_ge(a["h"], CH))
            if STAGES >= 2:
                ctx_pe(pe)
            if STAGES >= 3:
                ffn_pe(pe)
            if STAGES >= 4:
                own_pe(pe, l1, chosen1, SW["bias1"], NSUB, lambda e: e.wait_ge(ff["x"], CH))
                attention_pe(pe, 1, lambda e, c: e.wait_ge(l1["h"], CH))
            if STAGES >= 5:
                own_pe(pe, l2, chosen2, SW["bias2"], NCAT, lambda e: e.wait_ge(at[1]["y"], CH))
                moe_pe(pe)

        @block.scalar
        def _(act):
            pooling_act(act)
            attention_act(act, 0)
            if STAGES >= 2:
                ctx_act(act)
            if STAGES >= 3:
                ffn_act(act)
            if STAGES >= 4:
                own_act(act, l1)
                attention_act(act, 1)
            if STAGES >= 5:
                own_act(act, l2)
                moe_act(act)

        @block.gpsimd
        def _(pool):
            pooling_pool(pool)
            attention_pool(pool, 0)
            if STAGES >= 2:
                ctx_pool(pool)
            if STAGES >= 3:
                ffn_pool(pool)
            if STAGES >= 4:
                attention_pool(pool, 1)
            if STAGES >= 5:
                moe_pool(pool)

        @block.vector
        def _(dve):
            pooling_dve(dve)
            attention_dve(dve, 0)
            powers_dve(dve)
            if STAGES >= 2:
                ctx_dve(dve)
            if STAGES >= 3:
                ffn_dve(dve)
            if STAGES >= 4:
                own_dve(dve, l1, IN["subject"])
                attention_dve(dve, 1)
            if STAGES >= 5:
                own_dve(dve, l2, IN["category"])
                moe_dve(dve)


def columns(spec, arrays):
    out = np.zeros((P, width(spec)), np.float32)
    at = 0
    for name, w in spec:
        x = np.asarray(arrays[name])
        out[:x.shape[0], at:at + w] = x.reshape(x.shape[0], w)
        at += w
    return out


def constants():
    p = np.arange(P)
    q, g = p % S, p // S
    k = np.arange(S)
    slopes = np.power(np.float32(2.0), -8.0 * np.arange(1, HEADS + 1, dtype=np.float32) / HEADS)
    head = g[:, None] * HG + np.arange(HG)[None, :]
    causal = k[None, :] <= q[:, None]
    rel = np.abs(q[:, None] - k[None, :]).astype(np.float32)
    alibi = np.where(causal[:, None, :], -slopes[head][:, :, None] * rel[:, None, :], np.float32(-NEG))
    e = np.arange(E)
    return columns(CONST, {
        "ident": np.eye(P), "alibi": alibi, "causal": np.where(causal, 0.0, -NEG), "pre": causal,
        "post": k[None, :] >= q[:, None], "cloze": k[None, :] != q[:, None], "empty": (WINDOW - 1 - q)[:, None],
        "hmask": (p[:, None] // HD) % HG == np.arange(HG)[None, :], "gmask": g[:, None] == np.arange(G)[None, :],
        "index": p[:, None], "tri": np.broadcast_to((e[None, :] < e[:, None]).reshape(1, -1), (P, E * E)),
        "ones": np.ones((P, P)), "magic": np.full((P, 1), MAGIC)})


def kernel(**inputs):
    import concourse.bacc as bacc
    from concourse.bass_utils import run_bass_kernel_spmd

    a = {k: np.asarray(v) for k, v in inputs.items()}

    def heads(w):
        return w.T.reshape(G, HG, HD, D).transpose(1, 0, 2, 3).reshape(D, D)

    def col(v):
        return v.reshape(-1, 1)

    def twice(v):
        return np.concatenate([v, v])

    def attn(wq, wk, wv, wo, bq, bk, bv, bo):
        return columns(ATTN, {"wq": wq.T, "wk": wk.T, "wv": wv.T, "wo": heads(wo), "bv": bv.reshape(1, -1),
                              "bq": col(bq), "bk": col(bk), "bo": col(bo)})

    def rows(v):
        return np.broadcast_to(v.reshape(1, -1), (P, v.size))

    def blocks(w):
        return w.reshape(-1, P, w.shape[1]).transpose(1, 0, 2).reshape(P, -1)

    def side(w):
        return w.transpose(1, 0, 2).reshape(w.shape[1], -1)

    x = a["x"].reshape(N, D)
    arrays = {
        "consts": constants(),
        "cond": columns(COND, {"W1": a["L0_cond_W1"], "b1": col(a["L0_cond_b1"]),
                               "vrep": np.broadcast_to(col(a["L0_cond_v"]), (32, P)),
                               "blend": twice(a["cond_1024"]).T, "tau_raws": col(twice(a["condB_tauraws"])),
                               "tau_ctx": np.broadcast_to(a["L0_cond2_tau_ctx"].reshape(1, 1), (P, 1))}),
        "attn0": attn(*(a["L0_attn_" + n] for n in ("wq", "wk", "wv", "wo", "bq", "bk", "bv", "bo"))),
        "ctx_w": columns(CTX, {"Wg0": a["L0_cond2_Wg"][:, :D].T, "Wg1": a["L0_cond2_Wg"][:, D:].T,
                               "Wsoma": a["L0_cond2_Wsoma"].T, "Wtemp": a["L0_cond2_Wtemp"].T,
                               "Wout": a["L0_cond2_Wout"].T, "Wn1": a["L0_cond2_Wn1"].T, "Wn2": twice(a["cond_256"]).T,
                               "bg": col(a["L0_cond2_bg"]), "bn1": col(a["L0_cond2_bn1"]), "bn2": col(twice(a["condB_bn2"])),
                               "bsoma": col(a["L0_cond2_bsoma"]), "btemp": col(a["L0_cond2_btemp"]),
                               "gamma": col(a["L0_cond2_gamma"]), "beta": col(a["L0_cond2_beta"])}),
        "ffn_w": columns(FFN, {"up": blocks(a["L0_ffn_w_up"]), "gate": blocks(a["L0_ffn_w_gate"]), "down": a["L0_ffn_w_down"]}),
        "attn1": attn(*(a["L1_attn_" + n] for n in ("Wq", "Wk", "Wv", "Wo", "bq", "bk", "bv", "bo"))),
        "sel_w": columns(SEL, {"bias1": a["L1_cond_bias"], "bias2": a["L1_cond2_b"]}),
        "moe_w": columns(MOE, {
            "Wup": side(a["L1_ffn_exp_Wup"]), "Wgt": side(a["L1_ffn_exp_Wg"]), "Wdn": side(a["L1_ffn_exp_Wdown"]),
            "Sup": a["L1_ffn_share_Wup"], "Sgt": a["L1_ffn_share_Wg"], "Sdn": a["L1_ffn_share_Wdown"],
            "bdn": np.concatenate([a["L1_ffn_exp_bdown"], twice(a["L1_ffn_share_bdown"].reshape(1, -1))]),
            "norm": rows(a["L1_ffn_norm_w"]), "rW": side(a["L1_ffn_router_W"]), "rb": rows(a["L1_ffn_router_b"]),
            "gb": rows(a["L1_ffn_gate_bias"]), "bup": a["L1_ffn_exp_bup"].T, "bgt": a["L1_ffn_exp_bg"].T,
            "sbup": a["L1_ffn_share_bup"].reshape(2, D).T, "sbgt": col(a["L1_ffn_share_bg"])}),
        "ints": np.concatenate([np.repeat(a["itok_B_0_2"].reshape(TILES, 4).T, S, axis=0),
                                rows(a["itok_B_0_7"]), rows(a["itok_B_0_30"])], axis=1).astype(np.int32),
        "x_fm": x.T, "x_tm": x.reshape(TILES, P, D).transpose(1, 0, 2).reshape(P, N),
        "w_subject": a["L1_cond_weight"].transpose(0, 2, 1), "w_category": a["L1_cond2_W"],
    }
    arrays = {k: np.ascontiguousarray(v) for k, v in arrays.items()}
    nc = bacc.Bacc("TRN2", target_bir_lowering=False, num_devices=1)
    args = [nc.dram_tensor(k, v.shape, mybir.dt.from_np(v.dtype), kind="ExternalInput").ap() for k, v in arrays.items()]
    args.append(nc.dram_tensor("out", (P, N), mybir.dt.float32, kind="ExternalOutput").ap())
    program(nc, *args, stage=STAGE)
    got = run_bass_kernel_spmd(nc, [arrays], core_ids=[0]).results[0]["out"]
    if STAGE < 5:
        return got.T.reshape(B, S, D)
    return got.reshape(P, TILES, D).transpose(1, 0, 2).reshape(B, S, D)
```

```python
import numpy as np
import concourse.bass as bass
from concourse import mybir
from contextlib import ExitStack

B, S, D = 64, 32, 128
N = B * S
P = 128
TILES = N // P
CH = 4
CT = N // CH
TPC = CT // P
CB = CT // S
HEADS, HD = 16, 8
G, HG = 4, 4
WINDOW = 128
TR = 64
F = 384
FT = F // P
QB = 32
NSUB, NCAT = 8, 32
E = 6
NEG = 1e30
STAGE = 5
MAGIC = 12582912.0
QMAX = 32767.0

CONST = [("ident", P), ("alibi", HG * S), ("causal", S), ("pre", S), ("post", S), ("cloze", S),
         ("empty", 1), ("hmask", HG), ("gmask", G), ("index", 1), ("tri", E * E), ("ones", P), ("magic", 1)]
COND = [("W1", 32), ("b1", 1), ("vrep", P), ("blend", 2 * TR), ("tau_raws", 1), ("tau_ctx", 1)]
ATTN = [("wq", P), ("wk", P), ("wv", P), ("wo", P), ("bv", P), ("bq", 1), ("bk", 1), ("bo", 1)]
CTX = [("Wg0", P), ("Wg1", P), ("Wsoma", P), ("Wtemp", P), ("Wout", P), ("Wn1", 32), ("Wn2", P),
       ("bg", 1), ("bn1", 1), ("bn2", 1), ("bsoma", 1), ("btemp", 1), ("gamma", 1), ("beta", 1)]
FFN = [("up", FT * P), ("gate", FT * P), ("down", FT * P)]
SEL = [("bias1", P), ("bias2", P)]
MOE = [("Wup", E * P), ("Wgt", E * P), ("Wdn", E * P), ("Sup", 2 * P), ("Sgt", P), ("Sdn", P),
       ("bdn", P), ("norm", 2 * P), ("rW", 2 * E), ("rb", 2 * E), ("gb", 2 * E),
       ("bup", E), ("bgt", E), ("sbup", 2), ("sbgt", 1)]
INTS = [("prompt", TILES), ("subject", B), ("category", B)]


def width(fields):
    return sum(w for _, w in fields)


def lags():
    out = []
    for lag in range(S):
        valid = S - lag
        even = valid + valid % 2
        nb = min(B, CT // S * (S // (1 << (even - 1).bit_length())))
        for b in range(0, B, nb):
            out.append((lag, b, nb, even, valid))
    return out


def program(nc, consts, cond, attn0, ctx_w, ffn_w, attn1, sel_w, moe_w, ints, x_fm, x_tm, w_subject, w_category,
            out, stage=9):
    f32, f32r, i32 = mybir.dt.float32, mybir.dt.float32r, mybir.dt.int32
    ALU, ACT, AX = mybir.AluOpType, mybir.ActivationFunctionType, mybir.AxisListType
    es = ExitStack()
    with es:
        def sb(name, cols, dt=f32):
            return es.enter_context(nc.sbuf_tensor(name, [P, cols], dt))

        def sem(name):
            return es.enter_context(nc.semaphore(name))

        def fields(t, spec):
            at, found = 0, {}
            for name, w in spec:
                found[name] = t[:, at:at + w]
                at += w
            return found

        def over(ap, axis, n):
            ap = ap.unsqueeze(axis)
            shape = list(ap.shape)
            shape[axis] = n
            return ap.broadcast_to(shape)

        t_const, t_cond = sb("t_const", width(CONST)), sb("t_cond", width(COND))
        t_attn = [sb("t_attn0", width(ATTN)), sb("t_attn1", width(ATTN))]
        t_ctx, t_ffn, t_sel = sb("t_ctx", width(CTX)), sb("t_ffn", width(FFN)), sb("t_sel", width(SEL))
        t_moe, t_int = sb("t_moe", width(MOE)), sb("t_int", width(INTS), i32)
        K, C0, W2, FW = fields(t_const, CONST), fields(t_cond, COND), fields(t_ctx, CTX), fields(t_ffn, FFN)
        AW = [fields(t, ATTN) for t in t_attn]
        SW, MW, IN = fields(t_sel, SEL), fields(t_moe, MOE), fields(t_int, INTS)
        X = sb("X", N)
        H = sb("H", N)
        chosen = sb("chosen", B * P)
        x_tok = chosen[:, S * P:S * P + N]
        powers = sb("powers", S * P, f32r)
        mod_high, mod_low = sb("mod_high", N, f32r), sb("mod_low", N, f32r)
        wT = sb("wT", 3 * FT * P)
        small = sb("small", 1280)
        ARENA = 21504
        arena = sb("arena", ARENA)
        PS = es.enter_context(nc.psum_tensor("PS", [P, 8 * CT], f32))

        def bank(i, n=1):
            return PS[:, i * CT:(i + n) * CT]

        def chunk(t, c):
            return t[:, c * CT:(c + 1) * CT]

        small_at, arena_at = [0], [0]

        def cols(n):
            small_at[0] += n
            assert small_at[0] <= 1280
            return small[:, small_at[0] - n:small_at[0]]

        def region(n):
            arena_at[0] += n
            assert arena_at[0] <= ARENA, arena_at
            return arena[:, arena_at[0] - n:arena_at[0]]

        l_const, l_x, l_int, l_attn0, l_ctx, l_ffn, l_attn1, l_sel, l_moe = [
            sem("loaded_" + n) for n in ("const", "x", "int", "attn0", "ctx", "ffn", "attn1", "sel", "moe")]
        chosen1, chosen2 = sem("chosen1_loaded"), sem("chosen2_loaded")
        dve_step = sem("dve_step")
        stored = [sem("stored_even"), sem("stored_odd")]

        vector_steps = [0]

        def note(ins):
            vector_steps[0] += 1
            ins.then_inc(dve_step, 1)

        def join():
            nc.vector.wait_ge(dve_step, vector_steps[0])

        def link(ins):
            note(ins)
            join()

        def mk(stage_name, *what):
            return {w: sem(stage_name + "_" + w) for w in what}

        a = mk("pool", "tanh_ps", "tanh", "score_ps", "masked", "exped", "mats", "zeroed", "ps", "h", "blend_max", "blend_exp",
               "power", "power0", "powers", "split")
        at = [mk(f"attn{i}", "zeroed", "qk_ps", "v_ps", "qk", "v_act", "v_dve", "s_ps", "biased", "maxed",
                 "shifted", "exped", "recip", "normed", "probT", "o_ps", "o", "y_ps", "y", "scales", "emd") for i in range(2)]
        c2 = mk("ctx", "ones", "h1_ps", "h1", "soma_ps", "soma", "scanned", "wg_ps", "wg", "gated", "mod_ps",
                "mod", "mod_split", "zeroed", "lag_ps", "prod", "added", "temporal", "gate_ps", "gate", "somagate", "out_ps",
                "xc", "sq", "var", "std", "y", "y_ps", "yt", "bT_ps")
        ff = mk("ffn", "w", "wT_ps", "wT", "amax", "amaxT_ps", "gmax", "gmaxb_ps", "scale", "hq", "up_ps", "copied",
                "magic", "uq", "gq", "sig", "om", "o", "down_ps", "x")
        l1 = mk("sub", "hot", "ps", "tok", "tr_ps", "h")
        l2 = mk("cat", "hot", "ps", "tok", "tr_ps", "h")
        mo = mk("moe", "fuse_ps", "fuse_act", "fused", "logit_ps", "logit", "masked", "exped", "w", "wT_ps", "wT", "split",
                "xhigh", "xsplit", "up_ps", "gt_ps", "s", "hh", "dn_ps", "eo", "acc_ps", "y", "sq", "ss", "rstd",
                "normed", "tr_ps", "xf", "fin", "half")

        block = es.enter_context(nc.Block())

        arena_at[0] = 0
        TH = region(N)
        MASK, NEGM, SC, EX = region(CT), region(CT), region(CT), region(CT)
        TMPM = region(CT)
        MATS = region(N)
        POW = chosen[:, 0:S * P]
        pt = cols(TILES); e0 = cols(TILES); e1 = cols(TILES); e2 = cols(TILES)
        pcnt, pmax, psum_ = cols(TILES), cols(TILES), cols(TILES)
        alpha = cols(1); alpha_t = cols(1); alpha_c = cols(1); alpha_ct = cols(1)
        bmax = cols(1); bsum = cols(1)
        arena_at[0] = 0
        PARTS, PT, PB = 2 * CH, CT // 2, CB // 2
        Q2, K2, T2 = ([region(PB * P) for _ in range(2)] for _ in range(3))
        S3 = [region(PB * P) for _ in range(3)]
        V_ALL = region(3 * CB * P)
        V3 = [V_ALL[:, n * CB * P:(n + 1) * CB * P] for n in range(3)]
        OT = [region(PT) for _ in range(2)]
        qscale, qbias, kbias = cols(G), cols(G), cols(HG)
        NR = PB * HG
        smax, ssum, semt = ([cols(NR) for _ in range(3)] for _ in range(3))

        def qv(t):
            return t.rearrange("p (b g s) -> p b g s", b=PB, g=G)

        def score_bank(j, n):
            return bank(3 + 2 * (j % 2) + n)

        def score_rows(j):
            return S3[j % 3].rearrange("p (r s) -> p r s", s=S)

        def pooling_pe(pe):
            pe.wait_ge(l_const, 32)
            pe.wait_ge(l_x, 32)
            for c in range(CH):
                pe.matmul(bank(c)[0:32, :], C0["W1"], chunk(X, c), start=True, stop=True).then_inc(a["tanh_ps"], 1)
            for c in range(CH):
                pe.wait_ge(a["tanh"], c + 1)
                pe.matmul(bank(4 + c), C0["vrep"][0:32, :], TH[0:32, c * CT:(c + 1) * CT], start=True, stop=True)\
                    .then_inc(a["score_ps"], 1)
            pe.wait_ge(a["mats"], 4)
            for t in range(TILES):
                ins = pe.matmul(PS[:, t * P:(t + 1) * P], x_tok[:, t * P:(t + 1) * P], MATS[:, t * P:(t + 1) * P],
                                start=True, stop=True)
                if t % TPC == TPC - 1:
                    ins.then_inc(a["ps"], 1)
            pe.wait_ge(a["blend_exp"], 1)
            pe.transpose(bank(4)[:, 0:P], C0["blend"], K["ident"]).then_inc(c2["bT_ps"], 1)

        def pooling_act(act):
            act.wait_ge(l_const, 32)
            for c in range(CH):
                act.wait_ge(a["tanh_ps"], c + 1)
                act.activation(TH[0:32, c * CT:(c + 1) * CT], bank(c)[0:32, :], ACT.Tanh, bias=C0["b1"][0:32, :])\
                    .then_inc(a["tanh"], 1)
            act.activation(alpha_t, C0["tau_raws"], ACT.Exp).then_inc(a["power"], 1)
            act.activation(alpha_ct, C0["tau_ctx"], ACT.Exp).then_inc(a["power"], 1)
            act.wait_ge(a["blend_max"], 1)
            act.activation(C0["blend"], C0["blend"], ACT.Exp).then_inc(a["exped"], 1)
            act.wait_ge(a["masked"], 1)
            act.activation(EX, SC, ACT.Exp).then_inc(a["exped"], 1)
            for c in range(CH):
                act.wait_ge(a["ps"], c + 1)
                act.activation(chunk(H, c), bank(c), ACT.Copy).then_inc(a["h"], 1)

        def pooling_pool(pool):
            pool.memset(MATS, 0.0).then_inc(a["zeroed"], 1)
            pool.memset(V_ALL, 0.0).then_inc(at[0]["zeroed"], 1)
            pool.wait_ge(a["power0"], 1)
            for lag in range(1, S):
                pool.tensor_scalar(POW[:, lag * P:(lag + 1) * P], POW[:, (lag - 1) * P:lag * P], alpha, None, ALU.mult)\
                    .then_inc(a["powers"], 1)
                pool.wait_ge(a["powers"], lag)

        def pooling_dve(dve):
            dve.wait_ge(l_const, 32)
            link(dve.tensor_reduce(bmax, C0["blend"][:, 0:TR], AX.X, ALU.max))
            dve.tensor_scalar(C0["blend"], C0["blend"], bmax, None, ALU.subtract).then_inc(a["blend_max"], 1)
            dve.wait_ge(a["power"], 2)
            link(dve.tensor_scalar(alpha_t, alpha_t, 1.0, None, ALU.add))
            link(dve.reciprocal(alpha, alpha_t))
            link(dve.tensor_scalar(alpha_ct, alpha_ct, 1.0, None, ALU.add))
            link(dve.reciprocal(alpha_c, alpha_ct))
            dve.wait_ge(a["exped"], 1)
            link(dve.tensor_reduce(bsum, C0["blend"][:, 0:TR], AX.X, ALU.add))
            link(dve.reciprocal(bsum, bsum))
            dve.tensor_scalar(C0["blend"], C0["blend"], bsum, None, ALU.mult).then_inc(a["blend_exp"], 1)
            dve.wait_ge(l_int, 16)
            link(dve.tensor_copy(pt, IN["prompt"]))
            note(dve.tensor_scalar(e0, pt, 0.0, None, ALU.is_equal))
            link(dve.tensor_scalar(e1, pt, 1.0, None, ALU.is_equal))
            link(dve.tensor_tensor(e2, e0, e1, ALU.add))
            link(dve.tensor_scalar(e2, e2, -1.0, 1.0, ALU.mult, ALU.add))
            m3 = MASK.rearrange("p (t s) -> p t s", t=TILES)
            tmp3 = TMPM.rearrange("p (t s) -> p t s", t=TILES)
            link(dve.tensor_tensor(m3, over(K["pre"], 1, TILES), over(e0, 2, S), ALU.mult))
            link(dve.tensor_tensor(tmp3, over(K["post"], 1, TILES), over(e1, 2, S), ALU.mult))
            link(dve.tensor_tensor(MASK, MASK, TMPM, ALU.add))
            link(dve.tensor_tensor(tmp3, over(K["cloze"], 1, TILES), over(e2, 2, S), ALU.mult))
            link(dve.tensor_tensor(MASK, MASK, TMPM, ALU.add))
            link(dve.tensor_reduce(pcnt, m3, AX.X, ALU.add))
            link(dve.tensor_scalar(NEGM, MASK, 1.0, NEG, ALU.subtract, ALU.mult))
            dve.wait_ge(a["score_ps"], CH)
            sc3 = SC.rearrange("p (t s) -> p t s", t=TILES)
            ps3 = bank(4, 4).rearrange("p (t q s) -> p t q s", t=TILES, q=4)
            for q in range(4):
                r = slice(32 * q, 32 * q + 32)
                note(dve.tensor_tensor(sc3[r], ps3[r, :, q, :], m3[r], ALU.mult))
            join()
            link(dve.tensor_tensor(SC, SC, NEGM, ALU.add))
            link(dve.tensor_reduce(pmax, sc3, AX.X, ALU.max))
            dve.tensor_tensor(sc3, sc3, over(pmax, 2, S), ALU.subtract).then_inc(a["masked"], 1)
            dve.wait_ge(a["exped"], 2)
            ex3 = EX.rearrange("p (t s) -> p t s", t=TILES)
            link(dve.tensor_reduce(psum_, ex3, AX.X, ALU.add))
            link(dve.tensor_tensor(psum_, psum_, pcnt, ALU.mult))
            link(dve.reciprocal(psum_, psum_))
            link(dve.tensor_tensor(ex3, ex3, over(psum_, 2, S), ALU.mult))
            dve.wait_ge(a["zeroed"], 1)
            mats = MATS.rearrange("p (t q s) -> p t q s", t=TILES, q=4)
            for q in range(4):
                r = slice(32 * q, 32 * q + 32)
                dve.transpose(mats[r, :, q, :], ex3[r]).then_inc(a["mats"], 1)
            dve.wait_ge(c2["bT_ps"], 1)
            dve.tensor_copy(POW[:, 0:P], bank(4)[:, 0:P]).then_inc(a["power0"], 1)

        def attention_pe(pe, i, src_ready):
            s, w = at[i], AW[i]
            pe.wait_ge((l_attn0, l_attn1)[i], 16)
            src_ready(pe)

            def project(j):
                if j >= 2:
                    pe.wait_ge(s["qk"], j - 1)
                src = H[:, j * PT:(j + 1) * PT]
                pe.matmul(bank(j % 2)[:, 0:PT], w["wq"], src, start=True, stop=True)
                pe.matmul(bank(j % 2)[:, PT:2 * PT], w["wk"], src, start=True, stop=True).then_inc(s["qk_ps"], 1)
                if j % 2:
                    return
                c = j // 2
                if c:
                    pe.wait_ge(s["v_act"], c)
                    pe.wait_ge(s["v_dve"], c)
                pe.matmul(bank(2), K["ones"][0:1, :], over(w["bv"][0:1, :], 1, TPC), start=True, stop=False)
                for t in range(TPC):
                    ins = pe.matmul(bank(2)[:, t * P:(t + 1) * P], H[:, c * CT + t * P:c * CT + (t + 1) * P], w["wv"],
                                    start=False, stop=t == TPC - 1)
                ins.then_inc(s["v_ps"], 1)

            def scores(j):
                pe.wait_ge(s["qk"], j + 1)
                for b in range(PB):
                    if b % 4 == 0 and j >= 2:
                        pe.wait_ge(s["biased"], 2 * (j - 2) + b // 4 + 1)
                    r = slice(b * P, (b + 1) * P)
                    o = score_bank(j, b // 4)[:, (b % 4) * P:(b % 4 + 1) * P]
                    ins = pe.matmul(o, Q2[j % 2][:, r], K2[j % 2][:, r], start=True, stop=True)
                    if b % 4 == 3:
                        ins.then_inc(s["s_ps"], 1)

            def mix(j):
                c = j // 2
                pe.wait_ge(s["probT"], j + 1)
                pe.wait_ge(s["v_act"], c + 1)
                pe.wait_ge(s["v_dve"], c + 1)
                if j:
                    pe.wait_ge(s["y"], j)
                for b in range(PB):
                    for h in range(HG):
                        at_v = ((j % 2) * PB + b) * P + h * S
                        at_p = b * P + h * S
                        ins = pe.matmul(bank(7)[32 * h:32 * h + 32, b * S:(b + 1) * S], V3[c % 3][:, at_v:at_v + S],
                                        T2[j % 2][:, at_p:at_p + S], start=True, stop=True, tile_position=(0, 32 * h))
                ins.then_inc(s["o_ps"], 1)
                pe.wait_ge(s["o"], j + 1)
                pe.matmul(bank(7)[:, PT:2 * PT], w["wo"], OT[j % 2], start=True, stop=True).then_inc(s["y_ps"], 1)

            project(0)
            project(1)
            scores(0)
            for j in range(PARTS + 2):
                if j + 1 < PARTS:
                    scores(j + 1)
                if j + 2 < PARTS:
                    project(j + 2)
                if j >= 2:
                    mix(j - 2)

        def attention_act(act, i):
            s, w = at[i], AW[i]

            def expand(j):
                if j >= 2:
                    act.wait_ge(s["s_ps"], 2 * (j - 1))
                act.wait_ge(s["qk_ps"], j + 1)
                q = bank(j % 2)[:, 0:PT].rearrange("p (b s) -> p b s", b=PB)
                for g in range(G):
                    act.activation(qv(Q2[j % 2])[:, :, g, :], q, ACT.Identity, bias=qbias[:, g:g + 1],
                                   scale=qscale[:, g:g + 1])
                k = bank(j % 2)[:, PT:2 * PT].rearrange("p (b s) -> p b s", b=PB)
                for h in range(HG):
                    ins = act.activation(qv(K2[j % 2])[:, :, h, :], k, ACT.Identity, bias=kbias[:, h:h + 1],
                                         scale=K["hmask"][:, h:h + 1])
                ins.then_inc(s["qk"], 1)
                if j % 2 == 0:
                    move_v(act, s, j // 2, 0, s["v_act"])

            act.wait_ge(s["scales"], 1)
            expand(0)
            expand(1)
            for j in range(PARTS + 2):
                if j + 2 < PARTS:
                    expand(j + 2)
                if j < PARTS:
                    act.wait_ge(s["shifted"], j + 1)
                    act.activation(S3[j % 3], S3[j % 3], ACT.Exp).then_inc(s["exped"], 1)
                    if i == 0:
                        act.activation(semt[j % 3], smax[j % 3], ACT.Exp, scale=-1.0).then_inc(s["emd"], 1)
                if j >= 2:
                    act.wait_ge(s["o_ps"], j - 1)
                    act.activation(OT[(j - 2) % 2], bank(7)[:, 0:PT], ACT.Copy).then_inc(s["o"], 1)

        def move_v(eng, s, c, half, done):
            if c == 0:
                eng.wait_ge(s["zeroed"], 1)
            if c >= 3:
                eng.wait_ge(s["o_ps"], 2 * (c - 2))
            eng.wait_ge(s["v_ps"], c + 1)
            v = bank(2).rearrange("p (t g h d) -> p t g h d", t=TPC, g=G, h=HG)
            dst = V3[c % 3].rearrange("p (t q h g d) -> p t q h g d", t=TPC, q=4, h=HG, g=G)
            for q in range(2 * half, 2 * half + 2):
                for g in range(G):
                    o, n = dst[32 * g:32 * g + 32, :, q, :, g, :], v[32 * q:32 * q + 32, :, g, :, :]
                    ins = eng.activation(o, n, ACT.Copy) if half == 0 else eng.tensor_copy(o, n)
            ins.then_inc(done, 1)

        def attention_pool(pool, i):
            s = at[i]
            if i == 1:
                pool.wait_ge(l1["tok"], CH)
                pool.memset(V_ALL, 0.0).then_inc(s["zeroed"], 1)
            for j in range(PARTS + 1):
                if j < PARTS:
                    rows = score_rows(j)
                    pool.wait_ge(s["maxed"], j + 1)
                    pool.tensor_tensor(rows, rows, over(smax[j % 3], 2, S), ALU.subtract).then_inc(s["shifted"], 1)
                if j:
                    rows = score_rows(j - 1)
                    pool.wait_ge(s["recip"], j)
                    pool.tensor_tensor(rows, rows, over(ssum[(j - 1) % 3], 2, S), ALU.mult).then_inc(s["normed"], 1)

        def attention_dve(dve, i):
            s, w = at[i], AW[i]
            dve.wait_ge((l_attn0, l_attn1)[i], 16)
            scale = 1.0 / float(np.sqrt(HD))
            note(dve.tensor_scalar(kbias, K["hmask"], w["bk"], None, ALU.mult))
            link(dve.tensor_scalar(qscale, K["gmask"], scale, None, ALU.mult))
            dve.tensor_scalar(qbias, qscale, w["bq"], None, ALU.mult).then_inc(s["scales"], 1)

            def scores(j):
                for n in range(2):
                    dve.wait_ge(s["s_ps"], 2 * j + n + 1)
                    o, p_ = S3[j % 3][:, n * CT:(n + 1) * CT], score_bank(j, n)
                    if i == 0:
                        o, p_ = (x.rearrange("p (r s) -> p r s", s=S) for x in (o, p_))
                        bias = over(K["causal"], 1, 4 * HG)
                    else:
                        o, p_ = (x.rearrange("p (b r) -> p b r", b=4) for x in (o, p_))
                        bias = over(K["alibi"], 1, 4)
                    dve.tensor_tensor(o, p_, bias, ALU.add).then_inc(s["biased"], 1)
                dve.wait_ge(s["biased"], 2 * j + 2)
                if i == 0:
                    link(dve.tensor_reduce(smax[j % 3], score_rows(j), AX.X, ALU.max))
                    dve.tensor_scalar(smax[j % 3], smax[j % 3], 0.0, None, ALU.max).then_inc(s["maxed"], 1)
                else:
                    dve.tensor_reduce(smax[j % 3], score_rows(j), AX.X, ALU.max).then_inc(s["maxed"], 1)

            def sums(j):
                dve.wait_ge(s["exped"], j + 1)
                link(dve.tensor_reduce(ssum[j % 3], score_rows(j), AX.X, ALU.add))
                if i == 0:
                    dve.wait_ge(s["emd"], j + 1)
                    link(dve.scalar_tensor_tensor(ssum[j % 3], semt[j % 3], K["empty"], ssum[j % 3], ALU.mult, ALU.add))
                dve.reciprocal(ssum[j % 3], ssum[j % 3]).then_inc(s["recip"], 1)

            def transpose(j):
                dve.wait_ge(s["normed"], j + 1)
                if j >= 2:
                    dve.wait_ge(s["o_ps"], j - 1)
                dve.transpose(T2[j % 2], S3[j % 3]).then_inc(s["probT"], 1)

            def residual(j):
                dve.wait_ge(s["y_ps"], j + 1)
                x = X[:, j * PT:(j + 1) * PT]
                dve.scalar_tensor_tensor(x, bank(7)[:, PT:2 * PT], w["bo"], x, ALU.add, ALU.add).then_inc(s["y"], 1)

            move_v(dve, s, 0, 1, s["v_dve"])
            for j in range(PARTS + 3):
                if j < PARTS:
                    if j >= 3:
                        dve.wait_ge(s["probT"], j - 2)
                    scores(j)
                if 1 <= j <= PARTS:
                    sums(j - 1)
                if j >= 3:
                    residual(j - 3)
                if 2 <= j <= PARTS + 1:
                    transpose(j - 2)
                if j + 2 < PARTS and j % 2 == 0:
                    move_v(dve, s, j // 2 + 1, 1, s["v_dve"])

        arena_at[0] = 0
        COEF, CTXT, WG, MOD, H1, SOMA, GATED, TPOOL, TDVE = (region(N) for _ in range(9))
        PP, PD = [region(CT) for _ in range(4)], [region(CT) for _ in range(2)]
        XC, SQ, YL, GATE, SOMAG = COEF, CTXT, GATED, WG, MOD
        nmean, nvar, nstd = cols(TILES), cols(TILES), cols(TILES)
        LAGS = lags()
        ON_DVE = [u % 3 == 2 for u in range(len(LAGS))]

        def ctx_pe(pe):
            pe.wait_ge(l_ctx, 16)
            pe.wait_ge(at[0]["y"], PARTS)
            for c in range(CH):
                pe.matmul(bank(c)[0:32, :], W2["Wn1"], chunk(X, c), start=True, stop=True).then_inc(c2["h1_ps"], 1)
            for c in range(CH):
                pe.matmul(bank(4 + c), W2["Wsoma"], chunk(X, c), start=True, stop=True).then_inc(c2["soma_ps"], 1)
            for c in range(CH):
                pe.wait_ge(c2["h1"], c + 1)
                pe.matmul(bank(c), W2["Wg0"], chunk(X, c), start=True, stop=False)
                pe.wait_ge(c2["scanned"], 1)
                pe.matmul(bank(c), W2["Wg1"], chunk(CTXT, c), start=False, stop=True).then_inc(c2["wg_ps"], 1)
            for c in range(CH):
                pe.wait_ge(c2["soma"], c + 1)
                pe.matmul(bank(4 + c), W2["Wn2"][0:32, :], H1[0:32, c * CT:(c + 1) * CT], start=True, stop=True)\
                    .then_inc(c2["mod_ps"], 1)
            pe.wait_ge(c2["mod_split"], 1)
            pe.wait_ge(c2["wg"], CH)
            pe.wait_ge(a["split"], 1)
            for u, (lag, b0, nb, even, valid) in enumerate(LAGS):
                if u >= 8:
                    pe.wait_ge(c2["prod"], u - 7)
                w = powers[:, lag * P:(lag + 1) * P]
                o = bank(u % 8)[:, 0:nb * even]
                for part in (mod_high, mod_low):
                    r = part[:, :].rearrange("p (b s) -> p b s", b=B)[:, b0:b0 + nb, 0:even]
                    ins = pe.matmul(o, w, r, start=part is mod_high, stop=part is mod_low)
                ins.then_inc(c2["lag_ps"], 1)
            for c in range(CH):
                pe.wait_ge(c2["temporal"], 1)
                pe.matmul(bank(c), W2["Wtemp"], chunk(TPOOL, c), start=True, stop=True).then_inc(c2["gate_ps"], 1)
            for t in range(TILES):
                if t % TPC == 0:
                    pe.wait_ge(c2["somagate"], t // TPC + 1)
                ins = pe.matmul(PS[:, 4 * CT + t * P:4 * CT + (t + 1) * P], SOMAG[:, t * P:(t + 1) * P], W2["Wout"],
                                start=True, stop=True)
                if t % TPC == TPC - 1:
                    ins.then_inc(c2["out_ps"], 1)
            pe.wait_ge(c2["gate"], CH)
            pe.wait_ge(ff["w"], 1)
            for k in range(3 * FT):
                ins = pe.transpose(PS[:, k * P:(k + 1) * P], t_ffn[:, k * P:(k + 1) * P], K["ident"])
            ins.then_inc(ff["wT_ps"], 1)
            pe.wait_ge(ff["wT"], 1)
            pe.wait_ge(c2["y"], 1)
            for t in range(TILES):
                ins = pe.transpose(PS[:, t * P:(t + 1) * P], YL[:, t * P:(t + 1) * P], K["ident"])
                if t % TPC == TPC - 1:
                    ins.then_inc(c2["y_ps"], 1)

        def ctx_act(act):
            for c in range(CH):
                act.wait_ge(c2["h1_ps"], c + 1)
                act.activation(H1[0:32, c * CT:(c + 1) * CT], bank(c)[0:32, :], ACT.Gelu, bias=W2["bn1"][0:32, :])\
                    .then_inc(c2["h1"], 1)
            for c in range(CH):
                act.wait_ge(c2["soma_ps"], c + 1)
                act.activation(chunk(SOMA, c), bank(4 + c), ACT.Gelu, bias=W2["bsoma"]).then_inc(c2["soma"], 1)
            for c in range(CH):
                act.wait_ge(c2["wg_ps"], c + 1)
                act.activation(chunk(WG, c), bank(c), ACT.Sigmoid, bias=W2["bg"]).then_inc(c2["wg"], 1)
            for c in range(CH):
                act.wait_ge(c2["mod_ps"], c + 1)
                act.activation(chunk(MOD, c), bank(4 + c), ACT.Sigmoid, bias=W2["bn2"]).then_inc(c2["mod"], 1)
            act.wait_ge(c2["gated"], 1)
            for c in range(CH):
                act.wait_ge(c2["gate_ps"], c + 1)
                act.activation(chunk(GATE, c), bank(c), ACT.Sigmoid, bias=W2["btemp"]).then_inc(c2["gate"], 1)
            act.wait_ge(ff["wT_ps"], 1)
            act.activation(wT[:, :], PS[:, 0:3 * FT * P], ACT.Copy).then_inc(ff["wT"], 1)
            act.wait_ge(c2["xc"], 1)
            act.activation(SQ, XC, ACT.Square).then_inc(c2["sq"], 1)
            act.wait_ge(c2["var"], 1)
            act.activation(nstd, nvar, ACT.Sqrt).then_inc(c2["std"], 1)
            for c in range(CH):
                act.wait_ge(c2["y_ps"], c + 1)
                act.activation(chunk(H, c), bank(c), ACT.Identity, bias=W2["beta"], scale=W2["gamma"]).then_inc(c2["yt"], 1)

        def ctx_pool(pool):
            pool.wait_ge(at[0]["y"], PARTS)
            first = COEF.rearrange("p (b s) -> p b s", s=S)
            pool.memset(first[:, :, 1:S], 1.0).then_inc(c2["ones"], 1)
            pool.memset(first[:, :, 0:1], 0.0).then_inc(c2["ones"], 1)
            pool.memset(TPOOL, 0.0).then_inc(c2["zeroed"], 1)
            pool.memset(TDVE, 0.0).then_inc(c2["zeroed"], 1)
            t3 = TPOOL.rearrange("p (b s) -> p b s", s=S)
            k = 0
            for u, (lag, b0, nb, even, valid) in enumerate(LAGS):
                if ON_DVE[u]:
                    continue
                pool.wait_ge(c2["prod"], u + 1)
                if k:
                    pool.wait_ge(c2["added"], k)
                else:
                    pool.wait_ge(c2["zeroed"], 2)
                o = t3[:, b0:b0 + nb, lag:S]
                pool.tensor_tensor(o, o, PP[k % 4][:, 0:nb * valid].rearrange("p (b s) -> p b s", b=nb), ALU.add)\
                    .then_inc(c2["added"], 1)
                k += 1

        def powers_dve(dve):
            dve.wait_ge(a["powers"], S - 1)
            link(dve.tensor_copy(powers[:, :], POW))
            dve.tensor_tensor(powers[TR:P, :], POW[TR:P], powers[TR:P, :].bitcast(f32), ALU.subtract).then_inc(a["split"], 1)

        def ctx_dve(dve):
            dve.wait_ge(c2["ones"], 2)
            link(dve.tensor_scalar(COEF, COEF, alpha_c, None, ALU.mult))
            dve.tensor_tensor_scan(CTXT, COEF, X[:, :], 0.0, ALU.mult, ALU.add).then_inc(c2["scanned"], 1)
            dve.wait_ge(l_ffn, 16)
            nb = 3 * FT * P // QB
            wb = t_ffn[:, :].rearrange("p (n b) -> p n b", b=QB)
            link(dve.tensor_reduce(wscale, wb, AX.X, ALU.max, apply_absolute_value=True))
            link(dve.tensor_scalar(wscale, wscale, 1.0 / 7.0, 1e-12, ALU.mult, ALU.max))
            link(dve.reciprocal(winv, wscale))
            link(dve.tensor_tensor(wb, wb, over(winv, 2, QB), ALU.mult))
            link(dve.tensor_scalar(t_ffn[:, :], t_ffn[:, :], MAGIC, MAGIC + 7.0, ALU.add, ALU.min))
            link(dve.tensor_scalar(t_ffn[:, :], t_ffn[:, :], MAGIC - 8.0, MAGIC, ALU.max, ALU.subtract))
            dve.tensor_tensor(wb, wb, over(wscale, 2, QB), ALU.mult).then_inc(ff["w"], 1)
            for c in range(CH):
                dve.wait_ge(c2["wg"], c + 1)
                ins = dve.tensor_tensor(chunk(GATED, c), chunk(X, c), chunk(WG, c), ALU.mult)
            ins.then_inc(c2["gated"], 1)
            dve.wait_ge(c2["mod"], CH)
            link(dve.tensor_scalar(MOD, MOD, 0.5, None, ALU.add))
            link(dve.tensor_copy(mod_high[:, :], MOD))
            dve.tensor_tensor(mod_low[:, :], MOD, mod_high[:, :].bitcast(f32), ALU.subtract).then_inc(c2["mod_split"], 1)
            dve.wait_ge(c2["gated"], 1)
            dve.wait_ge(c2["zeroed"], 2)
            g3 = GATED.rearrange("p (b s) -> p b s", s=S)
            t3 = TDVE.rearrange("p (b s) -> p b s", s=S)
            k = d = 0
            for u, (lag, b0, nb, even, valid) in enumerate(LAGS):
                dve.wait_ge(c2["lag_ps"], u + 1)
                if ON_DVE[u]:
                    to = PD[d % 2]
                    d += 1
                else:
                    if k >= 4:
                        dve.wait_ge(c2["added"], k - 3)
                    to = PP[k % 4]
                    k += 1
                prod = to[:, 0:nb * valid].rearrange("p (b s) -> p b s", b=nb)
                m = bank(u % 8)[:, 0:nb * even].rearrange("p (b s) -> p b s", b=nb)[:, :, 0:valid]
                dve.tensor_tensor(prod, m, g3[:, b0:b0 + nb, 0:valid], ALU.mult).then_inc(c2["prod"], 1)
                if ON_DVE[u]:
                    dve.wait_ge(c2["prod"], u + 1)
                    o = t3[:, b0:b0 + nb, lag:S]
                    link(dve.tensor_tensor(o, o, prod, ALU.add))
            dve.wait_ge(c2["added"], k)
            dve.tensor_tensor(TPOOL, TPOOL, TDVE, ALU.add).then_inc(c2["temporal"], 1)
            for c in range(CH):
                dve.wait_ge(c2["gate"], c + 1)
                dve.tensor_tensor(chunk(SOMAG, c), chunk(SOMA, c), chunk(GATE, c), ALU.mult).then_inc(c2["somagate"], 1)
            dve.wait_ge(c2["out_ps"], CH)
            o3 = bank(4, 4).rearrange("p (t d) -> p t d", t=TILES)
            x3 = XC.rearrange("p (t d) -> p t d", t=TILES)
            link(dve.tensor_reduce(nmean, o3, AX.X, ALU.add))
            link(dve.tensor_scalar(nmean, nmean, -1.0 / D, None, ALU.mult))
            dve.tensor_tensor(x3, o3, over(nmean, 2, D), ALU.add).then_inc(c2["xc"], 1)
            dve.wait_ge(c2["sq"], 1)
            link(dve.tensor_reduce(nvar, SQ.rearrange("p (t d) -> p t d", t=TILES), AX.X, ALU.add))
            dve.tensor_scalar(nvar, nvar, 1.0 / D, 1e-5, ALU.mult, ALU.add).then_inc(c2["var"], 1)
            dve.wait_ge(c2["std"], 1)
            link(dve.reciprocal(nstd, nstd))
            dve.tensor_tensor(YL.rearrange("p (t d) -> p t d", t=TILES), x3, over(nstd, 2, D), ALU.mult).then_inc(c2["y"], 1)

        arena_at[0] = 0
        U, GT, SG = (region(FT * N) for _ in range(3))
        wscale, winv = cols(3 * FT * P // QB), cols(3 * FT * P // QB)
        amx, amc, gsc = cols(2 * FT * CH), cols(4 + 1), cols(10)
        UNITS = [(f, c) for f in range(FT) for c in range(CH)]

        def span(t, f, c=None):
            return t[:, f * N:(f + 1) * N] if c is None else t[:, f * N + c * CT:f * N + (c + 1) * CT]

        MAXIMA = 5

        def global_max_pe(pe, n):
            pe.wait_ge(ff["amax"], n + 1)
            pe.transpose(bank(7)[0:1, 0:P], amc[:, n:n + 1], K["ident"]).then_inc(ff["amaxT_ps"], 1)
            pe.wait_ge(ff["gmax"], n + 1)
            pe.matmul(bank(7)[:, P:P + 2], K["ones"][0:1, :], over(gsc[0:1, 2 * n:2 * n + 1], 1, 2), start=True, stop=True)\
                .then_inc(ff["gmaxb_ps"], 1)

        def global_max_dve(dve, n, part):
            dve.tensor_reduce(amc[:, n:n + 1], part, AX.X, ALU.max).then_inc(ff["amax"], 1)
            dve.wait_ge(ff["amaxT_ps"], n + 1)
            dve.tensor_reduce(gsc[0:1, 2 * n:2 * n + 1], bank(7)[0:1, 0:P], AX.X, ALU.max).then_inc(ff["gmax"], 1)
            dve.wait_ge(ff["gmaxb_ps"], n + 1)
            link(dve.tensor_scalar(gsc[:, 2 * n:2 * n + 1], bank(7)[:, P:P + 1], 1.0 / QMAX, 1e-12, ALU.mult, ALU.max))
            dve.reciprocal(gsc[:, 2 * n + 1:2 * n + 2], gsc[:, 2 * n:2 * n + 1]).then_inc(ff["scale"], 1)

        def scale(n):
            return gsc[:, 2 * n:2 * n + 1]

        def inverse(n):
            return gsc[:, 2 * n + 1:2 * n + 2]

        def ffn_pe(pe):
            global_max_pe(pe, 0)
            pe.wait_ge(ff["hq"], 1)
            for v in range(2 * len(UNITS)):
                f, c = UNITS[v % len(UNITS)]
                if v >= 6:
                    pe.wait_ge(ff["copied"], v - 5)
                k = (0 if v < len(UNITS) else FT) + f
                pe.matmul(bank(v % 6), wT[:, k * P:(k + 1) * P], chunk(H, c), start=True, stop=True).then_inc(ff["up_ps"], 1)
            fuse_transposes_pe(pe)
            global_max_pe(pe, 1)
            global_max_pe(pe, 2)
            fuse_products_pe(pe)
            global_max_pe(pe, 3)
            global_max_pe(pe, 4)
            for f in range(FT):
                pe.wait_ge(ff["o"], f + 1)
                for c in range(CH):
                    if f == 0:
                        pe.wait_ge(mo["fuse_act"], 2)
                    ins = pe.matmul(bank(c), wT[:, (2 * FT + f) * P:(2 * FT + f + 1) * P], span(U, f, c),
                                    start=f == 0, stop=f == FT - 1)
                    if f == FT - 1:
                        ins.then_inc(ff["down_ps"], 1)

        def ffn_act(act):
            act.wait_ge(ff["hq"], 1)
            for v in range(2 * len(UNITS)):
                f, c = UNITS[v % len(UNITS)]
                act.wait_ge(ff["up_ps"], v + 1)
                act.activation(span(U if v < len(UNITS) else GT, f, c), bank(v % 6), ACT.Copy).then_inc(ff["copied"], 1)

            def to_integers(t, n):
                for f in range(FT):
                    act.activation(span(t, f), span(t, f), ACT.Identity, bias=K["magic"], scale=inverse(n))\
                        .then_inc(ff["magic"], 1)

            fuse_transposed_act(act)
            act.wait_ge(ff["scale"], 2)
            act.wait_ge(ff["copied"], 2 * len(UNITS))
            to_integers(GT, 1)
            fuse_act(act)
            act.wait_ge(ff["scale"], 3)
            for f in range(FT):
                act.wait_ge(ff["gq"], f + 1)
                act.activation(span(SG, f), span(GT, f), ACT.Sigmoid).then_inc(ff["sig"], 1)
            to_integers(U, 2)
            act.wait_ge(ff["scale"], 4)
            to_integers(GT, 3)
            act.wait_ge(ff["scale"], 5)
            act.wait_ge(ff["magic"], 3 * FT)
            to_integers(U, 4)

        def clamp(eng, t, f):
            return eng.tensor_scalar(span(t, f), span(t, f), MAGIC + QMAX, MAGIC - QMAX - 1.0, ALU.min, ALU.max)

        def dequant(eng, t, f, n):
            return eng.tensor_scalar(span(t, f), span(t, f), MAGIC, scale(n), ALU.subtract, ALU.mult)

        def ffn_pool(pool):
            fuse_pool(pool)
            for f in range(FT):
                pool.wait_ge(ff["magic"], FT + f + 1)
                clamp(pool, U, f).then_inc(ff["uq"], 1)
                pool.wait_ge(ff["uq"], 2 * f + 1)
                dequant(pool, U, f, 2).then_inc(ff["uq"], 1)

        def ffn_dve(dve):
            for c in range(CH):
                dve.wait_ge(c2["yt"], c + 1)
                link(dve.tensor_reduce(amx[:, c:c + 1], chunk(H, c), AX.X, ALU.max, apply_absolute_value=True))
            global_max_dve(dve, 0, amx[:, 0:CH])
            dve.wait_ge(ff["scale"], 1)
            link(dve.tensor_scalar(H[:, :], H[:, :], inverse(0), MAGIC, ALU.mult, ALU.add))
            link(dve.tensor_scalar(H[:, :], H[:, :], MAGIC + QMAX, MAGIC - QMAX - 1.0, ALU.min, ALU.max))
            dve.tensor_scalar(H[:, :], H[:, :], MAGIC, scale(0), ALU.subtract, ALU.mult).then_inc(ff["hq"], 1)
            for v in range(2 * FT):
                dve.wait_ge(ff["copied"], CH * (v + 1))
                ins = dve.tensor_reduce(amx[:, v:v + 1], span(U if v < FT else GT, v % FT), AX.X, ALU.max,
                                        apply_absolute_value=True)
            link(ins)
            global_max_dve(dve, 1, amx[:, FT:2 * FT])
            global_max_dve(dve, 2, amx[:, 0:FT])
            for f in range(FT):
                dve.wait_ge(ff["magic"], f + 1)
                link(clamp(dve, GT, f))
                dequant(dve, GT, f, 1).then_inc(ff["gq"], 1)
            for f in range(FT):
                dve.wait_ge(ff["sig"], f + 1)
                link(dve.tensor_scalar(span(SG, f), span(SG, f), 65536.0, MAGIC, ALU.mult, ALU.add))
                link(dve.tensor_scalar(span(SG, f), span(SG, f), MAGIC, MAGIC + 65535.0, ALU.max, ALU.min))
                link(dve.tensor_scalar(span(SG, f), span(SG, f), MAGIC, 1.0 / 65536.0, ALU.subtract, ALU.mult))
                link(dve.tensor_tensor(span(GT, f), span(GT, f), span(SG, f), ALU.mult))
                link(dve.tensor_reduce(amx[:, f:f + 1], span(GT, f), AX.X, ALU.max, apply_absolute_value=True))
            global_max_dve(dve, 3, amx[:, 0:FT])
            for f in range(FT):
                dve.wait_ge(ff["magic"], 2 * FT + f + 1)
                link(clamp(dve, GT, f))
                link(dequant(dve, GT, f, 3))
                dve.wait_ge(ff["uq"], 2 * f + 2)
                dve.tensor_tensor(span(U, f), span(U, f), span(GT, f), ALU.mult).then_inc(ff["om"], 1)
                dve.wait_ge(ff["om"], f + 1)
                link(dve.tensor_reduce(amx[:, f:f + 1], span(U, f), AX.X, ALU.max, apply_absolute_value=True))
            global_max_dve(dve, 4, amx[:, 0:FT])
            for f in range(FT):
                dve.wait_ge(ff["magic"], 3 * FT + f + 1)
                link(clamp(dve, U, f))
                dequant(dve, U, f, 4).then_inc(ff["o"], 1)
            for c in range(CH):
                dve.wait_ge(ff["down_ps"], c + 1)
                dve.tensor_tensor(chunk(X, c), chunk(X, c), bank(c), ALU.add).then_inc(ff["x"], 1)

        arena_at[0] = 0
        TOK, HOT = region(N), region(N)
        idcol = cols(B)
        gbias, gbias_x = cols(2 + E), cols(E)

        def own_pe(pe, s, loaded, bias, rows, x_ready):
            pe.wait_ge(s["hot"], 1)
            pe.wait_ge(l_sel, 16)
            pe.wait_ge(loaded, 16 * B)
            x_ready(pe)
            for t in range(TILES):
                o = PS[:, 4 * CT + t * P:4 * CT + (t + 1) * P]
                pe.matmul(o, HOT[0:rows, t * P:(t + 1) * P], bias[0:rows, :], start=True, stop=False)
                for q in range(4):
                    b = 4 * t + q
                    ins = pe.matmul(o[32 * q:32 * q + 32, :], X[:, b * S:(b + 1) * S], chosen[:, b * P:(b + 1) * P],
                                    start=False, stop=True, tile_position=(0, 32 * q))
                ins.then_inc(s["ps"], 1)
            for t in range(TILES):
                if t % TPC == 0:
                    pe.wait_ge(s["tok"], t // TPC + 1)
                ins = pe.transpose(PS[:, t * P:(t + 1) * P], TOK[:, t * P:(t + 1) * P], K["ident"])
                if t % TPC == TPC - 1:
                    ins.then_inc(s["tr_ps"], 1)

        def own_act(act, s):
            for c in range(CH):
                act.wait_ge(s["ps"], TPC * (c + 1))
                act.activation(chunk(TOK, c), bank(4 + c), ACT.Copy).then_inc(s["tok"], 1)
            for c in range(CH):
                act.wait_ge(s["tr_ps"], c + 1)
                act.activation(chunk(H, c), bank(c), ACT.Copy).then_inc(s["h"], 1)

        def own_dve(dve, s, ids):
            link(dve.tensor_copy(idcol, ids))
            dve.tensor_scalar(HOT.rearrange("p (b s) -> p b s", b=B), over(idcol, 2, S), K["index"], None, ALU.is_equal)\
                .then_inc(s["hot"], 1)

        arena_at[0] = 0
        TOKN = region(N)
        XF = region(N)
        SB, HH = ([region(CT) for _ in range(3)] for _ in range(2))
        ACC, Y, YSQ = region(CT), region(CT), region(CT)
        OUTT = [region(CT) for _ in range(2)]
        WTX = region(CT)
        LG, BI, SEL_, TA = (region(TILES * E) for _ in range(4))
        PAIR, PAIR2 = region(TILES * E * E), region(TILES * E * E)
        rmx, rsm = region(TILES), region(TILES)
        WX = region(2 * TILES * 8)
        ss, rstd, half = (region(TPC) for _ in range(3))
        ORDER = [2, 0, 1, 3, 4, 5, 6, 7]
        UN = len(ORDER)
        NCH = 2 * CH
        ALL = UN * NCH
        GROUPS = [range(0, CH), range(CH, CH + 2), range(CH + 2, NCH)]
        UP_HIGH, UP_LOW, GT_HIGH, GT_LOW = (powers[:, n * UN * P:(n + 1) * UN * P] for n in range(4))
        WUP, WSUP = t_moe[:, 0:E * P], MW["Sup"]

        def unit(u):
            return u // UN, u % UN, ORDER[u % UN]

        def piece(t, k):
            return t[:, k * P:(k + 1) * P]

        def source(n):
            return chunk(H if n < CH else XF, n % CH)

        def moe_pe(pe):
            pe.wait_ge(l_moe, 16)
            pe.wait_ge(mo["fused"], 1)

            def logits(g):
                for n in GROUPS[g]:
                    if n < CH:
                        pe.wait_ge(l2["h"], n + 1)
                    else:
                        pe.wait_ge(mo["xf"], n - CH + 1)
                    for t in range(TPC):
                        at_t = 8 * ((n - GROUPS[g][0]) * TPC + t)
                        ins = pe.matmul(bank(7)[:, at_t:at_t + E], source(n)[:, t * P:(t + 1) * P],
                                        MW["rW"][:, (n // CH) * E:(n // CH + 1) * E], start=True, stop=True)
                ins.then_inc(mo["logit_ps"], 1)

            def up_gate(u):
                n, _, k = unit(u)
                if n == 0:
                    pe.wait_ge(mo["split"], 1)
                else:
                    pe.wait_ge(mo["xsplit"], n)
                if u >= 2:
                    pe.wait_ge(mo["hh"], u - 1)
                for to, high, low, done in ((bank(u % 2), UP_HIGH, UP_LOW, mo["up_ps"]),
                                            (bank(2 + u % 2), GT_HIGH, GT_LOW, mo["gt_ps"])):
                    xh, xl = chunk(mod_high, n % CH), chunk(mod_low, n % CH)
                    pe.matmul(to, piece(high, k), xh, start=True, stop=False)
                    pe.matmul(to, piece(high, k), xl, start=False, stop=False)
                    pe.matmul(to, piece(low, k), xh, start=False, stop=True).then_inc(done, 1)

            def down(u):
                n, _, k = unit(u)
                pe.wait_ge(mo["hh"], u + 1)
                if k >= 2:
                    v = E * n + k - 2
                    if v >= 2:
                        pe.wait_ge(mo["eo"], v - 1)
                    to, w = bank(4 + v % 2), piece(MW["Wdn"], k - 2)
                else:
                    if n and k == 0:
                        pe.wait_ge(mo["y"], n)
                    to, w = bank(6), MW["Sdn"]
                for t in range(TPC):
                    ins = pe.matmul(to[:, t * P:(t + 1) * P], HH[u % 3][:, t * P:(t + 1) * P], w,
                                    start=k >= 2 or (k == 0 and t == 0), stop=k >= 2, skip_group_check=True)
                ins.then_inc(mo["dn_ps"], 1)

            def tail(n):
                if n < CH:
                    pe.wait_ge(mo["normed"], n + 1)
                src = chunk(TOKN if n < CH else X, n % CH)
                for t in range(TPC):
                    ins = pe.transpose(bank(7)[:, t * P:(t + 1) * P], src[:, t * P:(t + 1) * P], K["ident"])
                ins.then_inc(mo["tr_ps"], 1)

            def beside(n, k):
                if k == 1 and n in (3, 5):
                    pe.wait_ge(mo["wT"], n)
                    logits((n - 1) // 2)
                if k == 3 and n:
                    pe.wait_ge(mo["wT"], n)
                    pe.wait_ge(mo["logit"], 1 + (n >= 3) + (n >= 5))
                    tail(n - 1)
                if k == 5:
                    if n == 0:
                        pe.wait_ge(mo["logit"], 1)
                    elif n <= CH:
                        pe.wait_ge(mo["xf"], n)
                    else:
                        pe.wait_ge(mo["fin"], n - CH)
                    pe.wait_ge(mo["w"], 1 + (n >= CH) + (n >= CH + 2))
                    for t in range(TPC):
                        at_t = 8 * (TPC * n + t)
                        ins = pe.transpose(bank(7)[0:8, t * P:(t + 1) * P], WX[:, at_t:at_t + 8], K["ident"])
                    ins.then_inc(mo["wT_ps"], 1)
                if k == 7:
                    pe.wait_ge(mo["wT"], n + 1)
                    for t in range(TPC):
                        ins = pe.matmul(bank(6)[:, t * P:(t + 1) * P], WTX[0:8, t * P:(t + 1) * P], MW["bdn"][0:8, :],
                                        start=False, stop=True, skip_group_check=True)
                    ins.then_inc(mo["acc_ps"], 1)

            logits(0)
            up_gate(0)
            for u in range(ALL):
                if u + 1 < ALL:
                    up_gate(u + 1)
                beside(u // UN, u % UN)
                down(u)
            tail(NCH - 1)

        def moe_act(act):
            def gated(u):
                n, _, k = unit(u)
                act.wait_ge(mo["gt_ps"], u + 1)
                if u >= 3:
                    act.wait_ge(mo["hh"], u - 2)
                act.activation(SB[u % 3], bank(2 + u % 2), ACT.Silu, bias=gbias[:, k:k + 1]).then_inc(mo["s"], 1)

            def weigh(g):
                nt = TPC * len(GROUPS[g])
                act.wait_ge(mo["masked"], g + 1)
                act.activation(TA[:, 0:nt * E], TA[:, 0:nt * E], ACT.Exp).then_inc(mo["exped"], 1)

            act.wait_ge(mo["fused"], 1)
            weigh(0)
            for u in range(ALL):
                n, at_k, _ = unit(u)
                gated(u)
                if at_k == 5 and n in (3, 5):
                    weigh((n - 1) // 2)

        def moe_pool(pool):
            pool.wait_ge(l2["tok"], CH)
            pool.memset(half, -0.5).then_inc(mo["half"], 1)
            pool.memset(WX, 1.0).then_inc(mo["half"], 1)
            pool.wait_ge(mo["half"], 2)

            def split(n):
                x, high, low = source(n), chunk(mod_high, n % CH), chunk(mod_low, n % CH)
                if n < CH:
                    pool.wait_ge(l2["h"], n + 1)
                else:
                    pool.wait_ge(mo["xf"], n - CH + 1)
                pool.tensor_copy(high, x).then_inc(mo["xhigh"], 1)
                pool.wait_ge(mo["xhigh"], n)
                pool.tensor_tensor(low, x, high.bitcast(f32), ALU.subtract).then_inc(mo["xsplit"], 1)

            for n in range(1, CH):
                split(n)
            for n in range(NCH):
                pool.wait_ge(mo["y"], n + 1)
                pool.tensor_tensor(YSQ, Y, Y, ALU.mult).then_inc(mo["sq"], 1)
                pool.wait_ge(mo["ss"], n + 1)
                pool.tensor_tensor(rstd, ss, half, ALU.pow).then_inc(mo["rstd"], 1)
                if n < CH:
                    split(CH + n)

        def moe_dve(dve):
            def logit(g):
                nt = TPC * len(GROUPS[g])
                i = GROUPS[g][0] // CH
                lg = LG[:, 0:nt * E].rearrange("p (t e) -> p t e", t=nt)
                dve.wait_ge(mo["logit_ps"], g + 1)
                b7 = bank(7)[:, 0:8 * nt].rearrange("p (t e) -> p t e", t=nt)[:, :, 0:E]
                dve.tensor_tensor(lg, b7, over(MW["rb"][:, i * E:(i + 1) * E], 1, nt), ALU.add).then_inc(mo["logit"], 1)

            def choose(g):
                nt = TPC * len(GROUPS[g])
                i = GROUPS[g][0] // CH
                lgf, bif, self_, taf = (x[:, 0:nt * E] for x in (LG, BI, SEL_, TA))
                pf, qf = (x[:, 0:nt * E * E] for x in (PAIR, PAIR2))
                lg, bi, sel, ta = (x.rearrange("p (t e) -> p t e", t=nt) for x in (lgf, bif, self_, taf))
                p4, q4 = (x.rearrange("p (t e f) -> p t e f", t=nt, e=E) for x in (pf, qf))
                dve.wait_ge(mo["logit"], g + 1)
                link(dve.tensor_tensor(bi, lg, over(MW["gb"][:, i * E:(i + 1) * E], 1, nt), ALU.add))
                note(dve.tensor_tensor(p4, over(bi, 2, E), over(bi, 3, E), ALU.is_gt))
                link(dve.tensor_tensor(q4, over(bi, 2, E), over(bi, 3, E), ALU.is_equal))
                q3 = qf.rearrange("p (t e) -> p t e", t=nt)
                link(dve.tensor_tensor(q3, q3, over(K["tri"], 1, nt), ALU.mult))
                link(dve.tensor_tensor(pf, pf, qf, ALU.add))
                link(dve.tensor_reduce(sel, p4, AX.X, ALU.add))
                link(dve.tensor_scalar(self_, self_, 2.0, None, ALU.is_lt))
                note(dve.tensor_tensor(bif, lgf, self_, ALU.mult))
                link(dve.tensor_scalar(taf, self_, 1.0, NEG, ALU.subtract, ALU.mult))
                link(dve.tensor_tensor(taf, taf, bif, ALU.add))
                link(dve.tensor_reduce(rmx[:, 0:nt], ta, AX.X, ALU.max))
                dve.tensor_tensor(ta, ta, over(rmx[:, 0:nt], 2, E), ALU.subtract).then_inc(mo["masked"], 1)

            def weights(g):
                nt = TPC * len(GROUPS[g])
                first = 8 * TPC * GROUPS[g][0]
                w3 = WX[:, first:first + 8 * nt].rearrange("p (t e) -> p t e", t=nt)[:, :, 0:E]
                ta = TA[:, 0:nt * E].rearrange("p (t e) -> p t e", t=nt)
                dve.wait_ge(mo["exped"], g + 1)
                if g == 0:
                    dve.wait_ge(mo["half"], 2)
                link(dve.tensor_reduce(rsm[:, 0:nt], ta, AX.X, ALU.add))
                link(dve.reciprocal(rsm[:, 0:nt], rsm[:, 0:nt]))
                dve.tensor_tensor(w3, ta, over(rsm[:, 0:nt], 2, E), ALU.mult).then_inc(mo["w"], 1)
                dve.wait_ge(mo["w"], g + 1)

            def hidden(u):
                _, _, k = unit(u)
                bias = MW["sbup"][:, k:k + 1] if k < 2 else MW["bup"][:, k - 2:k - 1]
                dve.wait_ge(mo["up_ps"], u + 1)
                dve.wait_ge(mo["s"], u + 1)
                if u >= 3:
                    dve.wait_ge(mo["dn_ps"], u - 2)
                dve.scalar_tensor_tensor(HH[u % 3], bank(u % 2), bias, SB[u % 3], ALU.add, ALU.mult).then_inc(mo["hh"], 1)

            def combine(u):
                n, _, k = unit(u)
                if k < 2:
                    return
                e = k - 2
                v = E * n + e
                dve.wait_ge(mo["dn_ps"], u + 1)
                if v:
                    dve.wait_ge(mo["eo"], v)
                if e == 0 and n:
                    dve.wait_ge(mo["y"], n)
                if e == 0 and n >= CH:
                    dve.wait_ge(mo["normed"], n - CH + 1)
                for t in range(TPC):
                    r = slice(t * P, (t + 1) * P)
                    at_w = 8 * (TPC * n + t) + e
                    base = chunk(TOKN, n % CH) if e == 0 else ACC
                    ins = dve.scalar_tensor_tensor(ACC[:, r], bank(4 + v % 2)[:, r], WX[:, at_w:at_w + 1], base[:, r],
                                                   ALU.mult, ALU.add)
                ins.then_inc(mo["eo"], 1)

            def total(n):
                dve.wait_ge(mo["eo"], E * (n + 1))
                dve.wait_ge(mo["acc_ps"], n + 1)
                dve.wait_ge(mo["dn_ps"], UN * n + 3)
                if n:
                    dve.wait_ge(mo["normed"], n)
                dve.tensor_tensor(Y, ACC, bank(6), ALU.add).then_inc(mo["y"], 1)

            def sum_squares(n):
                dve.wait_ge(mo["sq"], n + 1)
                link(dve.tensor_reduce(ss, YSQ.rearrange("p (t d) -> p t d", t=TPC), AX.X, ALU.add))
                dve.tensor_scalar(ss, ss, 1.0 / D, 1e-6, ALU.mult, ALU.add).then_inc(mo["ss"], 1)

            def norm(n):
                i = n // CH
                dve.wait_ge(mo["rstd"], n + 1)
                if n >= CH:
                    dve.wait_ge(mo["tr_ps"], n - CH + 1)
                for t in range(TPC):
                    r = slice(t * P, (t + 1) * P)
                    ins = dve.scalar_tensor_tensor(chunk(TOKN, n % CH)[:, r], Y[:, r], rstd[:, t:t + 1],
                                                   MW["norm"][:, i * P:(i + 1) * P], ALU.mult, ALU.mult)
                ins.then_inc(mo["normed"], 1)

            def finish(n):
                dve.wait_ge(mo["tr_ps"], n + 1)
                if n < CH:
                    dve.tensor_copy(chunk(XF, n), bank(7)).then_inc(mo["xf"], 1)
                else:
                    dve.wait_ge(mo["normed"], n + 1)
                    if n >= CH + 2:
                        dve.wait_ge(stored[n % 2], 16 * ((n - CH) // 2))
                    dve.tensor_tensor(OUTT[n % 2], chunk(TOKN, n % CH), bank(7), ALU.add).then_inc(mo["fin"], 1)

            dve.wait_ge(l2["h"], 1)
            link(dve.tensor_copy(chunk(mod_high, 0), chunk(H, 0)))
            dve.tensor_tensor(chunk(mod_low, 0), chunk(H, 0), chunk(mod_high, 0).bitcast(f32), ALU.subtract)\
                .then_inc(mo["split"], 1)
            logit(0)
            choose(0)
            for u in range(ALL):
                n, at_k, _ = unit(u)
                hidden(u)
                if u == 0:
                    weights(0)
                if u:
                    combine(u - 1)
                if at_k == 0 and n:
                    total(n - 1)
                if at_k == 1 and n:
                    sum_squares(n - 1)
                if at_k == 2:
                    if n:
                        norm(n - 1)
                    if n in (3, 5):
                        logit((n - 1) // 2)
                if at_k == 4 and n:
                    finish(n - 1)
                if at_k == 5 and n in (3, 5):
                    choose((n - 1) // 2)
                if at_k == 6:
                    dve.wait_ge(mo["wT_ps"], n + 1)
                    if n:
                        dve.wait_ge(mo["acc_ps"], n)
                    dve.tensor_copy(WTX[0:8, :], bank(7)[0:8, :]).then_inc(mo["wT"], 1)
                if at_k == 7 and n in (3, 5):
                    weights((n - 1) // 2)
            combine(ALL - 1)
            total(NCH - 1)
            sum_squares(NCH - 1)
            norm(NCH - 1)
            finish(NCH - 1)

        arena_at[0] = 3 * FT * N
        UPT, GTW = region(UN * P), region(UN * P)

        def fuse_transposes_pe(pe):
            pe.wait_ge(l_moe, 16)
            pe.wait_ge(ff["copied"], 2 * len(UNITS))
            for k in range(UN):
                w = piece(WSUP, k) if k < 2 else piece(WUP, k - 2)
                ins = pe.transpose(PS[:, k * P:(k + 1) * P], w, K["ident"])
            ins.then_inc(mo["fuse_ps"], 1)

        def fuse_products_pe(pe):
            pe.wait_ge(mo["fuse_act"], 1)
            for k in range(UN):
                gt = MW["Sgt"] if k < 2 else piece(MW["Wgt"], k - 2)
                bias = MW["sbup"][:, k:k + 1] if k < 2 else MW["bup"][:, k - 2:k - 1]
                pe.matmul(PS[:, 2 * CT + k * P:2 * CT + (k + 1) * P], piece(UPT, k), gt, start=True, stop=True)
                ins = pe.matmul(bank(4)[:, 2 * k:2 * k + 2], gt, over(bias, 1, 2), start=True, stop=True)
            ins.then_inc(mo["fuse_ps"], 1)

        def fuse_transposed_act(act):
            act.wait_ge(mo["fuse_ps"], 1)
            act.activation(UPT, bank(0, 2), ACT.Copy).then_inc(mo["fuse_act"], 1)

        def fuse_act(act):
            act.wait_ge(mo["fuse_ps"], 2)
            act.activation(GTW, bank(2, 2), ACT.Copy)
            act.activation(GT_HIGH, bank(2, 2), ACT.Copy)
            act.activation(UP_HIGH[:, 0:2 * P], WSUP, ACT.Copy)
            act.activation(UP_HIGH[:, 2 * P:UN * P], WUP, ACT.Copy)
            act.activation(gbias[:, 0:2], bank(4)[:, 0:4:2], ACT.Identity, bias=MW["sbgt"])
            act.activation(gbias_x, bank(4)[:, 4:2 * UN:2], ACT.Copy).then_inc(mo["fuse_act"], 1)

        def fuse_pool(pool):
            pool.wait_ge(mo["fuse_act"], 2)
            pool.tensor_tensor(GT_LOW, GTW, GT_HIGH.bitcast(f32), ALU.subtract)
            pool.tensor_tensor(UP_LOW[:, 0:2 * P], WSUP, UP_HIGH[:, 0:2 * P].bitcast(f32), ALU.subtract)
            pool.tensor_tensor(UP_LOW[:, 2 * P:UN * P], WUP, UP_HIGH[:, 2 * P:UN * P].bitcast(f32), ALU.subtract)
            pool.tensor_tensor(gbias[:, 2:UN], gbias_x, MW["bgt"], ALU.add).then_inc(mo["fused"], 1)

        STAGES = stage

        @block.sync
        def _(sp):
            for dst, src, s in ((t_const, consts, l_const), (t_cond, cond, l_const), (X, x_fm, l_x), (x_tok, x_tm, l_x),
                                (t_int, ints, l_int), (t_attn[0], attn0, l_attn0), (t_ctx, ctx_w, l_ctx),
                                (t_ffn, ffn_w, l_ffn), (t_sel, sel_w, l_sel), (t_attn[1], attn1, l_attn1),
                                (t_moe, moe_w, l_moe)):
                sp.dma_start(dst[:, :], src).then_inc(s, 16)
            sp.wait_ge(l_int, 16)
            sp.wait_ge(a["split"], 1)
            for b in range(B):
                i = sp.value_load(IN["subject"][0:1, b:b + 1], min_val=0, max_val=NSUB - 1)
                sp.dma_start(chosen[:, b * P:(b + 1) * P],
                             w_subject[bass.ds(i, 1), :, :].rearrange("a p n -> p (a n)")).then_inc(chosen1, 16)
            if stage >= 5:
                sp.wait_ge(l1["ps"], TILES)
                for b in range(B):
                    i = sp.value_load(IN["category"][0:1, b:b + 1], min_val=0, max_val=NCAT - 1)
                    sp.dma_start(chosen[:, b * P:(b + 1) * P],
                                 w_category[bass.ds(i, 1), :, :].rearrange("a p n -> p (a n)")).then_inc(chosen2, 16)
                for j in range(CH):
                    sp.wait_ge(mo["fin"], j + 1)
                    sp.dma_start(out[:, j * CT:(j + 1) * CT], OUTT[j % 2]).then_inc(stored[j % 2], 16)
                for s in stored:
                    sp.wait_ge(s, 16 * CH // 2)
            else:
                last = {1: at[0]["y"], 2: c2["yt"], 3: ff["x"], 4: at[1]["y"], 6: l1["h"]}[stage]
                sp.wait_ge(last, PARTS if stage in (1, 4) else CH)
                sp.wait_ge(chosen1, 16 * B)
                sp.dma_start(out, (H if stage == 2 else X)[:, :]).then_inc(stored[0], 16)
                sp.wait_ge(stored[0], 16)

        @block.tensor
        def _(pe):
            pooling_pe(pe)
            attention_pe(pe, 0, lambda e: e.wait_ge(a["h"], CH))
            if STAGES >= 2:
                ctx_pe(pe)
            if STAGES >= 3:
                ffn_pe(pe)
            if STAGES >= 4:
                own_pe(pe, l1, chosen1, SW["bias1"], NSUB, lambda e: e.wait_ge(ff["x"], CH))
                attention_pe(pe, 1, lambda e: e.wait_ge(l1["h"], CH))
            if STAGES >= 5:
                own_pe(pe, l2, chosen2, SW["bias2"], NCAT, lambda e: e.wait_ge(at[1]["y"], PARTS))
                moe_pe(pe)

        @block.scalar
        def _(act):
            pooling_act(act)
            attention_act(act, 0)
            if STAGES >= 2:
                ctx_act(act)
            if STAGES >= 3:
                ffn_act(act)
            if STAGES >= 4:
                own_act(act, l1)
                attention_act(act, 1)
            if STAGES >= 5:
                own_act(act, l2)
                moe_act(act)

        @block.gpsimd
        def _(pool):
            pooling_pool(pool)
            attention_pool(pool, 0)
            if STAGES >= 2:
                ctx_pool(pool)
            if STAGES >= 3:
                ffn_pool(pool)
            if STAGES >= 4:
                attention_pool(pool, 1)
            if STAGES >= 5:
                moe_pool(pool)

        @block.vector
        def _(dve):
            pooling_dve(dve)
            attention_dve(dve, 0)
            powers_dve(dve)
            if STAGES >= 2:
                ctx_dve(dve)
            if STAGES >= 3:
                ffn_dve(dve)
            if STAGES >= 4:
                own_dve(dve, l1, IN["subject"])
                attention_dve(dve, 1)
            if STAGES >= 5:
                own_dve(dve, l2, IN["category"])
                moe_dve(dve)


def columns(spec, arrays):
    out = np.zeros((P, width(spec)), np.float32)
    at = 0
    for name, w in spec:
        x = np.asarray(arrays[name])
        out[:x.shape[0], at:at + w] = x.reshape(x.shape[0], w)
        at += w
    return out


def constants():
    p = np.arange(P)
    q, g = p % S, p // S
    k = np.arange(S)
    slopes = np.power(np.float32(2.0), -8.0 * np.arange(1, HEADS + 1, dtype=np.float32) / HEADS)
    head = g[:, None] * HG + np.arange(HG)[None, :]
    causal = k[None, :] <= q[:, None]
    rel = np.abs(q[:, None] - k[None, :]).astype(np.float32)
    alibi = np.where(causal[:, None, :], -slopes[head][:, :, None] * rel[:, None, :], np.float32(-NEG))
    e = np.arange(E)
    return columns(CONST, {
        "ident": np.eye(P), "alibi": alibi, "causal": np.where(causal, 0.0, -NEG), "pre": causal,
        "post": k[None, :] >= q[:, None], "cloze": k[None, :] != q[:, None], "empty": (WINDOW - 1 - q)[:, None],
        "hmask": (p[:, None] // HD) % HG == np.arange(HG)[None, :], "gmask": g[:, None] == np.arange(G)[None, :],
        "index": p[:, None], "tri": np.broadcast_to((e[None, :] < e[:, None]).reshape(1, -1), (P, E * E)),
        "ones": np.ones((P, P)), "magic": np.full((P, 1), MAGIC)})


def kernel(**inputs):
    import concourse.bacc as bacc
    from concourse.bass_utils import run_bass_kernel_spmd

    a = {k: np.asarray(v) for k, v in inputs.items()}

    def heads(w):
        return w.T.reshape(G, HG, HD, D).transpose(1, 0, 2, 3).reshape(D, D)

    def col(v):
        return v.reshape(-1, 1)

    def twice(v):
        return np.concatenate([v, v])

    def attn(wq, wk, wv, wo, bq, bk, bv, bo):
        return columns(ATTN, {"wq": wq.T, "wk": wk.T, "wv": wv.T, "wo": heads(wo), "bv": bv.reshape(1, -1),
                              "bq": col(bq), "bk": col(bk), "bo": col(bo)})

    def rows(v):
        return np.broadcast_to(v.reshape(1, -1), (P, v.size))

    def blocks(w):
        return w.reshape(-1, P, w.shape[1]).transpose(1, 0, 2).reshape(P, -1)

    def side(w):
        return w.transpose(1, 0, 2).reshape(w.shape[1], -1)

    x = a["x"].reshape(N, D)
    arrays = {
        "consts": constants(),
        "cond": columns(COND, {"W1": a["L0_cond_W1"], "b1": col(a["L0_cond_b1"]),
                               "vrep": np.broadcast_to(col(a["L0_cond_v"]), (32, P)),
                               "blend": twice(a["cond_1024"]).T, "tau_raws": col(twice(a["condB_tauraws"])),
                               "tau_ctx": np.broadcast_to(a["L0_cond2_tau_ctx"].reshape(1, 1), (P, 1))}),
        "attn0": attn(*(a["L0_attn_" + n] for n in ("wq", "wk", "wv", "wo", "bq", "bk", "bv", "bo"))),
        "ctx_w": columns(CTX, {"Wg0": a["L0_cond2_Wg"][:, :D].T, "Wg1": a["L0_cond2_Wg"][:, D:].T,
                               "Wsoma": a["L0_cond2_Wsoma"].T, "Wtemp": a["L0_cond2_Wtemp"].T,
                               "Wout": a["L0_cond2_Wout"].T, "Wn1": a["L0_cond2_Wn1"].T, "Wn2": twice(a["cond_256"]).T,
                               "bg": col(a["L0_cond2_bg"]), "bn1": col(a["L0_cond2_bn1"]), "bn2": col(twice(a["condB_bn2"])),
                               "bsoma": col(a["L0_cond2_bsoma"]), "btemp": col(a["L0_cond2_btemp"]),
                               "gamma": col(a["L0_cond2_gamma"]), "beta": col(a["L0_cond2_beta"])}),
        "ffn_w": columns(FFN, {"up": blocks(a["L0_ffn_w_up"]), "gate": blocks(a["L0_ffn_w_gate"]), "down": a["L0_ffn_w_down"]}),
        "attn1": attn(*(a["L1_attn_" + n] for n in ("Wq", "Wk", "Wv", "Wo", "bq", "bk", "bv", "bo"))),
        "sel_w": columns(SEL, {"bias1": a["L1_cond_bias"], "bias2": a["L1_cond2_b"]}),
        "moe_w": columns(MOE, {
            "Wup": side(a["L1_ffn_exp_Wup"]), "Wgt": side(a["L1_ffn_exp_Wg"]), "Wdn": side(a["L1_ffn_exp_Wdown"]),
            "Sup": a["L1_ffn_share_Wup"], "Sgt": a["L1_ffn_share_Wg"], "Sdn": a["L1_ffn_share_Wdown"],
            "bdn": np.concatenate([a["L1_ffn_exp_bdown"], twice(a["L1_ffn_share_bdown"].reshape(1, -1))]),
            "norm": rows(a["L1_ffn_norm_w"]), "rW": side(a["L1_ffn_router_W"]), "rb": rows(a["L1_ffn_router_b"]),
            "gb": rows(a["L1_ffn_gate_bias"]), "bup": a["L1_ffn_exp_bup"].T, "bgt": a["L1_ffn_exp_bg"].T,
            "sbup": a["L1_ffn_share_bup"].reshape(2, D).T, "sbgt": col(a["L1_ffn_share_bg"])}),
        "ints": np.concatenate([np.repeat(a["itok_B_0_2"].reshape(TILES, 4).T, S, axis=0),
                                rows(a["itok_B_0_7"]), rows(a["itok_B_0_30"])], axis=1).astype(np.int32),
        "x_fm": x.T, "x_tm": x.reshape(TILES, P, D).transpose(1, 0, 2).reshape(P, N),
        "w_subject": a["L1_cond_weight"].transpose(0, 2, 1), "w_category": a["L1_cond2_W"],
    }
    arrays = {k: np.ascontiguousarray(v) for k, v in arrays.items()}
    nc = bacc.Bacc("TRN2", target_bir_lowering=False, num_devices=1)
    args = [nc.dram_tensor(k, v.shape, mybir.dt.from_np(v.dtype), kind="ExternalInput").ap() for k, v in arrays.items()]
    args.append(nc.dram_tensor("out", (P, N), mybir.dt.float32, kind="ExternalOutput").ap())
    program(nc, *args, stage=STAGE)
    got = run_bass_kernel_spmd(nc, [arrays], core_ids=[0]).results[0]["out"]
    if STAGE < 5:
        return got.T.reshape(B, S, D)
    return got.reshape(P, TILES, D).transpose(1, 0, 2).reshape(B, S, D)
```

```python
import numpy as np
import concourse.bass as bass
from concourse import mybir
from contextlib import ExitStack

B, S, D = 64, 32, 128
N = B * S
P = 128
TILES = N // P
CH = 4
CT = N // CH
TPC = CT // P
CB = CT // S
HEADS, HD = 16, 8
G, HG = 4, 4
WINDOW = 128
TR = 64
F = 384
FT = F // P
QB = 32
NSUB, NCAT = 8, 32
E = 6
NEG = 1e30
MAGIC = 12582912.0
QMAX = 32767.0

CONST = [("ident", P), ("alibi", HG * S), ("causal", S), ("pre", S), ("post", S), ("cloze", S),
         ("empty", 1), ("hmask", HG), ("gmask", G), ("index", 1), ("tri", E * E), ("ones", P), ("magic", 1), ("minus_magic", 1)]
COND = [("W1", 32), ("b1", 1), ("vrep", P), ("blend", 2 * TR), ("tau_raws", 1), ("tau_ctx", 1)]
ATTN = [("wq", P), ("wk", P), ("wv", P), ("wo", P), ("bv", P), ("bq", 1), ("bk", 1), ("bo", 1)]
CTX = [("Wg0", P), ("Wg1", P), ("Wsoma", P), ("Wtemp", P), ("Wout", P), ("Wn1", 32), ("Wn2", P),
       ("bg", 1), ("bn1", 1), ("bn2", 1), ("bsoma", 1), ("btemp", 1), ("gamma", 1), ("beta", 1)]
FFN = [("up", FT * P), ("gate", FT * P), ("down", FT * P)]
SEL = [("bias1", P)]
MOE = [("Wup", E * P), ("Wgt", E * P), ("Wdn", E * P), ("Sup", 2 * P), ("Sgt", P), ("Sdn", P),
       ("bdn", P), ("norm", 2 * P), ("rW", 2 * E), ("rb", 2 * E), ("gb", 2 * E),
       ("bup", E), ("bgt", E), ("sbup", 2), ("sbgt", 1)]
INTS = [("prompt", TILES), ("subject", B), ("category", B)]


def width(fields):
    return sum(w for _, w in fields)


def lags():
    out = []
    for lag in range(S):
        valid = S - lag
        even = valid + valid % 2
        nb = min(B, CT // S * (S // (1 << (even - 1).bit_length())))
        for b in range(0, B, nb):
            out.append((lag, b, nb, even, valid))
    return out


def program(nc, consts, cond, attn0, ctx_w, ffn_w, attn1, sel_w, moe_w, ints, x_fm, x_tm, w_subject, w_category,
            out):
    f32, f32r, i32 = mybir.dt.float32, mybir.dt.float32r, mybir.dt.int32
    ALU, ACT, AX = mybir.AluOpType, mybir.ActivationFunctionType, mybir.AxisListType
    es = ExitStack()
    with es:
        def sb(name, cols, dt=f32):
            return es.enter_context(nc.sbuf_tensor(name, [P, cols], dt))

        def sem(name):
            return es.enter_context(nc.semaphore(name))

        def fields(t, spec):
            at, found = 0, {}
            for name, w in spec:
                found[name] = t[:, at:at + w]
                at += w
            return found

        def over(ap, axis, n):
            ap = ap.unsqueeze(axis)
            shape = list(ap.shape)
            shape[axis] = n
            return ap.broadcast_to(shape)

        t_const, t_cond = sb("t_const", width(CONST)), sb("t_cond", width(COND))
        t_attn = [sb("t_attn0", width(ATTN)), sb("t_attn1", width(ATTN))]
        t_ctx, t_ffn, t_sel = sb("t_ctx", width(CTX)), sb("t_ffn", width(FFN)), sb("t_sel", width(SEL))
        t_moe, t_int = sb("t_moe", width(MOE)), sb("t_int", width(INTS), i32)
        K, C0, W2 = fields(t_const, CONST), fields(t_cond, COND), fields(t_ctx, CTX)
        AW = [fields(t, ATTN) for t in t_attn]
        SW, MW, IN = fields(t_sel, SEL), fields(t_moe, MOE), fields(t_int, INTS)
        X = sb("X", N)
        H = sb("H", N)
        chosen = sb("chosen", B * P)
        x_tok = chosen[:, S * P:S * P + N]
        powers = sb("powers", S * P, f32r)
        mod_high, mod_low = sb("mod_high", N, f32r), sb("mod_low", N, f32r)
        wT = sb("wT", 3 * FT * P)
        small = sb("small", 1280)
        ARENA = 21504
        arena = sb("arena", ARENA)
        PS = es.enter_context(nc.psum_tensor("PS", [P, 8 * CT], f32))

        def bank(i, n=1):
            return PS[:, i * CT:(i + n) * CT]

        def chunk(t, c):
            return t[:, c * CT:(c + 1) * CT]

        small_at, arena_at = [0], [0]

        def cols(n):
            small_at[0] += n
            assert small_at[0] <= 1280
            return small[:, small_at[0] - n:small_at[0]]

        def region(n):
            arena_at[0] += n
            assert arena_at[0] <= ARENA, arena_at
            return arena[:, arena_at[0] - n:arena_at[0]]

        l_const, l_x, l_int, l_attn0, l_ctx, l_ffn, l_attn1, l_sel, l_moe = [
            sem("loaded_" + n) for n in ("const", "x", "int", "attn0", "ctx", "ffn", "attn1", "sel", "moe")]
        chosen1, chosen2 = sem("chosen1_loaded"), sem("chosen2_loaded")
        dve_step = sem("dve_step")
        stored = [sem("stored_even"), sem("stored_odd")]

        vector_steps = [0]

        def note(ins):
            vector_steps[0] += 1
            ins.then_inc(dve_step, 1)

        def join():
            nc.vector.wait_ge(dve_step, vector_steps[0])

        def link(ins):
            note(ins)
            join()

        def mk(stage_name, *what):
            return {w: sem(stage_name + "_" + w) for w in what}

        a = mk("pool", "tanh_ps", "tanh", "score_ps", "masked", "exped", "mats", "zeroed", "ps", "h", "blend_max", "blend_exp",
               "power", "power0", "powers", "split")
        at = [mk(f"attn{i}", "zeroed", "qk_ps", "v_ps", "qk", "v_act", "v_dve", "s_ps", "biased", "maxed",
                 "shifted", "exped", "recip", "normed", "probT", "o_ps", "o", "y_ps", "y", "scales", "emd") for i in range(2)]
        c2 = mk("ctx", "ones", "h1_ps", "h1", "soma_ps", "soma", "scanned", "wg_ps", "wg", "gated", "mod_ps",
                "mod", "mod_split", "zeroed", "lag_ps", "prod", "added", "temporal", "gate_ps", "gate", "somagate", "out_ps",
                "xc", "sq", "var", "std", "y", "y_ps", "yt", "bT_ps")
        ff = mk("ffn", "w", "wT_ps", "wT", "amax", "amaxT_ps", "gmax", "gmaxb_ps", "scale", "hq", "up_ps", "copied",
                "magic", "uq", "gq", "sig", "uint", "o", "down_ps", "x")
        l1 = mk("sub", "hot", "ps", "tok", "tr_ps", "h")
        l2 = mk("cat", "hot", "ps", "tok", "tr_ps", "h")
        mo = mk("moe", "fuse_ps", "fuse_act", "fused", "logit_ps", "logit", "masked", "exped", "w", "wT_ps", "wT", "split",
                "xhigh", "xsplit", "up_ps", "gt_ps", "s", "hh", "dn_ps", "eo", "acc_ps", "y", "sq", "ss", "rstd",
                "normed", "tr_ps", "xf", "fin", "half")

        block = es.enter_context(nc.Block())

        arena_at[0] = 0
        TH = region(N)
        MASK, NEGM, SC, EX = region(CT), region(CT), region(CT), region(CT)
        TMPM = region(CT)
        MATS = region(N)
        POW = chosen[:, 0:S * P]
        pt = cols(TILES); e0 = cols(TILES); e1 = cols(TILES); e2 = cols(TILES)
        pcnt, pmax, psum_ = cols(TILES), cols(TILES), cols(TILES)
        alpha = cols(1); alpha_t = cols(1); alpha_c = cols(1); alpha_ct = cols(1)
        bmax = cols(1); bsum = cols(1)
        arena_at[0] = 0
        PARTS, PT, PB = 2 * CH, CT // 2, CB // 2
        Q2, K2, T2 = ([region(PB * P) for _ in range(2)] for _ in range(3))
        S3 = [region(PB * P) for _ in range(3)]
        V_ALL = region(3 * CB * P)
        V3 = [V_ALL[:, n * CB * P:(n + 1) * CB * P] for n in range(3)]
        OT = [region(PT) for _ in range(2)]
        qscale, qbias, kbias = cols(G), cols(G), cols(HG)
        NR = PB * HG
        smax, ssum, semt = ([cols(NR) for _ in range(3)] for _ in range(3))

        def qv(t):
            return t.rearrange("p (b g s) -> p b g s", b=PB, g=G)

        def mix_bank(j):
            return bank(7 if j < PARTS - 2 else j % 2)

        def score_bank(j, n):
            return bank(3 + 2 * (j % 2) + n)

        def score_rows(j):
            return S3[j % 3].rearrange("p (r s) -> p r s", s=S)

        def pooling_pe(pe):
            pe.wait_ge(a["blend_exp"], 1)
            pe.transpose(bank(4)[:, 0:P], C0["blend"], K["ident"]).then_inc(c2["bT_ps"], 1)
            pe.wait_ge(l_x, 32)
            for c in range(CH):
                pe.matmul(bank(c)[0:32, :], C0["W1"], chunk(X, c), start=True, stop=True).then_inc(a["tanh_ps"], 1)
            pe.wait_ge(a["power0"], 1)
            for c in range(CH):
                pe.wait_ge(a["tanh"], c + 1)
                pe.matmul(bank(4 + c), C0["vrep"][0:32, :], TH[0:32, c * CT:(c + 1) * CT], start=True, stop=True)\
                    .then_inc(a["score_ps"], 1)
            pe.wait_ge(a["mats"], 4)
            for t in range(TILES):
                ins = pe.matmul(PS[:, 4 * CT + t * P:4 * CT + (t + 1) * P], x_tok[:, t * P:(t + 1) * P],
                                MATS[:, t * P:(t + 1) * P], start=True, stop=True)
                if t % TPC == TPC - 1:
                    ins.then_inc(a["ps"], 1)

        def pooling_act(act):
            act.wait_ge(l_const, 32)
            act.activation(alpha_t, C0["tau_raws"], ACT.Exp).then_inc(a["power"], 1)
            act.activation(alpha_ct, C0["tau_ctx"], ACT.Exp).then_inc(a["power"], 1)
            act.wait_ge(a["blend_max"], 1)
            act.activation(C0["blend"], C0["blend"], ACT.Exp).then_inc(a["exped"], 1)
            for c in range(CH):
                act.wait_ge(a["tanh_ps"], c + 1)
                act.activation(TH[0:32, c * CT:(c + 1) * CT], bank(c)[0:32, :], ACT.Tanh, bias=C0["b1"][0:32, :])\
                    .then_inc(a["tanh"], 1)
            act.wait_ge(a["masked"], 1)
            act.activation(EX, SC, ACT.Exp).then_inc(a["exped"], 1)
            for c in range(CH):
                act.wait_ge(a["ps"], c + 1)
                act.activation(chunk(H, c), bank(4 + c), ACT.Copy).then_inc(a["h"], 1)

        def pooling_pool(pool):
            pool.memset(MATS, 0.0).then_inc(a["zeroed"], 1)
            pool.memset(V_ALL, 0.0).then_inc(at[0]["zeroed"], 1)
            pool.wait_ge(a["power0"], 1)
            for lag in range(1, S):
                pool.tensor_scalar(POW[:, lag * P:(lag + 1) * P], POW[:, (lag - 1) * P:lag * P], alpha, None, ALU.mult)\
                    .then_inc(a["powers"], 1)
                pool.wait_ge(a["powers"], lag)

        def pooling_dve(dve):
            dve.wait_ge(l_const, 32)
            link(dve.tensor_reduce(bmax, C0["blend"][:, 0:TR], AX.X, ALU.max))
            dve.tensor_scalar(C0["blend"], C0["blend"], bmax, None, ALU.subtract).then_inc(a["blend_max"], 1)
            dve.wait_ge(a["power"], 2)
            link(dve.tensor_scalar(alpha_t, alpha_t, 1.0, None, ALU.add))
            link(dve.reciprocal(alpha, alpha_t))
            link(dve.tensor_scalar(alpha_ct, alpha_ct, 1.0, None, ALU.add))
            link(dve.reciprocal(alpha_c, alpha_ct))
            dve.wait_ge(a["exped"], 1)
            link(dve.tensor_reduce(bsum, C0["blend"][:, 0:TR], AX.X, ALU.add))
            link(dve.reciprocal(bsum, bsum))
            dve.tensor_scalar(C0["blend"], C0["blend"], bsum, None, ALU.mult).then_inc(a["blend_exp"], 1)
            dve.wait_ge(l_int, 16)
            link(dve.tensor_copy(pt, IN["prompt"]))
            note(dve.tensor_scalar(e0, pt, 0.0, None, ALU.is_equal))
            link(dve.tensor_scalar(e1, pt, 1.0, None, ALU.is_equal))
            link(dve.tensor_tensor(e2, e0, e1, ALU.add))
            link(dve.tensor_scalar(e2, e2, -1.0, 1.0, ALU.mult, ALU.add))
            dve.wait_ge(c2["bT_ps"], 1)
            dve.tensor_copy(POW[:, 0:P], bank(4)[:, 0:P]).then_inc(a["power0"], 1)
            m3 = MASK.rearrange("p (t s) -> p t s", t=TILES)
            tmp3 = TMPM.rearrange("p (t s) -> p t s", t=TILES)
            link(dve.tensor_tensor(m3, over(K["pre"], 1, TILES), over(e0, 2, S), ALU.mult))
            link(dve.tensor_tensor(tmp3, over(K["post"], 1, TILES), over(e1, 2, S), ALU.mult))
            link(dve.tensor_tensor(MASK, MASK, TMPM, ALU.add))
            link(dve.tensor_tensor(tmp3, over(K["cloze"], 1, TILES), over(e2, 2, S), ALU.mult))
            link(dve.tensor_tensor(MASK, MASK, TMPM, ALU.add))
            link(dve.tensor_reduce(pcnt, m3, AX.X, ALU.add))
            link(dve.tensor_scalar(NEGM, MASK, 1.0, NEG, ALU.subtract, ALU.mult))
            dve.wait_ge(a["score_ps"], CH)
            sc3 = SC.rearrange("p (t s) -> p t s", t=TILES)
            ps3 = bank(4, 4).rearrange("p (t q s) -> p t q s", t=TILES, q=4)
            for q in range(4):
                r = slice(32 * q, 32 * q + 32)
                note(dve.tensor_tensor(sc3[r], ps3[r, :, q, :], m3[r], ALU.mult))
            join()
            link(dve.tensor_tensor(SC, SC, NEGM, ALU.add))
            link(dve.tensor_reduce(pmax, sc3, AX.X, ALU.max))
            dve.tensor_tensor(sc3, sc3, over(pmax, 2, S), ALU.subtract).then_inc(a["masked"], 1)
            dve.wait_ge(a["exped"], 2)
            ex3 = EX.rearrange("p (t s) -> p t s", t=TILES)
            link(dve.tensor_reduce(psum_, ex3, AX.X, ALU.add))
            link(dve.tensor_tensor(psum_, psum_, pcnt, ALU.mult))
            link(dve.reciprocal(psum_, psum_))
            link(dve.tensor_tensor(ex3, ex3, over(psum_, 2, S), ALU.mult))
            dve.wait_ge(a["zeroed"], 1)
            mats = MATS.rearrange("p (t q s) -> p t q s", t=TILES, q=4)
            for q in range(4):
                r = slice(32 * q, 32 * q + 32)
                dve.transpose(mats[r, :, q, :], ex3[r]).then_inc(a["mats"], 1)

        def ffn_weights_dve(dve):
            dve.wait_ge(l_ffn, 16)
            wb = t_ffn[:, :].rearrange("p (n b) -> p n b", b=QB)
            link(dve.tensor_reduce(wscale, wb, AX.X, ALU.max, apply_absolute_value=True))
            link(dve.tensor_scalar(wscale, wscale, 1.0 / 7.0, 1e-12, ALU.mult, ALU.max))
            link(dve.reciprocal(winv, wscale))
            link(dve.tensor_tensor(wb, wb, over(winv, 2, QB), ALU.mult))
            link(dve.tensor_scalar(t_ffn[:, :], t_ffn[:, :], MAGIC, MAGIC + 7.0, ALU.add, ALU.min))
            link(dve.tensor_scalar(t_ffn[:, :], t_ffn[:, :], MAGIC - 8.0, MAGIC, ALU.max, ALU.subtract))
            dve.tensor_tensor(wb, wb, over(wscale, 2, QB), ALU.mult).then_inc(ff["w"], 1)
        def attention_pe(pe, i, src_ready):
            s, w = at[i], AW[i]
            pe.wait_ge((l_attn0, l_attn1)[i], 16)

            def project(j):
                if j >= 2:
                    pe.wait_ge(s["qk"], j - 1)
                src_ready(pe, j)
                src = H[:, j * PT:(j + 1) * PT]
                pe.matmul(bank(j % 2)[:, 0:PT], w["wq"], src, start=True, stop=True)
                pe.matmul(bank(j % 2)[:, PT:2 * PT], w["wk"], src, start=True, stop=True).then_inc(s["qk_ps"], 1)

            def values(c):
                if c:
                    pe.wait_ge(s["v_act"], c)
                    pe.wait_ge(s["v_dve"], c)
                pe.matmul(bank(2), K["ones"][0:1, :], over(w["bv"][0:1, :], 1, TPC), start=True, stop=False)
                for t in range(TPC):
                    ins = pe.matmul(bank(2)[:, t * P:(t + 1) * P], H[:, c * CT + t * P:c * CT + (t + 1) * P], w["wv"],
                                    start=False, stop=t == TPC - 1)
                ins.then_inc(s["v_ps"], 1)

            def scores(j):
                pe.wait_ge(s["qk"], j + 1)
                for b in range(PB):
                    if b % 4 == 0 and j >= 2:
                        pe.wait_ge(s["biased"], 2 * (j - 2) + b // 4 + 1)
                    r = slice(b * P, (b + 1) * P)
                    o = score_bank(j, b // 4)[:, (b % 4) * P:(b % 4 + 1) * P]
                    ins = pe.matmul(o, Q2[j % 2][:, r], K2[j % 2][:, r], start=True, stop=True)
                    if b % 4 == 3:
                        ins.then_inc(s["s_ps"], 1)

            def mix(j):
                c = j // 2
                pe.wait_ge(s["probT"], j + 1)
                pe.wait_ge(s["v_act"], c + 1)
                pe.wait_ge(s["v_dve"], c + 1)
                if 0 < j < PARTS - 2:
                    pe.wait_ge(s["y"], j)
                for b in range(PB):
                    for h in range(HG):
                        at_v = ((j % 2) * PB + b) * P + h * S
                        at_p = b * P + h * S
                        ins = pe.matmul(mix_bank(j)[32 * h:32 * h + 32, b * S:(b + 1) * S], V3[c % 3][:, at_v:at_v + S],
                                        T2[j % 2][:, at_p:at_p + S], start=True, stop=True, tile_position=(0, 32 * h))
                ins.then_inc(s["o_ps"], 1)

            def output(j):
                pe.wait_ge(s["o"], j + 1)
                pe.matmul(mix_bank(j)[:, PT:2 * PT], w["wo"], OT[j % 2], start=True, stop=True).then_inc(s["y_ps"], 1)

            project(0)
            values(0)
            project(1)
            scores(0)
            for j in range(PARTS + 3):
                if j + 2 < PARTS:
                    project(j + 2)
                if 3 <= j < PARTS:
                    output(j - 3)
                if j + 1 < PARTS:
                    scores(j + 1)
                if j == 0:
                    values(1)
                if 2 <= j <= PARTS + 1:
                    mix(j - 2)
                if j % 2 and j + 3 < PARTS:
                    values((j + 3) // 2)
                if j >= PARTS:
                    output(j - 3)

        def attention_act(act, i):
            s, w = at[i], AW[i]

            def expand(j):
                if j >= 2:
                    act.wait_ge(s["s_ps"], 2 * (j - 1))
                act.wait_ge(s["qk_ps"], j + 1)
                q = bank(j % 2)[:, 0:PT].rearrange("p (b s) -> p b s", b=PB)
                for g in range(G):
                    act.activation(qv(Q2[j % 2])[:, :, g, :], q, ACT.Identity, bias=qbias[:, g:g + 1],
                                   scale=qscale[:, g:g + 1])
                k = bank(j % 2)[:, PT:2 * PT].rearrange("p (b s) -> p b s", b=PB)
                for h in range(HG):
                    ins = act.activation(qv(K2[j % 2])[:, :, h, :], k, ACT.Identity, bias=kbias[:, h:h + 1],
                                         scale=K["hmask"][:, h:h + 1])
                ins.then_inc(s["qk"], 1)

            act.wait_ge(s["scales"], 1)
            expand(0)
            move_v(act, s, 0, 0, s["v_act"])
            expand(1)
            for j in range(PARTS + 2):
                if j < PARTS:
                    act.wait_ge(s["shifted"], j + 1)
                    act.activation(S3[j % 3], S3[j % 3], ACT.Exp).then_inc(s["exped"], 1)
                    if i == 0:
                        act.activation(semt[j % 3], smax[j % 3], ACT.Exp, scale=-1.0).then_inc(s["emd"], 1)
                if j + 2 < PARTS:
                    expand(j + 2)
                if j >= 2:
                    act.wait_ge(s["o_ps"], j - 1)
                    act.activation(OT[(j - 2) % 2], mix_bank(j - 2)[:, 0:PT], ACT.Copy).then_inc(s["o"], 1)
                if j + 2 < PARTS and j % 2 == 0:
                    move_v(act, s, j // 2 + 1, 0, s["v_act"])

        def move_v(eng, s, c, half, done):
            if c == 0:
                eng.wait_ge(s["zeroed"], 1)
            if c >= 3:
                eng.wait_ge(s["o_ps"], 2 * (c - 2))
            eng.wait_ge(s["v_ps"], c + 1)
            v = bank(2).rearrange("p (t g h d) -> p t g h d", t=TPC, g=G, h=HG)
            dst = V3[c % 3].rearrange("p (t q h g d) -> p t q h g d", t=TPC, q=4, h=HG, g=G)
            for q in range(2 * half, 2 * half + 2):
                for g in range(G):
                    o, n = dst[32 * g:32 * g + 32, :, q, :, g, :], v[32 * q:32 * q + 32, :, g, :, :]
                    ins = eng.activation(o, n, ACT.Copy) if half == 0 else eng.tensor_copy(o, n)
            ins.then_inc(done, 1)

        def attention_pool(pool, i):
            s = at[i]
            if i == 1:
                pool.wait_ge(l1["tok"], CH + 1)
                pool.memset(V_ALL, 0.0).then_inc(s["zeroed"], 1)
            for j in range(PARTS + 1):
                if j < PARTS:
                    rows = score_rows(j)
                    pool.wait_ge(s["maxed"], j + 1)
                    pool.tensor_tensor(rows, rows, over(smax[j % 3], 2, S), ALU.subtract).then_inc(s["shifted"], 1)
                if j:
                    rows = score_rows(j - 1)
                    pool.wait_ge(s["recip"], j)
                    pool.tensor_tensor(rows, rows, over(ssum[(j - 1) % 3], 2, S), ALU.mult).then_inc(s["normed"], 1)

        def attention_dve(dve, i):
            s, w = at[i], AW[i]
            dve.wait_ge((l_attn0, l_attn1)[i], 16)
            scale = 1.0 / float(np.sqrt(HD))
            note(dve.tensor_scalar(kbias, K["hmask"], w["bk"], None, ALU.mult))
            link(dve.tensor_scalar(qscale, K["gmask"], scale, None, ALU.mult))
            dve.tensor_scalar(qbias, qscale, w["bq"], None, ALU.mult).then_inc(s["scales"], 1)
            if i == 1:
                hot_dve(dve, l2, IN["category"])

            def scores(j):
                for n in range(2):
                    dve.wait_ge(s["s_ps"], 2 * j + n + 1)
                    o, p_ = S3[j % 3][:, n * CT:(n + 1) * CT], score_bank(j, n)
                    if i == 0:
                        o, p_ = (x.rearrange("p (r s) -> p r s", s=S) for x in (o, p_))
                        bias = over(K["causal"], 1, 4 * HG)
                    else:
                        o, p_ = (x.rearrange("p (b r) -> p b r", b=4) for x in (o, p_))
                        bias = over(K["alibi"], 1, 4)
                    dve.tensor_tensor(o, p_, bias, ALU.add).then_inc(s["biased"], 1)
                dve.wait_ge(s["biased"], 2 * j + 2)
                if i == 0:
                    link(dve.tensor_reduce(smax[j % 3], score_rows(j), AX.X, ALU.max))
                    dve.tensor_scalar(smax[j % 3], smax[j % 3], 0.0, None, ALU.max).then_inc(s["maxed"], 1)
                else:
                    dve.tensor_reduce(smax[j % 3], score_rows(j), AX.X, ALU.max).then_inc(s["maxed"], 1)

            def sums(j):
                dve.wait_ge(s["exped"], j + 1)
                link(dve.tensor_reduce(ssum[j % 3], score_rows(j), AX.X, ALU.add))
                if i == 0:
                    dve.wait_ge(s["emd"], j + 1)
                    link(dve.scalar_tensor_tensor(ssum[j % 3], semt[j % 3], K["empty"], ssum[j % 3], ALU.mult, ALU.add))
                dve.reciprocal(ssum[j % 3], ssum[j % 3]).then_inc(s["recip"], 1)

            def transpose(j):
                dve.wait_ge(s["normed"], j + 1)
                if j >= 2:
                    dve.wait_ge(s["o_ps"], j - 1)
                dve.transpose(T2[j % 2], S3[j % 3]).then_inc(s["probT"], 1)

            def residual(j):
                dve.wait_ge(s["y_ps"], j + 1)
                x = X[:, j * PT:(j + 1) * PT]
                dve.scalar_tensor_tensor(x, mix_bank(j)[:, PT:2 * PT], w["bo"], x, ALU.add, ALU.add).then_inc(s["y"], 1)

            move_v(dve, s, 0, 1, s["v_dve"])
            for j in range(PARTS + 3):
                if j < PARTS:
                    if j >= 3:
                        dve.wait_ge(s["probT"], j - 2)
                    scores(j)
                if 1 <= j <= PARTS:
                    sums(j - 1)
                if 2 <= j <= PARTS + 1:
                    transpose(j - 2)
                if 3 <= j < PARTS:
                    residual(j - 3)
                if j == PARTS + 1:
                    residual(PARTS - 3)
                if j > PARTS:
                    residual(j - 3)
                if j % 2 == 0 and j + 2 < PARTS:
                    move_v(dve, s, j // 2 + 1, 1, s["v_dve"])

        arena_at[0] = 0
        COEF, CTXT, WG, MOD, H1, SOMA, GATED, TPOOL, TDVE = (region(N) for _ in range(9))
        PP, PD = [region(CT) for _ in range(4)], [region(CT) for _ in range(2)]
        XC, SQ, YL, GATE, SOMAG = COEF, CTXT, GATED, WG, MOD
        nmean, nvar, nstd = cols(TILES), cols(TILES), cols(TILES)
        LAGS = lags()
        ON_DVE = [u % 3 == 2 or (u > len(LAGS) - 12 and u % 3 == 1) for u in range(len(LAGS))]

        def ctx_pe(pe):
            pe.wait_ge(l_ctx, 16)
            pe.wait_ge(at[0]["y"], PARTS)
            for c in range(CH):
                pe.matmul(bank(c)[0:32, :], W2["Wn1"], chunk(X, c), start=True, stop=True).then_inc(c2["h1_ps"], 1)
            for c in range(CH):
                pe.wait_ge(c2["h1"], c + 1)
                pe.matmul(bank(4 + c), W2["Wn2"][0:32, :], H1[0:32, c * CT:(c + 1) * CT], start=True, stop=True)\
                    .then_inc(c2["mod_ps"], 1)
            for c in range(CH):
                pe.wait_ge(c2["h1"], c + 1)
                pe.matmul(bank(c), W2["Wg0"], chunk(X, c), start=True, stop=False)
                pe.wait_ge(c2["scanned"], 1)
                pe.matmul(bank(c), W2["Wg1"], chunk(CTXT, c), start=False, stop=True).then_inc(c2["wg_ps"], 1)
            pe.wait_ge(c2["mod_split"], CH)
            pe.wait_ge(c2["wg"], CH)
            pe.wait_ge(a["split"], 1)
            for u, (lag, b0, nb, even, valid) in enumerate(LAGS):
                if u % 8 == 7 and CH <= u // 8 < CH + 3:
                    n = u // 8 - CH
                    if n:
                        pe.wait_ge(ff["wT"], n)
                    else:
                        pe.wait_ge(c2["soma"], CH)
                        pe.wait_ge(ff["w"], 1)
                    for k in range(FT):
                        ins = pe.transpose(bank(7)[:, k * P:(k + 1) * P], piece(t_ffn, n * FT + k), K["ident"])
                    ins.then_inc(ff["wT_ps"], 1)
                if u % 8 == 7 and u // 8 < CH:
                    c = u // 8
                    if c:
                        pe.wait_ge(c2["soma"], c)
                    pe.matmul(bank(7), W2["Wsoma"], chunk(X, c), start=True, stop=True).then_inc(c2["soma_ps"], 1)
                if u >= 7:
                    pe.wait_ge(c2["prod"], u - 6)
                w = powers[:, lag * P:(lag + 1) * P]
                o = bank(u % 7)[:, 0:nb * even]
                for part in (mod_high, mod_low):
                    r = part[:, :].rearrange("p (b s) -> p b s", b=B)[:, b0:b0 + nb, 0:even]
                    ins = pe.matmul(o, w, r, start=part is mod_high, stop=part is mod_low)
                ins.then_inc(c2["lag_ps"], 1)
            for c in range(CH):
                pe.wait_ge(c2["temporal"], c + 1)
                pe.matmul(bank(c), W2["Wtemp"], chunk(TPOOL, c), start=True, stop=True).then_inc(c2["gate_ps"], 1)
            for t in range(TILES):
                if t % TPC == 0:
                    pe.wait_ge(c2["somagate"], t // TPC + 1)
                ins = pe.matmul(PS[:, 4 * CT + t * P:4 * CT + (t + 1) * P], SOMAG[:, t * P:(t + 1) * P], W2["Wout"],
                                start=True, stop=True)
                if t % TPC == TPC - 1:
                    ins.then_inc(c2["out_ps"], 1)
            pe.wait_ge(c2["gate"], CH)
            for t in range(TILES):
                pe.wait_ge(c2["y"], t // TPC + 1)
                ins = pe.transpose(PS[:, t * P:(t + 1) * P], YL[:, t * P:(t + 1) * P], K["ident"])
                if t % TPC == TPC - 1:
                    ins.then_inc(c2["y_ps"], 1)

        def ctx_act(act):
            act.wait_ge(a["powers"], S - 1)
            act.activation(powers[:, :], POW, ACT.Copy).then_inc(a["tanh"], 1)
            for c in range(CH):
                act.wait_ge(c2["h1_ps"], c + 1)
                act.activation(H1[0:32, c * CT:(c + 1) * CT], bank(c)[0:32, :], ACT.Gelu, bias=W2["bn1"][0:32, :])\
                    .then_inc(c2["h1"], 1)
            for c in range(CH):
                act.wait_ge(c2["mod_ps"], c + 1)
                act.activation(chunk(MOD, c), bank(4 + c), ACT.Sigmoid, bias=W2["bn2"]).then_inc(c2["mod"], 1)
            for c in range(CH):
                act.wait_ge(c2["wg_ps"], c + 1)
                act.activation(chunk(WG, c), bank(c), ACT.Sigmoid, bias=W2["bg"]).then_inc(c2["wg"], 1)
            for c in range(CH):
                act.wait_ge(c2["soma_ps"], c + 1)
                act.activation(chunk(SOMA, c), bank(7), ACT.Gelu, bias=W2["bsoma"]).then_inc(c2["soma"], 1)
            for n in range(3):
                act.wait_ge(ff["wT_ps"], n + 1)
                act.activation(wT[:, n * FT * P:(n + 1) * FT * P], bank(7)[:, 0:FT * P], ACT.Copy).then_inc(ff["wT"], 1)
            act.wait_ge(c2["gated"], 1)
            for c in range(CH):
                act.wait_ge(c2["gate_ps"], c + 1)
                act.activation(chunk(GATE, c), bank(c), ACT.Sigmoid, bias=W2["btemp"]).then_inc(c2["gate"], 1)
            for c in range(CH + 1):
                if c < CH:
                    act.wait_ge(c2["xc"], c + 1)
                    act.activation(chunk(SQ, c), chunk(XC, c), ACT.Square).then_inc(c2["sq"], 1)
                if c:
                    r = slice((c - 1) * TPC, c * TPC)
                    act.wait_ge(c2["var"], c)
                    act.activation(nstd[:, r], nvar[:, r], ACT.Sqrt).then_inc(c2["std"], 1)
            for c in range(CH):
                act.wait_ge(c2["y_ps"], c + 1)
                act.activation(chunk(H, c), bank(c), ACT.Identity, bias=W2["beta"], scale=W2["gamma"]).then_inc(c2["yt"], 1)

        def ctx_pool(pool):
            pool.wait_ge(at[0]["y"], PARTS)
            first = COEF.rearrange("p (b s) -> p b s", s=S)
            pool.memset(first[:, :, 1:S], 1.0).then_inc(c2["ones"], 1)
            pool.memset(first[:, :, 0:1], 0.0).then_inc(c2["ones"], 1)
            pool.memset(TPOOL, 0.0).then_inc(c2["zeroed"], 1)
            pool.memset(TDVE, 0.0).then_inc(c2["zeroed"], 1)
            pool.wait_ge(a["tanh"], CH + 1)
            pool.wait_ge(c2["zeroed"], 2)
            pool.tensor_tensor(powers[TR:P, :], POW[TR:P], powers[TR:P, :].bitcast(f32), ALU.subtract).then_inc(a["split"], 1)
            pool.wait_ge(a["split"], 1)
            t3 = TPOOL.rearrange("p (b s) -> p b s", s=S)
            k, writer = 0, {}
            for u, (lag, b0, nb, even, valid) in enumerate(LAGS):
                if ON_DVE[u]:
                    continue
                pool.wait_ge(c2["prod"], u + 1)
                last = max(writer.get(b, 0) for b in range(b0, b0 + nb, CB))
                if last:
                    pool.wait_ge(c2["added"], last)
                o = t3[:, b0:b0 + nb, lag:S]
                pool.tensor_tensor(o, o, PP[k % 4][:, 0:nb * valid].rearrange("p (b s) -> p b s", b=nb), ALU.add)\
                    .then_inc(c2["added"], 1)
                k += 1
                for b in range(b0, b0 + nb, CB):
                    writer[b] = k

        def ctx_dve(dve):
            dve.wait_ge(c2["ones"], 2)
            link(dve.tensor_scalar(COEF, COEF, alpha_c, None, ALU.mult))
            dve.tensor_tensor_scan(CTXT, COEF, X[:, :], 0.0, ALU.mult, ALU.add).then_inc(c2["scanned"], 1)
            for c in range(CH):
                dve.wait_ge(c2["mod"], c + 1)
                link(dve.tensor_scalar(chunk(mod_high, c), chunk(MOD, c), 0.5, None, ALU.add))
                dve.scalar_tensor_tensor(chunk(mod_low, c), chunk(MOD, c), 0.5, chunk(mod_high, c).bitcast(f32), ALU.add,
                                         ALU.subtract).then_inc(c2["mod_split"], 1)
            for c in range(CH):
                dve.wait_ge(c2["wg"], c + 1)
                ins = dve.tensor_tensor(chunk(GATED, c), chunk(X, c), chunk(WG, c), ALU.mult)
            ins.then_inc(c2["gated"], 1)
            dve.wait_ge(c2["gated"], 1)
            dve.wait_ge(c2["zeroed"], 2)
            g3 = GATED.rearrange("p (b s) -> p b s", s=S)
            t3 = TDVE.rearrange("p (b s) -> p b s", s=S)
            k = d = 0
            waiting = None
            for u, (lag, b0, nb, even, valid) in enumerate(LAGS):
                dve.wait_ge(c2["lag_ps"], u + 1)
                if ON_DVE[u]:
                    join()
                    to = PD[d % 2]
                    d += 1
                else:
                    if k >= 4:
                        dve.wait_ge(c2["added"], k - 3)
                    to = PP[k % 4]
                    k += 1
                prod = to[:, 0:nb * valid].rearrange("p (b s) -> p b s", b=nb)
                m = bank(u % 7)[:, 0:nb * even].rearrange("p (b s) -> p b s", b=nb)[:, :, 0:valid]
                dve.tensor_tensor(prod, m, g3[:, b0:b0 + nb, 0:valid], ALU.mult).then_inc(c2["prod"], 1)
                if waiting is not None:
                    w, o, p_ = waiting
                    dve.wait_ge(c2["prod"], w + 1)
                    join()
                    note(dve.tensor_tensor(o, o, p_, ALU.add))
                waiting = (u, t3[:, b0:b0 + nb, lag:S], prod) if ON_DVE[u] else None
            if waiting is not None:
                w, o, p_ = waiting
                dve.wait_ge(c2["prod"], w + 1)
                join()
                note(dve.tensor_tensor(o, o, p_, ALU.add))
            join()
            dve.wait_ge(c2["added"], k)
            for c in range(CH):
                dve.tensor_tensor(chunk(TPOOL, c), chunk(TPOOL, c), chunk(TDVE, c), ALU.add).then_inc(c2["temporal"], 1)
            for c in range(CH):
                dve.wait_ge(c2["soma"], c + 1)
                dve.wait_ge(c2["gate"], c + 1)
                dve.tensor_tensor(chunk(SOMAG, c), chunk(SOMA, c), chunk(GATE, c), ALU.mult).then_inc(c2["somagate"], 1)

            def tiles(t, c):
                return chunk(t, c).rearrange("p (t d) -> p t d", t=TPC)

            def centre(c):
                m = nmean[:, c * TPC:(c + 1) * TPC]
                dve.wait_ge(c2["out_ps"], c + 1)
                o3 = bank(4 + c).rearrange("p (t d) -> p t d", t=TPC)
                link(dve.tensor_reduce(m, o3, AX.X, ALU.add))
                link(dve.tensor_scalar(m, m, -1.0 / D, None, ALU.mult))
                dve.tensor_tensor(tiles(XC, c), o3, over(m, 2, D), ALU.add).then_inc(c2["xc"], 1)

            def variance(c):
                v = nvar[:, c * TPC:(c + 1) * TPC]
                dve.wait_ge(c2["sq"], c + 1)
                link(dve.tensor_reduce(v, tiles(SQ, c), AX.X, ALU.add))
                dve.tensor_scalar(v, v, 1.0 / D, 1e-5, ALU.mult, ALU.add).then_inc(c2["var"], 1)

            def divide(c):
                d = nstd[:, c * TPC:(c + 1) * TPC]
                dve.wait_ge(c2["std"], c + 1)
                link(dve.reciprocal(d, d))
                dve.wait_ge(c2["xc"], c + 1)
                dve.tensor_tensor(tiles(YL, c), tiles(XC, c), over(d, 2, D), ALU.mult).then_inc(c2["y"], 1)

            for c in range(CH + 2):
                if c < CH:
                    centre(c)
                if 1 <= c <= CH:
                    variance(c - 1)
                if c >= 2:
                    divide(c - 2)

        arena_at[0] = 0
        U, GT, SG = (region(FT * N) for _ in range(3))
        unit_of = cols(5)
        wscale, winv = cols(3 * FT * P // QB), cols(3 * FT * P // QB)
        amx, amc, gsc = cols(2 * FT * CH), cols(4 + 1), cols(10)
        UNITS = [(f, c) for f in range(FT) for c in range(CH)]

        def span(t, f, c=None):
            return t[:, f * N:(f + 1) * N] if c is None else t[:, f * N + c * CT:f * N + (c + 1) * CT]


        def global_max_pe(pe, n):
            pe.wait_ge(ff["amax"], n + 1)
            pe.transpose(bank(7)[0:1, 0:P], amc[:, n:n + 1], K["ident"]).then_inc(ff["amaxT_ps"], 1)
            pe.wait_ge(ff["gmax"], n + 1)
            pe.matmul(bank(7)[:, P:P + 2], K["ones"][0:1, :], over(gsc[0:1, 2 * n:2 * n + 1], 1, 2), start=True, stop=True)\
                .then_inc(ff["gmaxb_ps"], 1)

        def global_max_dve(dve, n, part, one=None):
            dve.tensor_reduce(amc[:, n:n + 1], part, AX.X, ALU.max).then_inc(ff["amax"], 1)
            dve.wait_ge(ff["amaxT_ps"], n + 1)
            dve.tensor_reduce(gsc[0:1, 2 * n:2 * n + 1], bank(7)[0:1, 0:P], AX.X, ALU.max).then_inc(ff["gmax"], 1)
            dve.wait_ge(ff["gmaxb_ps"], n + 1)
            if one is None:
                link(dve.tensor_scalar(scale(n), bank(7)[:, P:P + 1], 1.0 / QMAX, 1e-12, ALU.mult, ALU.max))
                dve.reciprocal(inverse(n), scale(n)).then_inc(ff["scale"], 1)
            else:
                link(dve.tensor_scalar(scale(n), bank(7)[:, P:P + 1], 1.0 / QMAX, one, ALU.mult, ALU.mult))
                link(dve.tensor_scalar(scale(n), scale(n), 1e-12, None, ALU.max))
                link(dve.reciprocal(inverse(n), scale(n)))
                dve.tensor_scalar(inverse(n), inverse(n), one, None, ALU.mult).then_inc(ff["scale"], 1)
            dve.wait_ge(ff["scale"], n + 1)

        def scale(n):
            return gsc[:, 2 * n:2 * n + 1]

        def inverse(n):
            return gsc[:, 2 * n + 1:2 * n + 2]

        def ffn_pe(pe):
            pe.wait_ge(ff["wT"], 3)
            global_max_pe(pe, 0)
            for v in range(2 * len(UNITS)):
                f, c = UNITS[v % len(UNITS)]
                if v >= 6:
                    pe.wait_ge(ff["copied"], v - 5)
                k = (0 if v < len(UNITS) else FT) + f
                pe.wait_ge(ff["hq"], c + 1)
                pe.matmul(bank(v % 6), wT[:, k * P:(k + 1) * P], chunk(H, c), start=True, stop=True).then_inc(ff["up_ps"], 1)
            fuse_transposes_pe(pe)
            global_max_pe(pe, 1)
            global_max_pe(pe, 2)
            fuse_products_pe(pe)
            global_max_pe(pe, 3)
            global_max_pe(pe, 4)
            for f in range(FT):
                pe.wait_ge(ff["o"], f + 1)
                for c in range(CH):
                    if f == 0:
                        pe.wait_ge(mo["fuse_act"], 2)
                    ins = pe.matmul(bank(c), wT[:, (2 * FT + f) * P:(2 * FT + f + 1) * P], span(U, f, c),
                                    start=f == 0, stop=f == FT - 1)
                    if f == FT - 1:
                        ins.then_inc(ff["down_ps"], 1)

        def ffn_act(act):
            act.wait_ge(ff["hq"], 1)
            for v in range(2 * len(UNITS)):
                f, c = UNITS[v % len(UNITS)]
                act.wait_ge(ff["up_ps"], v + 1)
                act.activation(span(U if v < len(UNITS) else GT, f, c), bank(v % 6), ACT.Copy).then_inc(ff["copied"], 1)

            def to_integers(t, f, n):
                act.activation(span(t, f), span(t, f), ACT.Identity, bias=K["magic"], scale=inverse(n))\
                    .then_inc(ff["magic"], 1)

            fuse_transposed_act(act)
            act.wait_ge(ff["scale"], 2)
            act.wait_ge(ff["copied"], 2 * len(UNITS))
            for f in range(FT):
                to_integers(GT, f, 1)
            for f in range(FT):
                act.wait_ge(ff["gq"], f + 1)
                act.activation(span(SG, f), span(GT, f), ACT.Sigmoid).then_inc(ff["sig"], 1)
                act.wait_ge(ff["sig"], 2 * f + 1)
                act.activation(span(SG, f), span(SG, f), ACT.Identity, bias=K["magic"], scale=65536.0)\
                    .then_inc(ff["sig"], 1)
            act.wait_ge(ff["scale"], 3)
            for f in range(FT):
                to_integers(U, f, 2)
            fuse_act(act)
            for f in range(FT):
                act.wait_ge(ff["scale"], 4)
                to_integers(GT, f, 3)
                act.wait_ge(ff["uq"], f + 1)
                act.activation(span(U, f), span(U, f), ACT.Identity, bias=K["minus_magic"]).then_inc(ff["uint"], 1)
            act.wait_ge(ff["scale"], 5)
            for f in range(FT):
                to_integers(U, f, 4)

        def ffn_dve(dve):
            for c in range(CH):
                dve.wait_ge(c2["yt"], c + 1)
                link(dve.tensor_reduce(amx[:, c:c + 1], chunk(H, c), AX.X, ALU.max, apply_absolute_value=True))
            global_max_dve(dve, 0, amx[:, 0:CH])
            dve.wait_ge(ff["scale"], 1)
            for c in range(CH):
                h = chunk(H, c)
                link(dve.tensor_scalar(h, h, inverse(0), MAGIC, ALU.mult, ALU.add))
                link(dve.tensor_scalar(h, h, MAGIC + QMAX, MAGIC - QMAX - 1.0, ALU.min, ALU.max))
                dve.tensor_scalar(h, h, MAGIC, scale(0), ALU.subtract, ALU.mult).then_inc(ff["hq"], 1)
            for v in range(2 * len(UNITS)):
                f, c = UNITS[v % len(UNITS)]
                dve.wait_ge(ff["copied"], v + 1)
                ins = dve.tensor_reduce(amx[:, v:v + 1], span(U if v < len(UNITS) else GT, f, c), AX.X, ALU.max,
                                        apply_absolute_value=True)
            link(ins)
            global_max_dve(dve, 1, amx[:, len(UNITS):2 * len(UNITS)])
            global_max_dve(dve, 2, amx[:, 0:len(UNITS)])

            def clamp(t, f):
                return dve.tensor_scalar(span(t, f), span(t, f), MAGIC + QMAX, MAGIC - QMAX - 1.0, ALU.min, ALU.max)

            for f in range(FT):
                dve.wait_ge(ff["magic"], f + 1)
                link(clamp(GT, f))
                dve.tensor_scalar(span(GT, f), span(GT, f), MAGIC, scale(1), ALU.subtract, ALU.mult).then_inc(ff["gq"], 1)
            for f in range(FT):
                dve.wait_ge(ff["sig"], 2 * f + 2)
                link(dve.tensor_scalar(span(SG, f), span(SG, f), MAGIC + 65535.0, MAGIC, ALU.min, ALU.max))
                link(dve.scalar_tensor_tensor(span(GT, f), span(SG, f), MAGIC, span(GT, f), ALU.subtract, ALU.mult))
                link(dve.tensor_reduce(amx[:, f:f + 1], span(GT, f), AX.X, ALU.max, apply_absolute_value=True))
            link(dve.memset(unit_of[:, 3:4], 1.0 / 65536.0))
            global_max_dve(dve, 3, amx[:, 0:FT], unit_of[:, 3:4])
            link(dve.tensor_scalar(unit_of[:, 4:5], scale(2), scale(3), None, ALU.mult))
            for f in range(FT):
                dve.wait_ge(ff["magic"], FT + f + 1)
                clamp(U, f).then_inc(ff["uq"], 1)
            for f in range(FT):
                dve.wait_ge(ff["magic"], 2 * FT + f + 1)
                link(clamp(GT, f))
                dve.wait_ge(ff["uint"], f + 1)
                link(dve.scalar_tensor_tensor(span(U, f), span(GT, f), MAGIC, span(U, f), ALU.subtract, ALU.mult))
                link(dve.tensor_reduce(amx[:, f:f + 1], span(U, f), AX.X, ALU.max, apply_absolute_value=True))
            global_max_dve(dve, 4, amx[:, 0:FT], unit_of[:, 4:5])
            for f in range(FT):
                dve.wait_ge(ff["magic"], 3 * FT + f + 1)
                link(clamp(U, f))
                dve.tensor_scalar(span(U, f), span(U, f), MAGIC, scale(4), ALU.subtract, ALU.mult).then_inc(ff["o"], 1)
            dve.wait_ge(mo["fused"], 1)
            hot_dve(dve, l1, IN["subject"])
            for c in range(CH):
                dve.wait_ge(ff["down_ps"], c + 1)
                dve.tensor_tensor(chunk(X, c), chunk(X, c), bank(c), ALU.add).then_inc(ff["x"], 1)

        arena_at[0] = 0
        TOK = region(N)
        arena_at[0] = 3 * FT * N
        HOT = region(N)
        idcol = cols(B)
        gbias, gbias_x = cols(2 + E), cols(E)

        own_bias = region(B)
        IDS = slice(32, 64)

        def own_pe(pe, s, loaded, bias, x_ready):
            pe.wait_ge(s["hot"], 1)
            pe.wait_ge(l_sel, 16)
            pe.matmul(bank(6)[:, 0:B], bias[IDS, :], HOT[IDS, 0:N:S], start=True, stop=True).then_inc(s["ps"], 1)
            pe.wait_ge(loaded, 16 * B)
            for c in range(CH + 1):
                if c < CH:
                    x_ready(pe, c)
                    for t in range(c * TPC, (c + 1) * TPC):
                        o = PS[:, 4 * CT + t * P:4 * CT + (t + 1) * P]
                        if t == 2 * TPC:
                            pe.wait_ge(s["tok"], 1)
                        for q in range(4):
                            b = 4 * t + q
                            ins = pe.matmul(o[32 * q:32 * q + 32, :], X[:, b * S:(b + 1) * S], chosen[:, b * P:(b + 1) * P],
                                            start=True, stop=True, tile_position=(0, 32 * q))
                        ins.then_inc(s["ps"], 1)
                if c:
                    pe.wait_ge(s["tok"], c + 1)
                    for t in range((c - 1) * TPC, c * TPC):
                        ins = pe.transpose(PS[:, 4 * CT + t * P:4 * CT + (t + 1) * P], TOK[:, t * P:(t + 1) * P], K["ident"])
                    ins.then_inc(s["tr_ps"], 1)

        def own_act(act, s):
            act.wait_ge(s["ps"], 1)
            act.activation(own_bias, bank(6)[:, 0:B], ACT.Copy).then_inc(s["tok"], 1)
            for c in range(CH):
                act.wait_ge(s["ps"], TPC * (c + 1) + 1)
                act.activation(chunk(TOK, c), bank(4 + c), ACT.Copy).then_inc(s["tok"], 1)

        def hot_dve(dve, s, ids):
            link(dve.tensor_copy(idcol, ids))
            dve.tensor_scalar(HOT.rearrange("p (b s) -> p b s", b=B), over(idcol, 2, S), K["index"], None, ALU.is_equal)\
                .then_inc(s["hot"], 1)

        def own_dve(dve, s):
            for c in range(CH):
                dve.wait_ge(s["tr_ps"], c + 1)
                h, p_ = (x.rearrange("p (b s) -> p b s", b=CB) for x in (chunk(H, c), bank(4 + c)))
                dve.tensor_tensor(h, p_, over(own_bias[:, c * CB:(c + 1) * CB], 2, S), ALU.add).then_inc(s["h"], 1)
                if s is l2 and c == 0:
                    split_first_dve(dve)

        arena_at[0] = 0
        TOKN = region(N)
        XF = region(N)
        SB, HH = ([region(CT) for _ in range(3)] for _ in range(2))
        ACC, Y, YSQ = region(CT), region(CT), region(CT)
        OUTT = [region(CT) for _ in range(2)]
        LG, BI, SEL_, TA = (region(TILES * E) for _ in range(4))
        PAIR, PAIR2 = region(TILES * E * E), region(TILES * E * E)
        rmx, rsm = region(TILES), region(TILES)
        WX = region(2 * TILES * 8)
        ss, rstd, half = (region(TPC) for _ in range(3))
        assert arena_at[0] <= 3 * FT * N
        ORDER = [2, 0, 1, 3, 4, 5, 6, 7]
        UN = len(ORDER)
        NCH = 2 * CH
        ALL = UN * NCH
        GROUPS = [range(0, CH), range(CH, CH + 2), range(CH + 2, NCH)]
        UP_HIGH, UP_LOW, GT_HIGH, GT_LOW = (powers[:, n * UN * P:(n + 1) * UN * P] for n in range(4))
        WUP, WSUP = t_moe[:, 0:E * P], MW["Sup"]

        def unit(u):
            return u // UN, u % UN, ORDER[u % UN]

        def piece(t, k):
            return t[:, k * P:(k + 1) * P]

        def source(n):
            return chunk(H if n < CH else XF, n % CH)

        def moe_pe(pe):
            pe.wait_ge(l_moe, 16)
            pe.wait_ge(mo["fused"], 1)

            def logits(g):
                for n in GROUPS[g]:
                    if n < CH:
                        pe.wait_ge(l2["h"], n + 1)
                    else:
                        pe.wait_ge(mo["xf"], n - CH + 1)
                    for t in range(TPC):
                        at_t = 8 * ((n - GROUPS[g][0]) * TPC + t)
                        ins = pe.matmul(bank(7)[:, at_t:at_t + E], source(n)[:, t * P:(t + 1) * P],
                                        MW["rW"][:, (n // CH) * E:(n // CH + 1) * E], start=True, stop=True)
                ins.then_inc(mo["logit_ps"], 1)

            def up_gate(u):
                n, _, k = unit(u)
                if n == 0:
                    pe.wait_ge(mo["split"], 1)
                else:
                    pe.wait_ge(mo["xsplit"], n)
                if u >= 2:
                    pe.wait_ge(mo["hh"], u - 1)
                for to, high, low, done in ((bank(u % 2), UP_HIGH, UP_LOW, mo["up_ps"]),
                                            (bank(2 + u % 2), GT_HIGH, GT_LOW, mo["gt_ps"])):
                    xh, xl = chunk(mod_high, n % CH), chunk(mod_low, n % CH)
                    pe.matmul(to, piece(high, k), xh, start=True, stop=False)
                    pe.matmul(to, piece(high, k), xl, start=False, stop=False)
                    pe.matmul(to, piece(low, k), xh, start=False, stop=True).then_inc(done, 1)

            def down(u):
                n, _, k = unit(u)
                pe.wait_ge(mo["hh"], u + 1)
                if k >= 2:
                    v = E * n + k - 2
                    if v >= 2:
                        pe.wait_ge(mo["eo"], v - 1)
                    to, w = bank(4 + v % 2), piece(MW["Wdn"], k - 2)
                else:
                    if n and k == 0:
                        pe.wait_ge(mo["y"], n)
                    to, w = bank(6), MW["Sdn"]
                for t in range(TPC):
                    ins = pe.matmul(to[:, t * P:(t + 1) * P], HH[u % 3][:, t * P:(t + 1) * P], w,
                                    start=k >= 2 or (k == 0 and t == 0), stop=k >= 2, skip_group_check=True)
                ins.then_inc(mo["dn_ps"], 1)

            def tail(n):
                if n < CH:
                    pe.wait_ge(mo["normed"], n + 1)
                src = chunk(TOKN if n < CH else X, n % CH)
                for t in range(TPC):
                    ins = pe.transpose(bank(7)[:, t * P:(t + 1) * P], src[:, t * P:(t + 1) * P], K["ident"])
                ins.then_inc(mo["tr_ps"], 1)

            def beside(n, k):
                if k == 1 and n in (3, 5):
                    pe.wait_ge(mo["wT"], n)
                    logits((n - 1) // 2)
                if k == 3 and n:
                    pe.wait_ge(mo["wT"], n)
                    pe.wait_ge(mo["logit"], 1 + (n >= 3) + (n >= 5))
                    tail(n - 1)
                if k == 5:
                    if n == 0:
                        pe.wait_ge(mo["logit"], 1)
                    elif n <= CH:
                        pe.wait_ge(mo["xf"], n)
                    else:
                        pe.wait_ge(mo["fin"], n - CH)
                    pe.wait_ge(mo["w"], 1 + (n >= CH) + (n >= CH + 2))
                    for t in range(TPC):
                        at_t = 8 * (TPC * n + t)
                        ins = pe.transpose(bank(7)[0:8, t * P:(t + 1) * P], WX[:, at_t:at_t + 8], K["ident"])
                    ins.then_inc(mo["wT_ps"], 1)
                if k == 7:
                    pe.wait_ge(mo["wT"], n + 1)
                    rows = 64 if n < CH else 8
                    wt = chunk(HOT, n % CH)
                    for t in range(TPC):
                        ins = pe.matmul(bank(6)[:, t * P:(t + 1) * P], wt[0:rows, t * P:(t + 1) * P],
                                        MW["bdn"][0:rows, :], start=False, stop=True, skip_group_check=True)
                    ins.then_inc(mo["acc_ps"], 1)

            up_gate(0)
            pe.wait_ge(l2["h"], CH)
            logits(0)
            for u in range(ALL):
                if u + 1 < ALL:
                    up_gate(u + 1)
                beside(u // UN, u % UN)
                down(u)
            tail(NCH - 1)

        def moe_act(act):
            def gated(u):
                n, _, k = unit(u)
                act.wait_ge(mo["gt_ps"], u + 1)
                if u >= 3:
                    act.wait_ge(mo["hh"], u - 2)
                act.activation(SB[u % 3], bank(2 + u % 2), ACT.Silu, bias=gbias[:, k:k + 1]).then_inc(mo["s"], 1)

            def weigh(g):
                nt = TPC * len(GROUPS[g])
                act.wait_ge(mo["masked"], g + 1)
                act.activation(TA[:, 0:nt * E], TA[:, 0:nt * E], ACT.Exp).then_inc(mo["exped"], 1)

            act.wait_ge(mo["fused"], 1)
            for u in range(ALL):
                n, at_k, _ = unit(u)
                gated(u)
                if u == 3:
                    weigh(0)
                if at_k == 7 and n in (3, 5):
                    weigh((n - 1) // 2)

        def moe_pool(pool):
            pool.wait_ge(l2["tok"], CH + 1)
            pool.memset(half, -0.5).then_inc(mo["half"], 1)
            pool.memset(WX, 1.0).then_inc(mo["half"], 1)
            pool.wait_ge(mo["half"], 2)

            def split(n):
                x, high, low = source(n), chunk(mod_high, n % CH), chunk(mod_low, n % CH)
                if n < CH:
                    pool.wait_ge(l2["h"], n + 1)
                else:
                    pool.wait_ge(mo["xf"], n - CH + 1)
                pool.tensor_copy(high, x).then_inc(mo["xhigh"], 1)
                pool.wait_ge(mo["xhigh"], n)
                pool.tensor_tensor(low, x, high.bitcast(f32), ALU.subtract).then_inc(mo["xsplit"], 1)

            for n in range(1, CH):
                split(n)
            for n in range(NCH):
                pool.wait_ge(mo["y"], n + 1)
                pool.tensor_tensor(YSQ, Y, Y, ALU.mult).then_inc(mo["sq"], 1)
                pool.wait_ge(mo["ss"], n + 1)
                pool.tensor_tensor(rstd, ss, half, ALU.pow).then_inc(mo["rstd"], 1)
                if n < CH:
                    split(CH + n)

        def split_first_dve(dve):
            dve.wait_ge(l2["h"], 1)
            link(dve.tensor_copy(chunk(mod_high, 0), chunk(H, 0)))
            dve.tensor_tensor(chunk(mod_low, 0), chunk(H, 0), chunk(mod_high, 0).bitcast(f32), ALU.subtract)\
                .then_inc(mo["split"], 1)

        def moe_dve(dve):
            def logit(g):
                nt = TPC * len(GROUPS[g])
                i = GROUPS[g][0] // CH
                lg = LG[:, 0:nt * E].rearrange("p (t e) -> p t e", t=nt)
                dve.wait_ge(mo["logit_ps"], g + 1)
                b7 = bank(7)[:, 0:8 * nt].rearrange("p (t e) -> p t e", t=nt)[:, :, 0:E]
                dve.tensor_tensor(lg, b7, over(MW["rb"][:, i * E:(i + 1) * E], 1, nt), ALU.add).then_inc(mo["logit"], 1)

            def choose(g, parts):
                nt = TPC * len(GROUPS[g])
                i = GROUPS[g][0] // CH
                lgf, bif, self_, taf = (x[:, 0:nt * E] for x in (LG, BI, SEL_, TA))
                pf, qf = (x[:, 0:nt * E * E] for x in (PAIR, PAIR2))
                lg, bi, sel, ta = (x.rearrange("p (t e) -> p t e", t=nt) for x in (lgf, bif, self_, taf))
                p4, q4 = (x.rearrange("p (t e f) -> p t e f", t=nt, e=E) for x in (pf, qf))
                if 0 in parts:
                    dve.wait_ge(mo["logit"], g + 1)
                    link(dve.tensor_tensor(bi, lg, over(MW["gb"][:, i * E:(i + 1) * E], 1, nt), ALU.add))
                    dve.tensor_tensor(p4, over(bi, 2, E), over(bi, 3, E), ALU.is_gt)
                    link(dve.tensor_tensor(q4, over(bi, 2, E), over(bi, 3, E), ALU.is_equal))
                if 1 in parts:
                    q3 = qf.rearrange("p (t e) -> p t e", t=nt)
                    link(dve.tensor_tensor(q3, q3, over(K["tri"], 1, nt), ALU.mult))
                    link(dve.tensor_tensor(pf, pf, qf, ALU.add))
                    link(dve.tensor_reduce(sel, p4, AX.X, ALU.add))
                    link(dve.tensor_scalar(self_, self_, 2.0, None, ALU.is_lt))
                if 2 in parts:
                    dve.tensor_tensor(bif, lgf, self_, ALU.mult)
                    link(dve.tensor_scalar(taf, self_, 1.0, NEG, ALU.subtract, ALU.mult))
                    link(dve.tensor_tensor(taf, taf, bif, ALU.add))
                    link(dve.tensor_reduce(rmx[:, 0:nt], ta, AX.X, ALU.max))
                    dve.tensor_tensor(ta, ta, over(rmx[:, 0:nt], 2, E), ALU.subtract).then_inc(mo["masked"], 1)

            def weights(g):
                nt = TPC * len(GROUPS[g])
                first = 8 * TPC * GROUPS[g][0]
                w3 = WX[:, first:first + 8 * nt].rearrange("p (t e) -> p t e", t=nt)[:, :, 0:E]
                ta = TA[:, 0:nt * E].rearrange("p (t e) -> p t e", t=nt)
                dve.wait_ge(mo["exped"], g + 1)
                if g == 0:
                    dve.wait_ge(mo["half"], 2)
                link(dve.tensor_reduce(rsm[:, 0:nt], ta, AX.X, ALU.add))
                link(dve.reciprocal(rsm[:, 0:nt], rsm[:, 0:nt]))
                dve.tensor_tensor(w3, ta, over(rsm[:, 0:nt], 2, E), ALU.mult).then_inc(mo["w"], 1)
                dve.wait_ge(mo["w"], g + 1)

            def hidden(u):
                _, _, k = unit(u)
                bias = MW["sbup"][:, k:k + 1] if k < 2 else MW["bup"][:, k - 2:k - 1]
                dve.wait_ge(mo["up_ps"], u + 1)
                dve.wait_ge(mo["s"], u + 1)
                if u >= 3:
                    dve.wait_ge(mo["dn_ps"], u - 2)
                dve.scalar_tensor_tensor(HH[u % 3], bank(u % 2), bias, SB[u % 3], ALU.add, ALU.mult).then_inc(mo["hh"], 1)

            def combine(u):
                n, _, k = unit(u)
                if k < 2:
                    return
                e = k - 2
                v = E * n + e
                dve.wait_ge(mo["dn_ps"], u + 1)
                if v:
                    dve.wait_ge(mo["eo"], v)
                if e == 0 and n:
                    dve.wait_ge(mo["y"], n)
                if e == 0 and n >= CH:
                    dve.wait_ge(mo["normed"], n - CH + 1)
                for t in range(TPC):
                    r = slice(t * P, (t + 1) * P)
                    at_w = 8 * (TPC * n + t) + e
                    base = chunk(TOKN, n % CH) if e == 0 else ACC
                    ins = dve.scalar_tensor_tensor(ACC[:, r], bank(4 + v % 2)[:, r], WX[:, at_w:at_w + 1], base[:, r],
                                                   ALU.mult, ALU.add)
                ins.then_inc(mo["eo"], 1)

            def total(n):
                dve.wait_ge(mo["eo"], E * (n + 1))
                dve.wait_ge(mo["acc_ps"], n + 1)
                dve.wait_ge(mo["dn_ps"], UN * n + 3)
                if n:
                    dve.wait_ge(mo["normed"], n)
                dve.tensor_tensor(Y, ACC, bank(6), ALU.add).then_inc(mo["y"], 1)

            def sum_squares(n):
                dve.wait_ge(mo["sq"], n + 1)
                link(dve.tensor_reduce(ss, YSQ.rearrange("p (t d) -> p t d", t=TPC), AX.X, ALU.add))
                dve.tensor_scalar(ss, ss, 1.0 / D, 1e-6, ALU.mult, ALU.add).then_inc(mo["ss"], 1)

            def norm(n):
                i = n // CH
                dve.wait_ge(mo["rstd"], n + 1)
                if n >= CH:
                    dve.wait_ge(mo["tr_ps"], n - CH + 1)
                for t in range(TPC):
                    r = slice(t * P, (t + 1) * P)
                    ins = dve.scalar_tensor_tensor(chunk(TOKN, n % CH)[:, r], Y[:, r], rstd[:, t:t + 1],
                                                   MW["norm"][:, i * P:(i + 1) * P], ALU.mult, ALU.mult)
                ins.then_inc(mo["normed"], 1)

            def finish(n):
                dve.wait_ge(mo["tr_ps"], n + 1)
                if n < CH:
                    dve.tensor_copy(chunk(XF, n), bank(7)).then_inc(mo["xf"], 1)
                else:
                    dve.wait_ge(mo["normed"], n + 1)
                    if n >= CH + 2:
                        dve.wait_ge(stored[n % 2], 16 * ((n - CH) // 2))
                    dve.tensor_tensor(OUTT[n % 2], chunk(TOKN, n % CH), bank(7), ALU.add).then_inc(mo["fin"], 1)

            for u in range(ALL):
                n, at_k, _ = unit(u)
                hidden(u)
                if u == 0:
                    logit(0)
                if u < 3:
                    choose(0, (u,))
                if u == 3:
                    weights(0)
                    combine(0)
                if u > 3:
                    combine(u - 1)
                if at_k == 0 and n:
                    total(n - 1)
                if at_k == 1 and n:
                    sum_squares(n - 1)
                if at_k == 2:
                    if n:
                        norm(n - 1)
                    if n in (3, 5):
                        logit((n - 1) // 2)
                if at_k == 4 and n:
                    finish(n - 1)
                if at_k in (3, 5, 6) and n in (3, 5):
                    choose((n - 1) // 2, ((3, 5, 6).index(at_k),))
                if at_k == 6:
                    dve.wait_ge(mo["wT_ps"], n + 1)
                    if n:
                        dve.wait_ge(mo["acc_ps"], n)
                    dve.tensor_copy(chunk(HOT, n % CH)[0:8, :], bank(7)[0:8, :]).then_inc(mo["wT"], 1)
                if at_k == 0 and n in (4, 6):
                    weights(n // 2 - 1)
            combine(ALL - 1)
            total(NCH - 1)
            sum_squares(NCH - 1)
            norm(NCH - 1)
            finish(NCH - 1)

        arena_at[0] = 3 * FT * N
        UPT, GTW = region(UN * P), region(UN * P)

        def fuse_transposes_pe(pe):
            pe.wait_ge(l_moe, 16)
            pe.wait_ge(ff["copied"], 2 * len(UNITS))
            for k in range(UN):
                w = piece(WSUP, k) if k < 2 else piece(WUP, k - 2)
                ins = pe.transpose(PS[:, k * P:(k + 1) * P], w, K["ident"])
            ins.then_inc(mo["fuse_ps"], 1)

        def fuse_products_pe(pe):
            pe.wait_ge(mo["fuse_act"], 1)
            for k in range(UN):
                gt = MW["Sgt"] if k < 2 else piece(MW["Wgt"], k - 2)
                bias = MW["sbup"][:, k:k + 1] if k < 2 else MW["bup"][:, k - 2:k - 1]
                pe.matmul(PS[:, 2 * CT + k * P:2 * CT + (k + 1) * P], piece(UPT, k), gt, start=True, stop=True)
                ins = pe.matmul(bank(4)[:, 2 * k:2 * k + 2], gt, over(bias, 1, 2), start=True, stop=True)
            ins.then_inc(mo["fuse_ps"], 1)

        def fuse_transposed_act(act):
            act.wait_ge(mo["fuse_ps"], 1)
            act.activation(UPT, bank(0, 2), ACT.Copy).then_inc(mo["fuse_act"], 1)

        def fuse_act(act):
            act.wait_ge(mo["fuse_ps"], 2)
            act.activation(GTW, bank(2, 2), ACT.Copy)
            act.activation(GT_HIGH, bank(2, 2), ACT.Copy)
            act.activation(UP_HIGH[:, 0:2 * P], WSUP, ACT.Copy)
            act.activation(UP_HIGH[:, 2 * P:UN * P], WUP, ACT.Copy)
            act.activation(gbias[:, 0:2], bank(4)[:, 0:4:2], ACT.Identity, bias=MW["sbgt"])
            act.activation(gbias_x, bank(4)[:, 4:2 * UN:2], ACT.Copy).then_inc(mo["fuse_act"], 1)

        def fuse_pool(pool):
            pool.wait_ge(mo["fuse_act"], 2)
            pool.tensor_tensor(GT_LOW, GTW, GT_HIGH.bitcast(f32), ALU.subtract)
            pool.tensor_tensor(UP_LOW[:, 0:2 * P], WSUP, UP_HIGH[:, 0:2 * P].bitcast(f32), ALU.subtract)
            pool.tensor_tensor(UP_LOW[:, 2 * P:UN * P], WUP, UP_HIGH[:, 2 * P:UN * P].bitcast(f32), ALU.subtract)
            pool.tensor_tensor(gbias[:, 2:UN], gbias_x, MW["bgt"], ALU.add).then_inc(mo["fused"], 1)

        @block.sync
        def _(sp):
            for dst, src, s in ((t_const, consts, l_const), (t_cond, cond, l_const), (t_int, ints, l_int),
                                (X, x_fm, l_x), (x_tok, x_tm, l_x), (t_attn[0], attn0, l_attn0), (t_ctx, ctx_w, l_ctx),
                                (t_ffn, ffn_w, l_ffn), (t_sel, sel_w, l_sel), (t_attn[1], attn1, l_attn1),
                                (t_moe, moe_w, l_moe)):
                sp.dma_start(dst[:, :], src).then_inc(s, 16)
            sp.wait_ge(l_int, 16)
            sp.wait_ge(a["split"], 1)
            with sp.Fori(0, B) as b:
                i = sp.value_load(IN["subject"][0:1, bass.ds(b, 1)], min_val=0, max_val=NSUB - 1)
                sp.dma_start(chosen[:, bass.ds(b * P, P)],
                             w_subject[bass.ds(i, 1), :, :].rearrange("a p n -> p (a n)")).then_inc(chosen1, 16)
            sp.wait_ge(l1["ps"], TILES + 1)
            for b in range(B):
                i = sp.value_load(IN["category"][0:1, b:b + 1], min_val=0, max_val=NCAT - 1)
                sp.dma_start(chosen[:, b * P:(b + 1) * P],
                             w_category[bass.ds(i, 1), :, :].rearrange("a p n -> p (a n)")).then_inc(chosen2, 16)
            for j in range(CH):
                sp.wait_ge(mo["fin"], j + 1)
                sp.dma_start(out[:, j * CT:(j + 1) * CT], OUTT[j % 2]).then_inc(stored[j % 2], 16)
            for s in stored:
                sp.wait_ge(s, 16 * CH // 2)

        @block.tensor
        def _(pe):
            pooling_pe(pe)
            attention_pe(pe, 0, lambda e, j: e.wait_ge(a["h"], j // 2 + 1))
            ctx_pe(pe)
            ffn_pe(pe)
            own_pe(pe, l1, chosen1, SW["bias1"], lambda e, c: e.wait_ge(ff["x"], c + 1))
            attention_pe(pe, 1, lambda e, j: e.wait_ge(l1["h"], j // 2 + 1))
            own_pe(pe, l2, chosen2, MW["bdn"], lambda e, c: e.wait_ge(at[1]["y"], 2 * c + 2))
            moe_pe(pe)

        @block.scalar
        def _(act):
            pooling_act(act)
            attention_act(act, 0)
            ctx_act(act)
            ffn_act(act)
            own_act(act, l1)
            attention_act(act, 1)
            own_act(act, l2)
            moe_act(act)

        @block.gpsimd
        def _(pool):
            pooling_pool(pool)
            attention_pool(pool, 0)
            ctx_pool(pool)
            fuse_pool(pool)
            attention_pool(pool, 1)
            moe_pool(pool)

        @block.vector
        def _(dve):
            pooling_dve(dve)
            ffn_weights_dve(dve)
            attention_dve(dve, 0)
            ctx_dve(dve)
            ffn_dve(dve)
            own_dve(dve, l1)
            attention_dve(dve, 1)
            own_dve(dve, l2)
            moe_dve(dve)


def columns(spec, arrays):
    out = np.zeros((P, width(spec)), np.float32)
    at = 0
    for name, w in spec:
        x = np.asarray(arrays[name])
        out[:x.shape[0], at:at + w] = x.reshape(x.shape[0], w)
        at += w
    return out


def constants():
    p = np.arange(P)
    q, g = p % S, p // S
    k = np.arange(S)
    slopes = np.power(np.float32(2.0), -8.0 * np.arange(1, HEADS + 1, dtype=np.float32) / HEADS)
    head = g[:, None] * HG + np.arange(HG)[None, :]
    causal = k[None, :] <= q[:, None]
    rel = np.abs(q[:, None] - k[None, :]).astype(np.float32)
    alibi = np.where(causal[:, None, :], -slopes[head][:, :, None] * rel[:, None, :], np.float32(-NEG))
    e = np.arange(E)
    return columns(CONST, {
        "ident": np.eye(P), "alibi": alibi, "causal": np.where(causal, 0.0, -NEG), "pre": causal,
        "post": k[None, :] >= q[:, None], "cloze": k[None, :] != q[:, None], "empty": (WINDOW - 1 - q)[:, None],
        "hmask": (p[:, None] // HD) % HG == np.arange(HG)[None, :], "gmask": g[:, None] == np.arange(G)[None, :],
        "index": p[:, None] - 32, "tri": np.broadcast_to((e[None, :] < e[:, None]).reshape(1, -1), (P, E * E)),
        "ones": np.ones((P, P)), "magic": np.full((P, 1), MAGIC),
        "minus_magic": np.full((P, 1), -MAGIC)})


def kernel(**inputs):
    import concourse.bacc as bacc
    from concourse.bass_utils import run_bass_kernel_spmd

    a = {k: np.asarray(v) for k, v in inputs.items()}

    def heads(w):
        return w.T.reshape(G, HG, HD, D).transpose(1, 0, 2, 3).reshape(D, D)

    def col(v):
        return v.reshape(-1, 1)

    def twice(v):
        return np.concatenate([v, v])

    def attn(wq, wk, wv, wo, bq, bk, bv, bo):
        return columns(ATTN, {"wq": wq.T, "wk": wk.T, "wv": wv.T, "wo": heads(wo), "bv": bv.reshape(1, -1),
                              "bq": col(bq), "bk": col(bk), "bo": col(bo)})

    def rows(v):
        return np.broadcast_to(v.reshape(1, -1), (P, v.size))

    def blocks(w):
        return w.reshape(-1, P, w.shape[1]).transpose(1, 0, 2).reshape(P, -1)

    def below(n, v):
        return np.concatenate([np.zeros((n, v.shape[1]), np.float32), v])

    def side(w):
        return w.transpose(1, 0, 2).reshape(w.shape[1], -1)

    x = a["x"].reshape(N, D)
    arrays = {
        "consts": constants(),
        "cond": columns(COND, {"W1": a["L0_cond_W1"], "b1": col(a["L0_cond_b1"]),
                               "vrep": np.broadcast_to(col(a["L0_cond_v"]), (32, P)),
                               "blend": twice(a["cond_1024"]).T, "tau_raws": col(twice(a["condB_tauraws"])),
                               "tau_ctx": np.broadcast_to(a["L0_cond2_tau_ctx"].reshape(1, 1), (P, 1))}),
        "attn0": attn(*(a["L0_attn_" + n] for n in ("wq", "wk", "wv", "wo", "bq", "bk", "bv", "bo"))),
        "ctx_w": columns(CTX, {"Wg0": a["L0_cond2_Wg"][:, :D].T, "Wg1": a["L0_cond2_Wg"][:, D:].T,
                               "Wsoma": a["L0_cond2_Wsoma"].T, "Wtemp": a["L0_cond2_Wtemp"].T,
                               "Wout": a["L0_cond2_Wout"].T, "Wn1": a["L0_cond2_Wn1"].T, "Wn2": twice(a["cond_256"]).T,
                               "bg": col(a["L0_cond2_bg"]), "bn1": col(a["L0_cond2_bn1"]), "bn2": col(twice(a["condB_bn2"])),
                               "bsoma": col(a["L0_cond2_bsoma"]), "btemp": col(a["L0_cond2_btemp"]),
                               "gamma": col(a["L0_cond2_gamma"]), "beta": col(a["L0_cond2_beta"])}),
        "ffn_w": columns(FFN, {"up": blocks(a["L0_ffn_w_up"]), "gate": blocks(a["L0_ffn_w_gate"]), "down": a["L0_ffn_w_down"]}),
        "attn1": attn(*(a["L1_attn_" + n] for n in ("Wq", "Wk", "Wv", "Wo", "bq", "bk", "bv", "bo"))),
        "sel_w": columns(SEL, {"bias1": below(32, a["L1_cond_bias"])}),
        "moe_w": columns(MOE, {
            "Wup": side(a["L1_ffn_exp_Wup"]), "Wgt": side(a["L1_ffn_exp_Wg"]), "Wdn": side(a["L1_ffn_exp_Wdown"]),
            "Sup": a["L1_ffn_share_Wup"], "Sgt": a["L1_ffn_share_Wg"], "Sdn": a["L1_ffn_share_Wdown"],
            "bdn": np.concatenate([a["L1_ffn_exp_bdown"], twice(a["L1_ffn_share_bdown"].reshape(1, -1)),
                                   below(32 - 8, a["L1_cond2_b"])]),
            "norm": rows(a["L1_ffn_norm_w"]), "rW": side(a["L1_ffn_router_W"]), "rb": rows(a["L1_ffn_router_b"]),
            "gb": rows(a["L1_ffn_gate_bias"]), "bup": a["L1_ffn_exp_bup"].T, "bgt": a["L1_ffn_exp_bg"].T,
            "sbup": a["L1_ffn_share_bup"].reshape(2, D).T, "sbgt": col(a["L1_ffn_share_bg"])}),
        "ints": np.concatenate([np.repeat(a["itok_B_0_2"].reshape(TILES, 4).T, S, axis=0),
                                rows(a["itok_B_0_7"]), rows(a["itok_B_0_30"])], axis=1).astype(np.int32),
        "x_fm": x.T, "x_tm": x.reshape(TILES, P, D).transpose(1, 0, 2).reshape(P, N),
        "w_subject": a["L1_cond_weight"].transpose(0, 2, 1), "w_category": a["L1_cond2_W"],
    }
    arrays = {k: np.ascontiguousarray(v) for k, v in arrays.items()}
    nc = bacc.Bacc("TRN2", target_bir_lowering=False, num_devices=1)
    args = [nc.dram_tensor(k, v.shape, mybir.dt.from_np(v.dtype), kind="ExternalInput").ap() for k, v in arrays.items()]
    args.append(nc.dram_tensor("out", (P, N), mybir.dt.float32, kind="ExternalOutput").ap())
    program(nc, *args)
    got = run_bass_kernel_spmd(nc, [arrays], core_ids=[0]).results[0]["out"]
    return got.reshape(P, TILES, D).transpose(1, 0, 2).reshape(B, S, D)
```
